# Optimizing a Trainium2 kernel written in Bass

```python
import numpy as np
import jax
import jax.numpy as jnp

def _softmax(x, axis=-1):
    return jax.nn.softmax(x, axis=axis)

def _gelu(x):
    return jax.nn.gelu(x, approximate=True)

def _silu(x):
    return jax.nn.silu(x)

def _sigmoid(x):
    return jax.nn.sigmoid(x)

def _layernorm(x, axis=-1, eps=1e-05):
    m = jnp.mean(x, axis=axis, keepdims=True)
    v = jnp.var(x, axis=axis, keepdims=True)
    return (x - m) / jnp.sqrt(v + eps)

def _scatter_add(tgt, idx, src, axis=0):
    return tgt.at[idx].add(src)

def _segment_sum(src, seg, n):
    return jax.ops.segment_sum(src, seg, n)
kernel_name = 'mk_seq_postln_d1_jaxref_r4_29c227'

def setup_inputs(seed: int=0):
    np.random.seed(seed)
    _w = jnp.asarray

    def _L0_attn_setup():
        import jax, jax.numpy as jnp
        import numpy as np
        import math
        B, N, D, H = (1, 1024, 256, 16)
        HS = D // H
        NEG_INF = -10000.0
        key = jax.random.key(seed)
        k1, k2, k3, k4, k5 = jax.random.split(key, 5)
        return {'encodings': jax.random.normal(k1, (B, N, D), dtype=jnp.float32), 'attn_W': jax.random.normal(k2, (D, 3 * D), dtype=jnp.float32) * 0.02, 'attn_b': jax.random.normal(k3, (3 * D,), dtype=jnp.float32) * 0.02, 'out_W': jax.random.normal(k4, (D, D), dtype=jnp.float32) * 0.02, 'out_b': jax.random.normal(k5, (D,), dtype=jnp.float32) * 0.02}
    _L0_attn_in = _L0_attn_setup()

    def _L0_ffn_setup():
        import jax, jax.numpy as jnp
        import numpy as np
        B, N, D = (4, 1024, 256)
        E, K, H, ITERS = (8, 2, 64, 2)
        DT = 0.1
        C = 2 * D

        def _gelu(x):
            return jax.nn.gelu(x, approximate=False)

        def _inl(ctrl, xs, vs, mu):
            a, b, g = jnp.split(ctrl, 3, axis=-1)
            v_next = jax.nn.sigmoid(a) * vs - jax.nn.softplus(b) * (xs - mu)
            x_next = xs + DT * jax.nn.sigmoid(g) * v_next
            return (x_next, v_next)

        def _experts(ctx, idx, w1, b1, w2, b2):
            out = jnp.zeros((ctx.shape[0], w2.shape[2]), ctx.dtype)
            for e in range(E):
                h = _gelu(ctx @ w1[e] + b1[e])
                o = h @ w2[e] + b2[e]
                out = out + jnp.where((idx == e)[:, None], o, jnp.float32(0))
            return out

        def _forward(x, integration_weight, mu, router_w1, router_b1, router_w2, router_b2, halt_w1, halt_b1, halt_w2, halt_b2, expert_w1, expert_b1, expert_w2, expert_b2, shared_w1, shared_b1, shared_w2, shared_b2, shared_weight, refine_w1, refine_b1, refine_w2, refine_b2):
            b, n, d = x.shape
            xf = x.reshape(b * n, d)
            logits = _gelu(xf @ router_w1 + router_b1) @ router_w2 + router_b2
            probs = jax.nn.softmax(logits, axis=-1)
            topk_p, topk_i = jax.lax.top_k(probs, K)
            topk_p = topk_p / jnp.sum(topk_p, axis=-1, keepdims=True)
            flat_idx = topk_i.reshape(-1)
            flat_w = topk_p.reshape(-1, 1)
            v = jnp.zeros_like(xf)
            integrated = xf
            for _ in range(ITERS):
                ctx = jnp.concatenate([integrated, v], axis=-1)
                shared_ctrl = _gelu(ctx @ shared_w1 + shared_b1) @ shared_w2 + shared_b2
                x_sh, v_sh = _inl(shared_ctrl, integrated, v, mu)
                sw = jax.nn.sigmoid(shared_weight)
                ctx_e = jnp.repeat(ctx, K, axis=0)
                x_e = jnp.repeat(integrated, K, axis=0)
                v_e = jnp.repeat(v, K, axis=0)
                ctrl = _experts(ctx_e, flat_idx, expert_w1, expert_b1, expert_w2, expert_b2)
                x_r, v_r = _inl(ctrl, x_e, v_e, mu)
                x_r = (x_r * flat_w).reshape(-1, K, d).sum(axis=1)
                v_r = (v_r * flat_w).reshape(-1, K, d).sum(axis=1)
                x_next = sw * x_sh + (1.0 - sw) * x_r
                v_next = sw * v_sh + (1.0 - sw) * v_r
                halt = jax.nn.sigmoid(_gelu(integrated @ halt_w1 + halt_b1) @ halt_w2 + halt_b2)
                integrated = integrated + halt * (x_next - integrated)
                v = v + halt * (v_next - v)
            refined = _gelu(integrated @ refine_w1 + refine_b1) @ refine_w2 + refine_b2
            out = xf + integration_weight * refined
            return out.reshape(b, n, d)
        key = jax.random.key(seed)
        ks = jax.random.split(key, 12)
        rn = lambda k, s, sc=0.02: jax.random.normal(k, s, dtype=jnp.float32) * sc
        z = lambda s: jnp.zeros(s, jnp.float32)
        return {'x': jax.random.normal(ks[0], (B, N, D), dtype=jnp.float32), 'integration_weight': jnp.full((D,), 0.5, jnp.float32), 'mu': z((D,)), 'router_w1': rn(ks[1], (D, D // 4)), 'router_b1': z((D // 4,)), 'router_w2': rn(ks[2], (D // 4, E)), 'router_b2': z((E,)), 'halt_w1': rn(ks[3], (D, D // 4)), 'halt_b1': z((D // 4,)), 'halt_w2': rn(ks[4], (D // 4, 1)), 'halt_b2': z((1,)), 'expert_w1': rn(ks[5], (E, C, H)), 'expert_b1': z((E, H)), 'expert_w2': rn(ks[6], (E, H, 3 * D)), 'expert_b2': z((E, 3 * D)), 'shared_w1': rn(ks[7], (C, H)), 'shared_b1': z((H,)), 'shared_w2': rn(ks[8], (H, 3 * D)), 'shared_b2': z((3 * D,)), 'shared_weight': jnp.float32(0.5), 'refine_w1': rn(ks[9], (D, 2 * D)), 'refine_b1': z((2 * D,)), 'refine_w2': rn(ks[10], (2 * D, D)), 'refine_b2': z((D,))}
    _L0_ffn_in = _L0_ffn_setup()
    _d = {'L0_attn_encodings': _L0_attn_in['encodings'], 'L0_attn_attn_W': _L0_attn_in['attn_W'], 'L0_attn_attn_b': _L0_attn_in['attn_b'], 'L0_attn_out_W': _L0_attn_in['out_W'], 'L0_attn_out_b': _L0_attn_in['out_b'], 'L0_ffn_integration_weight': _L0_ffn_in['integration_weight'], 'L0_ffn_mu': _L0_ffn_in['mu'], 'L0_ffn_router_w1': _L0_ffn_in['router_w1'], 'L0_ffn_router_b1': _L0_ffn_in['router_b1'], 'L0_ffn_router_w2': _L0_ffn_in['router_w2'], 'L0_ffn_router_b2': _L0_ffn_in['router_b2'], 'L0_ffn_halt_w1': _L0_ffn_in['halt_w1'], 'L0_ffn_halt_b1': _L0_ffn_in['halt_b1'], 'L0_ffn_halt_w2': _L0_ffn_in['halt_w2'], 'L0_ffn_halt_b2': _L0_ffn_in['halt_b2'], 'L0_ffn_expert_w1': _L0_ffn_in['expert_w1'], 'L0_ffn_expert_b1': _L0_ffn_in['expert_b1'], 'L0_ffn_expert_w2': _L0_ffn_in['expert_w2'], 'L0_ffn_expert_b2': _L0_ffn_in['expert_b2'], 'L0_ffn_shared_w1': _L0_ffn_in['shared_w1'], 'L0_ffn_shared_b1': _L0_ffn_in['shared_b1'], 'L0_ffn_shared_w2': _L0_ffn_in['shared_w2'], 'L0_ffn_shared_b2': _L0_ffn_in['shared_b2'], 'L0_ffn_shared_weight': _L0_ffn_in['shared_weight'], 'L0_ffn_refine_w1': _L0_ffn_in['refine_w1'], 'L0_ffn_refine_b1': _L0_ffn_in['refine_b1'], 'L0_ffn_refine_w2': _L0_ffn_in['refine_w2'], 'L0_ffn_refine_b2': _L0_ffn_in['refine_b2']}
    _x0 = _d['L0_attn_encodings']
    _d['L0_attn_encodings'] = jax.random.normal(jax.random.fold_in(jax.random.key(seed), 1), (8, 512, 256), dtype=_x0.dtype)
    del _x0
    return _d

def reference(L0_attn_encodings, L0_attn_attn_W, L0_attn_attn_b, L0_attn_out_W, L0_attn_out_b, L0_ffn_integration_weight, L0_ffn_mu, L0_ffn_router_w1, L0_ffn_router_b1, L0_ffn_router_w2, L0_ffn_router_b2, L0_ffn_halt_w1, L0_ffn_halt_b1, L0_ffn_halt_w2, L0_ffn_halt_b2, L0_ffn_expert_w1, L0_ffn_expert_b1, L0_ffn_expert_w2, L0_ffn_expert_b2, L0_ffn_shared_w1, L0_ffn_shared_b1, L0_ffn_shared_w2, L0_ffn_shared_b2, L0_ffn_shared_weight, L0_ffn_refine_w1, L0_ffn_refine_b1, L0_ffn_refine_w2, L0_ffn_refine_b2):

    def _L0_attn_ref(encodings, attn_W, attn_b, out_W, out_b):
        import jax, jax.numpy as jnp
        import numpy as np
        import math
        B, N, D, H = (1, 1024, 256, 16)
        HS = D // H
        NEG_INF = -10000.0
        b, n, d = encodings.shape
        qkv = encodings @ attn_W + attn_b
        qkv = qkv.reshape(b, n, H, 3 * HS).transpose(0, 2, 1, 3)
        q, k, v = jnp.split(qkv, 3, axis=-1)
        scores = jnp.einsum('bhki,bhqi->bhkq', k, q) / math.sqrt(HS)
        mask = jnp.arange(n)[:, None] <= jnp.arange(n)[None, :]
        scores = jnp.where(mask, scores, jnp.float32(NEG_INF))
        prob = jax.nn.softmax(scores, axis=2)
        combined = jnp.einsum('bhkq,bhkl->bhql', prob, v)
        out = combined.transpose(0, 2, 1, 3).reshape(b, n, d)
        return out @ out_W + out_b

    def _L0_ffn_ref(x, integration_weight, mu, router_w1, router_b1, router_w2, router_b2, halt_w1, halt_b1, halt_w2, halt_b2, expert_w1, expert_b1, expert_w2, expert_b2, shared_w1, shared_b1, shared_w2, shared_b2, shared_weight, refine_w1, refine_b1, refine_w2, refine_b2):
        import jax, jax.numpy as jnp
        import numpy as np
        B, N, D = (4, 1024, 256)
        E, K, H, ITERS = (8, 2, 64, 2)
        DT = 0.1
        C = 2 * D

        def _gelu(x):
            return jax.nn.gelu(x, approximate=False)

        def _inl(ctrl, xs, vs, mu):
            a, b, g = jnp.split(ctrl, 3, axis=-1)
            v_next = jax.nn.sigmoid(a) * vs - jax.nn.softplus(b) * (xs - mu)
            x_next = xs + DT * jax.nn.sigmoid(g) * v_next
            return (x_next, v_next)

        def _experts(ctx, idx, w1, b1, w2, b2):
            out = jnp.zeros((ctx.shape[0], w2.shape[2]), ctx.dtype)
            for e in range(E):
                h = _gelu(ctx @ w1[e] + b1[e])
                o = h @ w2[e] + b2[e]
                out = out + jnp.where((idx == e)[:, None], o, jnp.float32(0))
            return out

        def _forward(x, integration_weight, mu, router_w1, router_b1, router_w2, router_b2, halt_w1, halt_b1, halt_w2, halt_b2, expert_w1, expert_b1, expert_w2, expert_b2, shared_w1, shared_b1, shared_w2, shared_b2, shared_weight, refine_w1, refine_b1, refine_w2, refine_b2):
            b, n, d = x.shape
            xf = x.reshape(b * n, d)
            logits = _gelu(xf @ router_w1 + router_b1) @ router_w2 + router_b2
            probs = jax.nn.softmax(logits, axis=-1)
            topk_p, topk_i = jax.lax.top_k(probs, K)
            topk_p = topk_p / jnp.sum(topk_p, axis=-1, keepdims=True)
            flat_idx = topk_i.reshape(-1)
            flat_w = topk_p.reshape(-1, 1)
            v = jnp.zeros_like(xf)
            integrated = xf
            for _ in range(ITERS):
                ctx = jnp.concatenate([integrated, v], axis=-1)
                shared_ctrl = _gelu(ctx @ shared_w1 + shared_b1) @ shared_w2 + shared_b2
                x_sh, v_sh = _inl(shared_ctrl, integrated, v, mu)
                sw = jax.nn.sigmoid(shared_weight)
                ctx_e = jnp.repeat(ctx, K, axis=0)
                x_e = jnp.repeat(integrated, K, axis=0)
                v_e = jnp.repeat(v, K, axis=0)
                ctrl = _experts(ctx_e, flat_idx, expert_w1, expert_b1, expert_w2, expert_b2)
                x_r, v_r = _inl(ctrl, x_e, v_e, mu)
                x_r = (x_r * flat_w).reshape(-1, K, d).sum(axis=1)
                v_r = (v_r * flat_w).reshape(-1, K, d).sum(axis=1)
                x_next = sw * x_sh + (1.0 - sw) * x_r
                v_next = sw * v_sh + (1.0 - sw) * v_r
                halt = jax.nn.sigmoid(_gelu(integrated @ halt_w1 + halt_b1) @ halt_w2 + halt_b2)
                integrated = integrated + halt * (x_next - integrated)
                v = v + halt * (v_next - v)
            refined = _gelu(integrated @ refine_w1 + refine_b1) @ refine_w2 + refine_b2
            out = xf + integration_weight * refined
            return out.reshape(b, n, d)
        return _forward(x, integration_weight, mu, router_w1, router_b1, router_w2, router_b2, halt_w1, halt_b1, halt_w2, halt_b2, expert_w1, expert_b1, expert_w2, expert_b2, shared_w1, shared_b1, shared_w2, shared_b2, shared_weight, refine_w1, refine_b1, refine_w2, refine_b2)
    x = L0_attn_encodings
    x = _layernorm(x + _L0_attn_ref(x, L0_attn_attn_W, L0_attn_attn_b, L0_attn_out_W, L0_attn_out_b), axis=-1)
    x = _layernorm(x + _L0_ffn_ref(x, L0_ffn_integration_weight, L0_ffn_mu, L0_ffn_router_w1, L0_ffn_router_b1, L0_ffn_router_w2, L0_ffn_router_b2, L0_ffn_halt_w1, L0_ffn_halt_b1, L0_ffn_halt_w2, L0_ffn_halt_b2, L0_ffn_expert_w1, L0_ffn_expert_b1, L0_ffn_expert_w2, L0_ffn_expert_b2, L0_ffn_shared_w1, L0_ffn_shared_b1, L0_ffn_shared_w2, L0_ffn_shared_b2, L0_ffn_shared_weight, L0_ffn_refine_w1, L0_ffn_refine_b1, L0_ffn_refine_w2, L0_ffn_refine_b2), axis=-1)
    return x

_drawn_inputs = setup_inputs


def setup_inputs(seed=0):
    import zlib

    import numpy as np

    out = dict(_drawn_inputs(seed))
    spreads = {'L0_ffn_integration_weight': (0.5, 0.6),
     'L0_ffn_mu': (0.0, 2.0),
     'L0_ffn_router_b1': (0.0, 2.0),
     'L0_ffn_router_b2': (0.0, 2.0),
     'L0_ffn_halt_b1': (0.0, 2.0),
     'L0_ffn_expert_b1': (0.0, 2.0),
     'L0_ffn_expert_b2': (0.0, 2.0),
     'L0_ffn_shared_b1': (0.0, 2.0),
     'L0_ffn_shared_b2': (0.0, 2.0),
     'L0_ffn_refine_b1': (0.0, 0.8),
     'L0_ffn_refine_b2': (0.0, 0.312)}
    factors = {'L0_attn_attn_W': 4.661,
     'L0_attn_attn_b': 8.0,
     'L0_attn_out_W': 4.148,
     'L0_attn_out_b': 2.901,
     'L0_ffn_router_w1': 55.968,
     'L0_ffn_router_w2': 41.442,
     'L0_ffn_halt_w1': 8.0,
     'L0_ffn_halt_w2': 8.0,
     'L0_ffn_expert_w1': 47.605,
     'L0_ffn_expert_w2': 40.157,
     'L0_ffn_shared_w1': 26.695,
     'L0_ffn_shared_w2': 23.083,
     'L0_ffn_refine_w1': 2.974,
     'L0_ffn_refine_w2': 2.76}
    for name, (base, spread) in spreads.items():
        noise = np.random.default_rng([zlib.crc32(name.encode()), seed]).standard_normal(out[name].shape)
        drawn = base * np.exp(spread * noise) if base else spread * noise
        out[name] = jnp.asarray(drawn.astype(out[name].dtype))
    for name, factor in factors.items():
        out[name] = (out[name] * factor).astype(out[name].dtype)
    return out
```

```python
from contextlib import ExitStack

import concourse.bass as bass
from concourse import mybir

ALU = mybir.AluOpType
ACT = mybir.ActivationFunctionType
AX = mybir.AxisListType
F32 = mybir.dt.float32
BF16 = mybir.dt.bfloat16
F16 = mybir.dt.float16
U32 = mybir.dt.uint32

P = 128
SEQS = 8
TOK = 512
NT = TOK // P
D = 256
KC = D // P
HEADS = 16
HS = D // HEADS
HPC = P // HS
STACK = 6 * HS
QK_SCALE = 1.0 / 4.0
VW = 32
NEG = -1.0e30
EPS = 1e-5
Q_PARTS = (0, 0, 0, 1, 1, 2)
K_PARTS = (0, 1, 2, 0, 1, 0)

E = 8
HID = 64
EC = E * HID // P
FC = EC + 1
HCOLS = FC * P
CTRL = 3 * D
RH = 2 * D
RC = RH // P
DT = 0.1
STREAMS = 3


class Steps:

    def __init__(self, per_round, rnd):
        self.before, self.per_round, self.n = rnd * per_round, per_round, 0

    def next(self):
        self.n += 1
        return self.before + self.n

    def end(self):
        assert self.n == self.per_round, (self.n, self.per_round)


NORM_STEPS = 6


def norm_buffers(sb, tag):
    shapes = {"stats": [P, NT, 6], "mv": [P, NT, 2], "var": [P, NT], "log": [P, NT], "rstd": [P, NT], "tmp": [P, NT]}
    return {name: sb(f"{tag}_{name}", shape, F32) for name, shape in shapes.items()}


def layer_norm(dve, nc, step, chain, res, n, sems, rnd):
    v, (var_ready, _, rstd_raw) = nc.vector, sems
    for t in range(NT):
        last = v.bn_stats(n["stats"][:, t, :], res[:, t, :])
    last.then_inc(step, 1)
    dve.wait_ge(step, chain.next())
    v.memset(n["tmp"][:], 0.0)
    for t in range(NT):
        last = v.bn_aggr(n["mv"][:, t, :], n["stats"][:, t, :])
    last.then_inc(step, 1)
    dve.wait_ge(step, chain.next())
    v.tensor_scalar(n["var"][:], n["mv"][:, :, 1], EPS, None, ALU.add).then_inc(var_ready, 1)
    dve.wait_ge(rstd_raw, rnd + 1)
    y, tmp = n["rstd"][:], n["tmp"][:]
    v.tensor_tensor(tmp, y, y, ALU.mult).then_inc(step, 1)
    dve.wait_ge(step, chain.next())
    v.tensor_tensor(tmp, tmp, n["var"][:], ALU.mult).then_inc(step, 1)
    dve.wait_ge(step, chain.next())
    v.tensor_scalar(tmp, tmp, -0.5, 1.5, ALU.mult, ALU.add).then_inc(step, 1)
    dve.wait_ge(step, chain.next())
    v.tensor_tensor(y, y, tmp, ALU.mult).then_inc(step, 1)
    dve.wait_ge(step, chain.next())


def rsqrt_guess(act, nc, n, sems, rnd):
    var_ready, rstd_step, rstd_raw = sems
    act.wait_ge(var_ready, rnd + 1)
    nc.scalar.activation(n["log"][:], n["var"][:], ACT.Ln).then_inc(rstd_step, 1)
    act.wait_ge(rstd_step, rnd + 1)
    nc.scalar.activation(n["rstd"][:], n["log"][:], ACT.Exp, scale=-0.5).then_inc(rstd_raw, 1)


def normalised(nc, out, res, n):
    for t in range(NT):
        last = nc.vector.tensor_scalar(out[:, t, :], res[:, t, :], n["mv"][:, t, 0:1], n["rstd"][:, t:t + 1],
                                       ALU.subtract, ALU.mult)
    return last


def attention(nc, encodings, attn_W, attn_b, out_W, out_b, parts_dram, normed_dram):
    with ExitStack() as ctx:
        def sb(name, shape, dt):
            return ctx.enter_context(nc.sbuf_tensor(name, shape, dt))

        primed = []

        def sem(name, start=0):
            s = ctx.enter_context(nc.semaphore(name))
            if start:
                primed.append((s, start))
            return s

        ps = ctx.enter_context(nc.psum_tensor("att_ps", [P, 8, 512], F32))
        PVB = 2
        SC = 3

        wqk = sb("wqk", [P, KC, 2, D], F32)
        wv = sb("wv", [P, KC, D], F32)
        wo = sb("wo", [P, KC, D], F32)
        bias_row = sb("bias_row", [1, 2, D], F32)
        bias_qk = sb("bias_qk", [P, 4], F32)
        bias_v = sb("bias_v", [P, D], F32)
        bias_o = sb("bias_o", [P, D], F32)
        one = sb("one", [1, 2], F32)
        ident = sb("ident", [P, P], F32)
        identb = sb("identb", [P, P], BF16)
        mask_q = sb("mask_q", [P, P], BF16)
        mask_k = sb("mask_k", [P, P], BF16)
        x_in = [sb(f"x_in{p}", [P, NT, D], F32) for p in range(2)]
        xo = [sb(f"xo{p}", [P, NT, D], F32) for p in range(2)]
        xT = sb("xT", [P, KC, TOK], F32)
        qk32 = sb("qk32", [P, 4, TOK], F32)
        parts = sb("parts", [P, 3, 4, TOK], BF16)
        q_stack = [sb(f"q_stack{p}", [STACK + 2, HEADS, TOK], BF16) for p in range(2)]
        k_stack = [sb(f"k_stack{p}", [STACK + 2, HEADS, TOK], BF16) for p in range(2)]
        values = [sb(f"values{p}", [P, NT, HEADS, VW], F32) for p in range(2)]
        probs = sb("probs", [P, 4, 5, TOK], F32)
        neg_max = sb("neg_max", [P, 2 * HEADS, NT], F32)
        max_parts = sb("max_parts", [HEADS * NT, 2, P], BF16)
        heads_out = sb("heads_out", [P, TOK], F32)
        rden = sb("rden", [P, NT, 4], F32)
        attn = sb("attn", [P, NT, D], F32)
        attnT = sb("attnT", [P, KC, TOK], F32)
        res = sb("res", [P, NT, D], F32)
        norm = norm_buffers(sb, "att")
        normed = sb("normed", [P, NT, D], F32)

        weights_in = sem("weights_in")
        const_step = sem("const_step")
        consts = sem("consts")
        bias_ps = sem("bias_ps")
        bias_ok = sem("bias_ok")
        x_full = [sem(f"x_full{p}") for p in range(2)]
        x_added = sem("x_added")
        front_filled = [sem(f"front_filled{i}") for i in range(2)]
        front_freed = [sem(f"front_freed{i}", 1) for i in range(2)]
        front_step = sem("front_step")
        parts_ready = sem("parts_ready", 1)
        parts_stored = sem("parts_stored", 1)
        stack_full = [sem(f"stack_full{p}") for p in range(2)]
        sc_filled = [sem(f"sc_filled{i}") for i in range(5)]
        sc_freed = [sem(f"sc_freed{i}", 1) for i in range(5)]
        pv_filled = sem("pv_filled")
        max_ready = sem("max_ready")
        max_rows_full = [sem(f"max_rows_full{p}") for p in range(2)]
        heads_ready = sem("heads_ready")
        attn_ready = sem("attn_ready", 1)
        back_step = sem("back_step")
        norm_sems = (sem("var_ready"), sem("rstd_step"), sem("rstd_raw"))
        normed_ready = sem("normed_ready")
        normed_stored = sem("normed_stored", 1)

        PAIRS = HEADS // 2
        SC_USES = [2 * PAIRS + (i < 4) for i in range(5)]
        WEIGHT_LOADS = KC * 3 + 5
        FRONT_STEPS, BACK_STEPS = 4, 5 + NORM_STEPS

        block = ctx.enter_context(nc.Block())
        x_dram = encodings.rearrange("s (t p) d -> s p t d", p=P)
        normed_out = normed_dram.rearrange("s (t p) d -> s p t d", p=P)

        def sequences(eng, front, back):
            front(0, 0, 0)
            with eng.Fori(0, SEQS // 2 - 1) as i:
                front(2 * i + 1, 1, i)
                back(2 * i, 0, i, True)
                front(2 * i + 2, 0, i + 1)
                back(2 * i + 1, 1, i, True)
            front(SEQS - 1, 1, SEQS // 2 - 1)
            back(SEQS - 2, 0, SEQS // 2 - 1, False)
            back(SEQS - 1, 1, SEQS // 2 - 1, False)

        @block.sync
        def _(sp):
            for s, start in primed:
                sp.sem_inc(s, start)
            w_cols = attn_W.rearrange("(c p) (h t d) -> t c p h d", p=P, t=3, d=HS)
            b_cols = attn_b.rearrange("(h t d) -> t h d", t=3, d=HS)
            sp.dma_start(x_in[0][:], x_dram[0]).then_inc(x_full[0], 16)
            for c in range(KC):
                for t in range(2):
                    sp.dma_start(wqk[:, c, t, :].rearrange("p (h d) -> p h d", d=HS),
                                 w_cols[t, c]).then_inc(weights_in, 16)
                sp.dma_start(wv[:, c, :].rearrange("p (h d) -> p h d", d=HS), w_cols[2, c]).then_inc(weights_in, 16)
            sp.dma_start(wo[:], out_W.rearrange("(c p) n -> p c n", p=P)).then_inc(weights_in, 16)
            for t in range(2):
                sp.dma_start(bias_row[0:1, t, :].rearrange("p (h d) -> p h d", d=HS),
                             b_cols[t].unsqueeze(0)).then_inc(weights_in, 16)
            sp.dma_start(bias_v[:].rearrange("p (h d) -> p h d", d=HS),
                         b_cols[2].partition_broadcast(P)).then_inc(weights_in, 16)
            sp.dma_start(bias_o[:], out_b.partition_broadcast(P)).then_inc(weights_in, 16)
            sp.dma_start(x_in[1][:], x_dram[1]).then_inc(x_full[1], 16)

            def front(b, p, nth):
                for half in range(2):
                    sp.wait_ge(parts_ready, 2 * b + half + 1 + 1)
                    for part in range(3):
                        sp.dma_start(parts_dram[b, half, part].rearrange("m f n -> f m n"),
                                     parts[:, part, 2 * half:2 * half + 2, :]).then_inc(parts_stored, 16)
                sp.wait_ge(parts_stored, 96 * (b + 1) + 1)
                for half, stack, rows in ((0, q_stack[p], Q_PARTS), (1, k_stack[p], K_PARTS)):
                    for j, part in enumerate(rows):
                        sp.dma_start(stack[j * HS:(j + 1) * HS, :, :],
                                     parts_dram[b, half, part].rearrange("m (h i) n -> i (m h) n", i=HS)
                                     ).then_inc(stack_full[p], 16)

            def back(b, p, nth, more):
                sp.wait_ge(max_ready, b + 1)
                for part in range(2):
                    sp.dma_start(q_stack[p][STACK + part:STACK + part + 1, :, :],
                                 max_parts[:, part, :]).then_inc(max_rows_full[p], 16)
                if more:
                    sp.wait_ge(x_added, b + 1)
                    sp.wait_ge(front_filled[1], 4 * b + 1)
                    sp.dma_start(x_in[p][:], x_dram[b + 2]).then_inc(x_full[p], 16)
                sp.wait_ge(normed_ready, b + 1)
                sp.dma_start(normed_out[b], normed[:]).then_inc(normed_stored, 16)

            sequences(sp, front, back)
            sp.wait_ge(normed_stored, 16 * SEQS + 1)

        @block.gpsimd
        def _(pool):
            steps = Steps(0, 0)
            g = nc.gpsimd
            g.memset(ident[:], 1.0).then_inc(const_step, 1)
            pool.wait_ge(const_step, steps.next())
            g.affine_select(out=ident[:], in_=ident[:], compare_op=ALU.is_equal, fill=0.0,
                            base=0, pattern=[[-1, P]], channel_multiplier=1).then_inc(const_step, 1)
            pool.wait_ge(const_step, steps.next())
            g.tensor_copy(identb[:], ident[:]).then_inc(const_step, 1)
            pool.wait_ge(const_step, steps.next())
            for mask, step in ((mask_q, 1), (mask_k, -1)):
                g.memset(mask[:], 0.0).then_inc(const_step, 1)
                pool.wait_ge(const_step, steps.next())
                g.affine_select(out=mask[:], in_=mask[:], compare_op=ALU.is_ge, fill=NEG,
                                base=0, pattern=[[-step, P]], channel_multiplier=step).then_inc(const_step, 1)
                pool.wait_ge(const_step, steps.next())
            g.memset(neg_max[:, HEADS:, :], 0.0).then_inc(const_step, 1)
            pool.wait_ge(const_step, steps.next())
            g.memset(one[:], 1.0).then_inc(consts, 1)
            pool.wait_ge(consts, 1)
            for p in range(2):
                g.memset(values[p][:], 0.0).then_inc(const_step, 1)
                pool.wait_ge(const_step, steps.next())
                g.memset(values[p][:, :, :, HS:HS + 1], 1.0).then_inc(const_step, 1)
                pool.wait_ge(const_step, steps.next())
            g.memset(k_stack[0][STACK:STACK + 2, :, :], 1.0).then_inc(const_step, 1)
            pool.wait_ge(const_step, steps.next())
            g.memset(k_stack[1][STACK:STACK + 2, :, :], 1.0).then_inc(consts, 1)
            pool.wait_ge(consts, 2)
            pool.wait_ge(weights_in, 16 * WEIGHT_LOADS)

            def residual(b, p, nth):
                pool.wait_ge(x_full[p], 16 * (nth + 1))
                if not (isinstance(b, int) and b < 2):
                    pool.wait_ge(sc_freed[3], SC_USES[3] * (b - 1) + 1)
                g.tensor_tensor(xo[p][:], x_in[p][:], bias_o[:].unsqueeze(1).to_broadcast([P, NT, D]),
                                ALU.add).then_inc(x_added, 1)

            residual(0, 0, 0)
            residual(1, 1, 0)
            with pool.Fori(1, SEQS // 2) as i:
                residual(2 * i, 0, i)
                residual(2 * i + 1, 1, i)

        @block.scalar
        def _(act):
            nc.scalar.preload_act_table_set("natural_log_exp_and_others")
            act.wait_ge(bias_ps, 1)
            nc.scalar.mul(bias_qk[:, 0:2], ps[:, PVB, 0:2], QK_SCALE)
            nc.scalar.copy(bias_qk[:, 2:4], ps[:, PVB, 2:4]).then_inc(bias_ok, 1)
            act.wait_ge(bias_ok, 1)

            def front(b, p, nth):
                act.wait_ge(front_filled[0], 4 * b + 1)
                nc.scalar.copy(xT[:, 0, :], ps[:, 0, :]).then_inc(front_freed[0], 1)
                for m in range(4):
                    bank, use = m % 2, 1 + m // 2
                    act.wait_ge(front_filled[bank], 4 * b + use + 1)
                    if m == 0:
                        act.wait_ge(parts_ready, 2 * b + 1)
                        act.wait_ge(parts_stored, 96 * b + 1)
                    scale = QK_SCALE if m < 2 else 1.0
                    nc.scalar.activation(qk32[:, m, :], ps[:, bank, :], ACT.Identity,
                                         bias=bias_qk[:, m:m + 1], scale=scale)
                    nc.scalar.activation(parts[:, 0, m, :], ps[:, bank, :], ACT.Identity,
                                         bias=bias_qk[:, m:m + 1], scale=scale).then_inc(front_freed[bank], 1)

            def heads(b, g):
                act.wait_ge(pv_filled, 9 * b + 1 + 2 * g + 1)
                nc.scalar.copy(heads_out[:], ps[:, PVB, :]).then_inc(heads_ready, 1)

            def back(b, p, nth, more):
                for pair in range(PAIRS):
                    if pair in (4, 6):
                        heads(b, pair // 2 - 2)
                    for u in range(5):
                        act.wait_ge(sc_filled[u], SC_USES[u] * b + PAIRS + pair + 1)
                        nc.scalar.activation(probs[:, pair % 4, u, :], ps[:, SC + u, :],
                                             ACT.Exp).then_inc(sc_freed[u], 1)
                heads(b, 2)
                heads(b, 3)
                act.wait_ge(sc_filled[0], SC_USES[0] * (b + 1))
                nc.scalar.copy(attnT[:, 0, :], ps[:, SC, :]).then_inc(sc_freed[0], 1)
                rsqrt_guess(act, nc, norm, norm_sems, b)

            sequences(act, front, back)

        @block.vector
        def _(dve):
            v = nc.vector

            def front(b, p, nth):
                dve.wait_ge(front_filled[1], 4 * b + 1)
                v.tensor_copy(xT[:, 1, :], ps[:, 1, :]).then_inc(front_freed[1], 1)
                fsteps = Steps(FRONT_STEPS, b)
                for half in range(2):
                    s = slice(2 * half, 2 * half + 2)
                    dve.wait_ge(front_freed[0], 4 * b + 2 + half + 1)
                    dve.wait_ge(front_freed[1], 4 * b + 2 + half + 1)
                    v.tensor_tensor(qk32[:, s, :], qk32[:, s, :], parts[:, 0, s, :], ALU.subtract).then_inc(front_step, 1)
                    dve.wait_ge(front_step, fsteps.next())
                    v.tensor_copy(parts[:, 1, s, :], qk32[:, s, :]).then_inc(front_step, 1)
                    dve.wait_ge(front_step, fsteps.next())
                    v.tensor_tensor(parts[:, 2, s, :], qk32[:, s, :], parts[:, 1, s, :],
                                    ALU.subtract).then_inc(parts_ready, 1)
                fsteps.end()
                if isinstance(b, int) and b == 0:
                    dve.wait_ge(consts, 2)
                for bank in range(2):
                    dve.wait_ge(front_filled[bank], 4 * b + 4)
                    for t in range(2):
                        last = v.tensor_tensor(
                            values[p][:, 2 * bank + t, :, 0:HS],
                            ps[:, bank, t * D:(t + 1) * D].rearrange("p (h d) -> p h d", d=HS),
                            bias_v[:].rearrange("p (h d) -> p h d", d=HS), ALU.add)
                    last.then_inc(front_freed[bank], 1)

            def row_max(out, scores):
                return v.tensor_reduce(out, scores, AX.X, ALU.max, negate=True)

            def back(b, p, nth, more):
                for pair in range(PAIRS):
                    for u in range(5):
                        dve.wait_ge(sc_filled[u], SC_USES[u] * b + pair + 1)
                        bank, h = ps[:, SC + u, :], 2 * pair + u // 3
                        if u in (0, 3):
                            last = row_max(neg_max[:, h, 3:4], bank)
                        elif u in (1, 4):
                            row_max(neg_max[:, h, 0:1], bank[:, 0:P])
                            last = row_max(neg_max[:, h, 2:3], bank[:, P:])
                        else:
                            last = row_max(neg_max[:, 2 * pair:2 * pair + 2, 1:2],
                                           bank.rearrange("p (a k) -> p a k", a=2))
                        last.then_inc(sc_freed[u], 1)
                chain = Steps(BACK_STEPS, b)
                dve.wait_ge(pv_filled, 9 * b + 1)
                mx = ps[0:HEADS * NT, PVB, 0:P]
                v.tensor_copy(max_parts[:, 0, :], mx).then_inc(back_step, 1)
                dve.wait_ge(back_step, chain.next())
                v.tensor_tensor(max_parts[:, 1, :], mx, max_parts[:, 0, :], ALU.subtract).then_inc(max_ready, 1)
                for g in range(4):
                    dve.wait_ge(pv_filled, 9 * b + 1 + 2 * g + 2)
                    o = ps[:, PVB, :].rearrange("p (t j c) -> p t j c", t=NT, c=VW)
                    v.reciprocal(rden[:], o[:, :, :, HS]).then_inc(back_step, 1)
                    dve.wait_ge(back_step, chain.next())
                    v.tensor_tensor(attn[:, :, g * 4 * HS:(g + 1) * 4 * HS].rearrange("p t (j d) -> p t j d", d=HS),
                                    o[:, :, :, 0:HS], rden[:].unsqueeze(3).to_broadcast([P, NT, 4, HS]),
                                    ALU.mult).then_inc(attn_ready, 1)
                dve.wait_ge(sc_filled[1], SC_USES[1] * (b + 1))
                v.tensor_copy(attnT[:, 1, :], ps[:, SC + 1, :]).then_inc(sc_freed[1], 1)
                dve.wait_ge(x_added, b + 1)
                for u in range(2):
                    dve.wait_ge(sc_filled[2 + u], SC_USES[2 + u] * (b + 1))
                    v.tensor_tensor(res[:, 2 * u:2 * u + 2, :],
                                    ps[:, SC + 2 + u, :].rearrange("p (t d) -> p t d", d=D),
                                    xo[p][:, 2 * u:2 * u + 2, :], ALU.add).then_inc(sc_freed[2 + u], 1)
                dve.wait_ge(sc_freed[3], SC_USES[3] * (b + 1) + 1)
                layer_norm(dve, nc, back_step, chain, res, norm, norm_sems, b)
                dve.wait_ge(normed_stored, 16 * b + 1)
                normalised(nc, normed, res, norm).then_inc(normed_ready, 1)
                chain.end()

            sequences(dve, front, back)

        @block.tensor
        def _(pe):
            t_ = nc.tensor
            pe.wait_ge(consts, 1)
            pe.wait_ge(weights_in, 16 * WEIGHT_LOADS)
            for m in range(4):
                last = t_.matmul(ps[:, PVB, m:m + 1], bias_row[0:1, m // 2, (m % 2) * P:(m % 2 + 1) * P],
                                 one[0:1, 0:1], start=True, stop=True)
            last.then_inc(bias_ps, 1)

            def front(b, p, nth):
                pe.wait_ge(x_full[p], 16 * (nth + 1))
                for c in range(KC):
                    pe.wait_ge(front_freed[c], 4 * b + 1)
                    for t in range(NT):
                        last = t_.transpose(ps[:, c, t * P:(t + 1) * P], x_in[p][:, t, c * P:(c + 1) * P], ident[:])
                    last.then_inc(front_filled[c], 1)
                for c in range(KC):
                    pe.wait_ge(front_freed[c], 4 * b + 1 + 1)
                for m in range(4):
                    bank, use = m % 2, 1 + m // 2
                    pe.wait_ge(front_freed[bank], 4 * b + use + 1)
                    for c in range(KC):
                        last = t_.matmul(ps[:, bank, :], wqk[:, c, m // 2, (m % 2) * P:(m % 2 + 1) * P],
                                         xT[:, c, :], start=(c == 0), stop=(c == KC - 1))
                    last.then_inc(front_filled[bank], 1)
                for t in range(NT):
                    bank = t // 2
                    if t % 2 == 0:
                        pe.wait_ge(front_freed[bank], 4 * b + 3 + 1)
                    for c in range(KC):
                        last = t_.matmul(ps[:, bank, (t % 2) * D:(t % 2 + 1) * D], xT[:, c, t * P:(t + 1) * P],
                                         wv[:, c, :], start=(c == 0), stop=(c == KC - 1))
                    if t % 2:
                        last.then_inc(front_filled[bank], 1)

            def scores(out, stationary, moving, mask, at):
                t_.matmul(out, stationary, moving, start=True, stop=False)
                return t_.matmul(out[:, at:at + P], identb[:], mask, start=False, stop=True)

            def back(b, p, nth, more):
                q, k = q_stack[p], k_stack[p]
                pe.wait_ge(stack_full[p], 16 * 12 * (nth + 1))

                def by_query(h, i, out):
                    return scores(out, q[0:STACK, h, i * P:(i + 1) * P], k[0:STACK, h, 0:(i + 1) * P],
                                  mask_q[:], i * P)

                def by_key(h, i, out):
                    return scores(out, k[:, h, i * P:(i + 1) * P], q[:, h, i * P:TOK], mask_k[:], 0)

                def pair_scores(pair, uses, blocks):
                    kind, four, one_and_three, two = blocks
                    for u in range(5):
                        pe.wait_ge(sc_freed[u], SC_USES[u] * b + uses + pair + 1)
                        h, bank = 2 * pair + u // 3, ps[:, SC + u, :]
                        if u in (0, 3):
                            last = kind(h, four, bank)
                        elif u in (1, 4):
                            for i, cols in one_and_three:
                                last = kind(h, i, bank[:, cols])
                        else:
                            kind(2 * pair, two, bank[:, 0:2 * P])
                            last = kind(2 * pair + 1, two, bank[:, 2 * P:])
                        last.then_inc(sc_filled[u], 1)
                    return last

                for pair in range(PAIRS):
                    pair_scores(pair, 0, (by_query, 3, ((0, slice(0, P)), (2, slice(P, 4 * P))), 1))
                pe.wait_ge(sc_freed[4], SC_USES[4] * b + PAIRS + 1)
                pe.wait_ge(attn_ready, 4 * b + 1)
                t_.transpose(ps[:, PVB, 0:P], neg_max[:].rearrange("p h t -> p (h t)"),
                             ident[:]).then_inc(pv_filled, 1)
                pe.wait_ge(max_rows_full[p], 32 * (nth + 1))

                def outputs(g, blocks):
                    pe.wait_ge(sc_freed[4], SC_USES[4] * b + PAIRS + 2 * g + 2 + 1)
                    if 0 in blocks:
                        pe.wait_ge(attn_ready, 4 * b + g + 1)
                    for i in blocks:
                        for j in range(4):
                            h, slot = 4 * g + j, (2 * g + j // 2) % 4
                            u0 = 3 * (j % 2)
                            src = {0: (u0, slice(0, TOK)), 1: (u0 + 1, slice(0, 3 * P)),
                                   2: (2, slice((j % 2) * 2 * P, (j % 2 + 1) * 2 * P)),
                                   3: (u0 + 1, slice(3 * P, TOK))}[i]
                            last = t_.matmul(ps[VW * j:VW * (j + 1), PVB, i * P:TOK], values[p][:, i, h, :],
                                             probs[:, slot, src[0], src[1]], start=(i == 0), stop=(i == NT - 1))
                    return last

                def transposed(g):
                    pe.wait_ge(heads_ready, 4 * b + g + 1)
                    for t in range(NT):
                        last = t_.transpose(ps[:, PVB, t * P:(t + 1) * P], heads_out[:, t * P:(t + 1) * P], ident[:])
                    last.then_inc(pv_filled, 1)

                for pair in range(PAIRS):
                    last = pair_scores(pair, PAIRS, (by_key, 0, ((1, slice(0, 3 * P)), (3, slice(3 * P, TOK))), 2))
                    if pair >= 2 and pair % 2 == 0:
                        outputs(pair // 2 - 1, (0, 1))
                    if pair >= 3 and pair % 2:
                        outputs(pair // 2 - 1, (2, 3)).then_inc(pv_filled, 1)
                        transposed(pair // 2 - 1)
                outputs(3, range(NT)).then_inc(pv_filled, 1)
                transposed(3)
                pe.wait_ge(attn_ready, 4 * b + 4 + 1)
                for c in range(KC):
                    pe.wait_ge(sc_freed[c], SC_USES[c] * (b + 1) - 1 + 1)
                    for t in range(NT):
                        last = t_.transpose(ps[:, SC + c, t * P:(t + 1) * P], attn[:, t, c * P:(c + 1) * P], ident[:])
                    last.then_inc(sc_filled[c], 1)
                for c in range(KC):
                    pe.wait_ge(sc_freed[c], SC_USES[c] * (b + 1) + 1)
                for t in range(NT):
                    u = 2 + t // 2
                    if t % 2 == 0:
                        pe.wait_ge(sc_freed[u], SC_USES[u] * (b + 1) - 1 + 1)
                    for c in range(KC):
                        last = t_.matmul(ps[:, SC + u, (t % 2) * D:(t % 2 + 1) * D], attnT[:, c, t * P:(t + 1) * P],
                                         wo[:, c, :], start=(c == 0), stop=(c == KC - 1))
                    if t % 2:
                        last.then_inc(sc_filled[u], 1)

            sequences(pe, front, back)
def experts(nc, w, normed_dram, out):
    with ExitStack() as ctx:
        def sb(name, shape, dt):
            return ctx.enter_context(nc.sbuf_tensor(name, shape, dt))

        primed = []

        def sem(name, start=0):
            s = ctx.enter_context(nc.semaphore(name))
            if start:
                primed.append((s, start))
            return s

        GROUPS, PAIR = SEQS, 2
        ps = ctx.enter_context(nc.psum_tensor("exp_ps", [P, 8, 512], F32))

        def ctrl_ps(s):
            return ps[:, 2 + 2 * s:4 + 2 * s, :].rearrange("p a n -> p (a n)")

        w1 = sb("w1", [P, 2, 2 * KC, HCOLS], F16)
        w2 = sb("w2", [P, 2, EC, CTRL], F16)
        w2_shared_top = sb("w2_shared_top", [P, CTRL], F16)
        w2_shared_low = sb("w2_shared_low", [P, CTRL], F16)
        b2_parts = sb("b2_parts", [P, CTRL], F16)
        rf1 = sb("rf1", [P, 2, KC, RH], F16)
        rf2 = sb("rf2", [P, 2, RC, D], F16)
        wrh = sb("wrh", [P, KC, P], F32)
        w2rh = sb("w2rh", [P, E + 1], F32)
        b1 = sb("b1", [P, FC], F32)
        rf_b1 = sb("rf_b1", [P, RC], F32)
        brh = sb("brh", [P, 1], F32)
        b2rh = sb("b2rh", [P, E + 1], F32)
        mu = sb("mu", [P, D], F32)
        iw = sb("iw", [P, D], F32)
        rf_b2 = sb("rf_b2", [P, D], F32)
        half = sb("half", [P, 1], F32)
        gate_in = sb("gate_in", [P, 1], F32)
        gate_t = sb("gate_t", [P, 1], F32)
        gate = sb("gate", [P, 2], F32)
        ident = sb("e_ident", [P, P], F32)
        identb = sb("e_identb", [P, P], F16)
        spread = sb("spread", [P, EC, P], F16)
        numbers = sb("numbers", [P, 3, E], F32)

        def two(name, shape, dt):
            return [sb(f"{name}{g}", shape, dt) for g in range(PAIR)]

        x1 = two("x1", [P, NT, D], F32)
        x2 = two("x2", [P, NT, D], F32)
        vh = two("vh", [P, NT, D], F32)
        xTp = two("xTp", [P, 2, KC, TOK], F16)
        vTp = two("vTp", [P, 2, KC, TOK], F16)
        onehot = two("onehot", [P, NT, 2, 3, E], F16)
        onehotT = two("onehotT", [P, 2, TOK], F16)
        masks = two("masks", [P, 2, EC, TOK], F16)
        weights = two("weights", [P, NT, STREAMS], F32)
        nw = two("nw", [P, NT, STREAMS], F32)
        nwx = two("nwx", [P, NT, STREAMS], F32)
        xT32 = sb("xT32", [P, KC, TOK], F32)
        xm = sb("xm", [P, NT, D], F32)
        v_or_res = sb("v_or_res", [P, KC * TOK], F32)
        vT32 = v_or_res[:].rearrange("p (c n) -> p c n", c=KC)
        res = v_or_res[:].rearrange("p (t d) -> p t d", t=NT)
        rh = sb("rh", [P, TOK], F32)
        g32 = sb("g32", [P, FC, TOK], F32)
        gp = sb("gp", [P, 2, EC, TOK], F16)
        routed = sb("routed", [P, 2, 2, EC, TOK], F16)
        shared_hl = sb("shared_hl", [P, TOK], F16)
        shared_h1 = sb("shared_h1", [P, TOK], F16)
        ctrl = sb("ctrl", [P, NT, STREAMS, CTRL], F32)
        sp = sb("sp", [P, NT, STREAMS, D], F32)
        logits = sb("logits", [P, NT, E + 1], F32)
        top = sb("top", [P, NT, 8], F32)
        top_at = sb("top_at", [P, NT, 8], U32)
        top_f = sb("top_f", [P, NT, 2], F32)
        gates = sb("gates", [P, NT, 2], F32)
        gates_t = sb("gates_t", [P, NT, 2], F32)
        halt = sb("halt", [P, NT], F32)
        norm = norm_buffers(sb, "exp")
        final = sb("final", [P, NT, D], F32)

        loaded = sem("loaded")
        const_step = sem("e_const_step")
        consts = sem("e_consts")
        setup_step = sem("setup_step")
        gate_ready = sem("gate_ready")
        biases_split = sem("biases_split")
        weights_ready = sem("weights_ready")
        rows_in = sem("rows_in")
        x_full = [sem(f"e_x_full{g}") for g in range(PAIR)]
        ring_filled = [sem(f"ring_filled{i}") for i in range(2)]
        ring_freed = [sem(f"ring_freed{i}", 1) for i in range(2)]
        ctrl_filled = [sem(f"ctrl_filled{s}") for s in range(STREAMS)]
        ctrl_freed = [sem(f"ctrl_freed{s}", 1) for s in range(STREAMS)]
        xlow_ready = sem("xlow_ready", 1)
        vlow_ready = sem("vlow_ready", 1)
        gates_ready = sem("gates_ready")
        gates_done = sem("gates_done")
        weights_done = sem("weights_done")
        onehot_ready = sem("onehot_ready")
        h_ready = sem("h_ready", 1)
        tanh_done = sem("tanh_done")
        abs_ready = sem("abs_ready")
        ln_ready = sem("ln_ready")
        xm_ready = sem("xm_ready")
        spx_ready = sem("spx_ready", 1)
        pool_step = sem("pool_step")
        tile_done = sem("tile_done", NT)
        dve_step = sem("dve_step")
        norm_sems = (sem("e_var_ready"), sem("e_rstd_step"), sem("e_rstd_raw"))
        res_ready = sem("e_res_ready")
        final_ready = sem("final_ready")
        final_stored = sem("final_stored", 1)

        STAGES = [(1, 0), (1, 1), (2, 0), (2, 1), (3, 0), (3, 1)]
        fills = []
        for it, g in STAGES:
            names = ["x0", "x1"]
            if it == 1:
                names += ["rh", "h4", "logits", "h0", "onehot", "h1", "mask00", "mask10", "mask01", "mask11",
                          "h2", "mask02", "mask12", "h3", "mask03", "mask13"]
            elif it == 2:
                names += ["v0", "v1", "rh", "h4", "logits", "h0", "h1", "h2", "h3"]
            else:
                names += ["h0", "h1", "h2", "h3"]
            fills += [(it, g, n) for n in names]
        assert len(fills) % 2 == 0
        FILLS = len(fills) // 2
        place = {f: (n % 2, n // 2) for n, f in enumerate(fills)}

        def before(it, g, of):
            return sum(of(*s) for s in STAGES[:STAGES.index((it, g))])

        def hs(it, g):
            return FC if it < 3 else RC

        H_ROUND = sum(hs(*s) for s in STAGES)
        CTRL_ROUND = [4 * NT + (PAIR if s < 2 else 0) for s in range(STREAMS)]

        LOAD_COUNT = 3 * 2 * KC + 3 * 5 + 10 + 6 + 2
        block = ctx.enter_context(nc.Block())
        x_dram = normed_dram.rearrange("s (t p) d -> s p t d", p=P)
        out_dram = out.rearrange("s (t p) d -> s p t d", p=P)
        stage = ctrl[:].rearrange("p t s n -> p (t s n)")
        at = 0

        def staged(shape):
            nonlocal at
            n = shape[0] * shape[1]
            view = stage[:, at:at + n].rearrange("p (a b) -> p a b", a=shape[0])
            at += n
            return view

        w1_32, w2_32, w2s_32 = staged((2 * KC, HCOLS)), staged((EC, CTRL)), staged((1, CTRL))
        rf1_32, rf2_32, b2_32 = staged((KC, RH)), staged((RC, D)), staged((1, CTRL))
        b2e32, b2s32 = b2_32[0:E, 0, :], b2_32[32:33, 0, :]
        b2_split = sp[:].rearrange("p t s d -> p (t s d)").bitcast(F16)[:, 0:3 * CTRL].rearrange(
            "p (a n) -> p a n", a=3)
        b2e_split, b2s_split = b2_split[0:E], b2_split[32:33]
        COLUMNS = ((0, 0), (1, 2), (2, 1))

        ROUNDS = GROUPS // PAIR

        def rounds(eng, body):
            with eng.Fori(0, ROUNDS - 1) as i:
                body(i, True)
            body(ROUNDS - 1, False)

        def after(i, it, g, more):
            at = STAGES.index((it, g)) + 1
            if at < len(STAGES):
                return (i, *STAGES[at])
            return (i + 1, *STAGES[0]) if more else None

        @block.sync
        def _(sync):
            for s, start in primed:
                sync.sem_inc(s, start)
            count = 0

            def load(dst, src):
                nonlocal count
                count += 1
                sync.dma_start(dst, src).then_inc(loaded, 16)

            for g in range(PAIR):
                sync.dma_start(x1[g][:], x_dram[g]).then_inc(x_full[g], 16)
            for c in range(2 * KC):
                load(w1_32[:, c, 0:E * HID].rearrange("p (e h) -> p e h", h=HID),
                     w["expert_w1"].rearrange("e (c p) h -> c p e h", p=P)[c])
                for r in range(2):
                    load(w1_32[:, c, E * HID + r * HID:E * HID + (r + 1) * HID],
                         w["shared_w1"][c * P:(c + 1) * P, :])
            w2_rows = w["expert_w2"].rearrange("e h n -> (e h) n").rearrange("(c p) n -> p c n", p=P)
            for dst, src in COLUMNS:
                d, s = slice(dst * D, (dst + 1) * D), slice(src * D, (src + 1) * D)
                load(w2_32[:, :, d], w2_rows[:, :, s])
                for r in range(2):
                    load(w2s_32[r * HID:(r + 1) * HID, 0, d], w["shared_w2"][:, s])
                load(b2e32[:, d], w["expert_b2"][:, s])
                load(b2s32[:, d], w["shared_b2"][s].unsqueeze(0))
            load(rf1_32, w["refine_w1"].rearrange("(c p) n -> p c n", p=P))
            load(rf2_32, w["refine_w2"].rearrange("(c p) n -> p c n", p=P))
            load(wrh[:, :, 0:HID], w["router_w1"].rearrange("(c p) n -> p c n", p=P))
            load(wrh[:, :, HID:P], w["halt_w1"].rearrange("(c p) n -> p c n", p=P))
            load(b2rh[:, 0:E], w["router_b2"].partition_broadcast(P))
            load(b2rh[:, E:E + 1], w["halt_b2"].partition_broadcast(P))
            load(mu[:], w["mu"].partition_broadcast(P))
            load(iw[:], w["integration_weight"].partition_broadcast(P))
            load(rf_b2[:], w["refine_b2"].partition_broadcast(P))
            load(gate_in[:], w["shared_weight"].partition_broadcast(P))
            with nc.allow_non_contiguous_dma(reason="biases as columns"):
                load(b1[:, 0:EC], w["expert_b1"].rearrange("e h -> (e h)").rearrange("(c p) -> p c", p=P))
                for r in range(2):
                    load(b1[r * HID:(r + 1) * HID, EC:FC], w["shared_b1"].unsqueeze(1))
                load(rf_b1[:], w["refine_b1"].rearrange("(c p) -> p c", p=P))
                load(brh[0:HID, :], w["router_b1"].unsqueeze(1))
                load(brh[HID:P, :], w["halt_b1"].unsqueeze(1))
            sync.wait_ge(consts, 1)
            load(w2rh[0:HID, 0:E], w["router_w2"])
            load(w2rh[HID:P, E:E + 1], w["halt_w2"])
            assert count == LOAD_COUNT, count
            sync.wait_ge(biases_split, 1)
            for part in range(3):
                sync.dma_start(w2_shared_low[HID + part:HID + part + 1, :],
                               b2s_split[:, part, :]).then_inc(rows_in, 16)
                sync.dma_start(b2_parts[part * E:(part + 1) * E, :], b2e_split[:, part, :]).then_inc(rows_in, 16)

            def store(i, g):
                sync.wait_ge(final_ready, PAIR * i + g + 1)
                sync.dma_start(out_dram[PAIR * i + g], final[:]).then_inc(final_stored, 16)

            def reload(i, g):
                sync.wait_ge(res_ready, 2 * (PAIR * i + g) + 2)
                sync.dma_start(x1[g][:], x_dram[PAIR * (i + 1) + g]).then_inc(x_full[g], 16)

            with sync.Fori(0, GROUPS // PAIR - 1) as i:
                for g in range(PAIR):
                    reload(i, g)
                    store(i, g)
            for g in range(PAIR):
                store(GROUPS // PAIR - 1, g)
            sync.wait_ge(final_stored, 16 * GROUPS + 1)

        @block.gpsimd
        def _(pool):
            steps = Steps(0, 0)
            gp_ = nc.gpsimd
            gp_.memset(w2rh[:], 0.0).then_inc(consts, 1)
            pool.wait_ge(consts, 1)
            gp_.memset(ident[:], 1.0).then_inc(const_step, 1)
            pool.wait_ge(const_step, steps.next())
            gp_.affine_select(out=ident[:], in_=ident[:], compare_op=ALU.is_equal, fill=0.0,
                              base=0, pattern=[[-1, P]], channel_multiplier=1).then_inc(const_step, 1)
            pool.wait_ge(const_step, steps.next())
            gp_.tensor_copy(identb[:], ident[:]).then_inc(const_step, 1)
            pool.wait_ge(const_step, steps.next())
            gp_.memset(half[:], 0.5).then_inc(const_step, 1)
            pool.wait_ge(const_step, steps.next())
            gp_.memset(spread[:], 1.0).then_inc(const_step, 1)
            pool.wait_ge(const_step, steps.next())
            gp_.affine_select(out=spread[:], in_=spread[:], compare_op=ALU.is_equal, fill=0.0, base=0,
                              pattern=[[-2, EC], [-1, 2], [0, HID]], channel_multiplier=1).then_inc(const_step, 1)
            pool.wait_ge(const_step, steps.next())
            for e in range(E):
                gp_.memset(numbers[:, :, e:e + 1], float(e)).then_inc(const_step, 1)
                pool.wait_ge(const_step, steps.next())
            for g in range(PAIR):
                gp_.memset(onehotT[g][:], 0.0).then_inc(const_step, 1)
                pool.wait_ge(const_step, steps.next())
            gp_.memset(b2_parts[:], 0.0).then_inc(const_step, 1)
            pool.wait_ge(const_step, steps.next())
            gp_.memset(w2_shared_low[:], 0.0).then_inc(const_step, 1)
            pool.wait_ge(const_step, steps.next())
            gp_.memset(shared_h1[:], 1.0).then_inc(consts, 1)
            pool.wait_ge(consts, 2)
            pool.wait_ge(loaded, 16 * LOAD_COUNT)

            def elementwise(i, it, g):
                n = 4 * i + before(it, g, lambda *s: 1)
                if it == 1:
                    pool.wait_ge(x_full[g], 16 * (i + 1))
                else:
                    pool.wait_ge(tile_done, NT * (n - 1) + NT)
                pool.wait_ge(spx_ready, NT * n + 1)
                src = x1 if it == 1 else x2
                gp_.tensor_tensor(xm[:], src[g][:], mu[:].unsqueeze(1).to_broadcast([P, NT, D]),
                                  ALU.subtract).then_inc(xm_ready, 1)
                pool.wait_ge(xm_ready, n + 1)
                for t in range(NT):
                    pool.wait_ge(ln_ready, NT * n + t + 1)
                    gp_.tensor_tensor(sp[:, t], sp[:, t], ctrl[:, t, :, 2 * D:], ALU.subtract).then_inc(pool_step, 1)
                    pool.wait_ge(pool_step, NT * n + t + 1)
                    gp_.tensor_tensor(sp[:, t], sp[:, t], xm[:, t, :].unsqueeze(1).to_broadcast([P, STREAMS, D]),
                                      ALU.mult).then_inc(spx_ready, 1)

            def body(i, more):
                for it, g in STAGES:
                    if it < 3:
                        elementwise(i, it, g)

            rounds(pool, body)

        @block.scalar
        def _(act):
            nc.scalar.preload_act_table_set("gelu_and_others")
            act.wait_ge(loaded, 16 * LOAD_COUNT)
            nc.scalar.activation(gate_t[:], gate_in[:], ACT.Tanh, scale=0.5).then_inc(gate_ready, 1)

            def filled(i, it, g, what):
                bank, use = place[it, g, what]
                act.wait_ge(ring_filled[bank], FILLS * i + use + 1)
                return ps[:, bank, :], ring_freed[bank]

            def transposed(i, it, g):
                n = 6 * i + before(it, g, lambda *s: 1)
                act.wait_ge(xlow_ready, n + 1)
                for c in range(KC):
                    src, free = filled(i, it, g, f"x{c}")
                    nc.scalar.copy(xT32[:, c, :], src)
                    nc.scalar.copy(xTp[g][:, 0, c, :], src).then_inc(free, 1)
                if it == 2:
                    act.wait_ge(vlow_ready, 2 * i + g + 1)
                    for c in range(KC):
                        src, free = filled(i, it, g, f"v{c}")
                        nc.scalar.copy(vT32[:, c, :], src)
                        nc.scalar.copy(vTp[g][:, 0, c, :], src).then_inc(free, 1)

            def gelu(i, it, g, c):
                bias = b1 if it < 3 else rf_b1
                src, free = filled(i, it, g, f"h{c}")
                nc.scalar.activation(g32[:, c, :], src, ACT.Gelu, bias=bias[:, c:c + 1])
                high = shared_hl[:] if c == EC else gp[:, 0, c, :]
                nc.scalar.activation(high, src, ACT.Gelu, bias=bias[:, c:c + 1]).then_inc(free, 1)

            def softplus_logs(i, it, g, tiles):
                n = 4 * i + before(it, g, lambda *s: 1)
                nc.scalar.preload_act_table_set("natural_log_exp_and_others")
                for t in tiles:
                    act.wait_ge(abs_ready, STREAMS * (NT * n + t + 1))
                    b = ctrl[:, t, :, 2 * D:]
                    nc.scalar.activation(b, b, ACT.Ln, scale=0.5, bias=half[:, 0:1]).then_inc(ln_ready, 1)
                nc.scalar.preload_act_table_set("gelu_and_others")

            def tanhs(i, it, g, t):
                n = 4 * i + before(it, g, lambda *s: 1)
                act.wait_ge(tile_done, NT * (n - 1) + t + 1 + NT)
                for s in range(STREAMS):
                    act.wait_ge(ctrl_filled[s], CTRL_ROUND[s] * i + NT * before(it, g, lambda *s: 1) + t + 1)
                    cols = slice(0, CTRL) if it == 2 else slice(D, CTRL)
                    width = CTRL if it == 2 else 2 * D
                    nc.scalar.activation(ctrl[:, t, s, cols], ctrl_ps(s)[:, 0:width], ACT.Tanh,
                                         scale=0.5).then_inc(tanh_done, 1)

            def body(i, more):
                for it, g in STAGES:
                    n = 4 * i + before(it, g, lambda *s: 1)
                    nxt = after(i, it, g, more)
                    if it < 3:
                        src, free = filled(i, it, g, "rh")
                        nc.scalar.activation(rh[:], src, ACT.Gelu, bias=brh[:, 0:1]).then_inc(free, 1)
                    act.wait_ge(h_ready, H_ROUND * i + before(it, g, hs) + 1)
                    if it == 3 and g == 1:
                        act.wait_ge(ctrl_filled[1], CTRL_ROUND[1] * i + 4 * NT + 1)
                    if it < 3:
                        gelu(i, it, g, EC)
                        gelu(i, it, g, 0)
                        act.wait_ge(gates_ready, n + 1)
                        nc.scalar.activation(gates_t[:], gates[:], ACT.Tanh, scale=0.5).then_inc(gates_done, 1)
                    else:
                        gelu(i, it, g, 0)
                    for c in range(1, EC if it < 3 else RC):
                        gelu(i, it, g, c)
                        if it == 1:
                            for m in ((0, 1) if c == 1 else (c,)):
                                src, free = filled(i, it, g, f"mask0{m}")
                                nc.scalar.copy(masks[g][:, 0, m, :], src).then_inc(free, 1)
                    if (it, g) in ((1, 1), (2, 0), (2, 1), (3, 0)):
                        softplus_logs(i, *STAGES[STAGES.index((it, g)) - 1], (2, 3))
                    if it < 3:
                        tanhs(i, it, g, 0)
                        tanhs(i, it, g, 1)
                        softplus_logs(i, it, g, (0, 1))
                        tanhs(i, it, g, 2)
                        transposed(*nxt)
                        tanhs(i, it, g, 3)
                    else:
                        if nxt:
                            transposed(*nxt)
                        nc.scalar.preload_act_table_set("natural_log_exp_and_others")
                        rsqrt_guess(act, nc, norm, norm_sems, PAIR * i + g)
                        nc.scalar.preload_act_table_set("gelu_and_others")

            transposed(0, *STAGES[0])
            rounds(act, body)

        DVE_ROUND = PAIR * (6 + EC + 3 * NT) + PAIR * (2 + 1 + EC + 5 * NT) + PAIR * (1 + NORM_STEPS)

        @block.vector
        def _(dve):
            v = nc.vector
            setup = Steps(0, 0)
            dve.wait_ge(loaded, 16 * LOAD_COUNT)
            dve.wait_ge(consts, 2)
            v.tensor_copy(w1[:, 0], w1_32)
            v.tensor_copy(w2[:, 0], w2_32)
            v.tensor_copy(w2_shared_top[:], w2s_32[:, 0, :])
            v.tensor_copy(rf1[:, 0], rf1_32)
            v.tensor_copy(rf2[:, 0], rf2_32)
            v.tensor_copy(b2e_split[:, 0, :], b2e32)
            v.tensor_copy(b2s_split[:, 0, :], b2s32).then_inc(setup_step, 1)
            dve.wait_ge(setup_step, setup.next())
            v.tensor_tensor(b2e32, b2e32, b2e_split[:, 0, :], ALU.subtract)
            v.tensor_tensor(b2s32, b2s32, b2s_split[:, 0, :], ALU.subtract).then_inc(setup_step, 1)
            dve.wait_ge(setup_step, setup.next())
            v.tensor_copy(b2e_split[:, 1, :], b2e32)
            v.tensor_copy(b2s_split[:, 1, :], b2s32).then_inc(setup_step, 1)
            dve.wait_ge(setup_step, setup.next())
            v.tensor_tensor(b2e_split[:, 2, :], b2e32, b2e_split[:, 1, :], ALU.subtract)
            v.tensor_tensor(b2s_split[:, 2, :], b2s32, b2s_split[:, 1, :],
                            ALU.subtract).then_inc(biases_split, 1)
            v.tensor_tensor(w1[:, 1], w1_32, w1[:, 0], ALU.subtract)
            v.tensor_tensor(w2[:, 1], w2_32, w2[:, 0], ALU.subtract)
            v.tensor_tensor(w2_shared_low[0:HID, :], w2s_32[0:HID, 0, :], w2_shared_top[0:HID, :], ALU.subtract)
            v.tensor_tensor(rf1[:, 1], rf1_32, rf1[:, 0], ALU.subtract)
            v.tensor_tensor(rf2[:, 1], rf2_32, rf2[:, 0], ALU.subtract).then_inc(weights_ready, 1)
            dve.wait_ge(weights_ready, 1)
            dve.wait_ge(gate_ready, 1)
            v.tensor_scalar(gate[:, 0:1], gate_t[:], 0.5, 0.5, ALU.mult, ALU.add)
            v.tensor_scalar(gate[:, 1:2], gate_t[:], -0.5, 0.5, ALU.mult, ALU.add).then_inc(setup_step, 1)
            dve.wait_ge(setup_step, setup.next())

            def filled(i, it, g, what):
                bank, use = place[it, g, what]
                dve.wait_ge(ring_filled[bank], FILLS * i + use + 1)
                return ps[:, bank, :], ring_freed[bank]

            def freed(i, it, g, what):
                bank, use = place[it, g, what]
                dve.wait_ge(ring_freed[bank], FILLS * i + use + 1 + 1)

            def low_parts(i, it, g):
                freed(i, it, g, "x0")
                freed(i, it, g, "x1")
                v.tensor_tensor(xTp[g][:, 1], xT32[:], xTp[g][:, 0], ALU.subtract).then_inc(xlow_ready, 1)
                if it == 2:
                    freed(i, it, g, "v0")
                    freed(i, it, g, "v1")
                    v.tensor_tensor(vTp[g][:, 1], vT32[:], vTp[g][:, 0], ALU.subtract).then_inc(vlow_ready, 1)

            def route(i, it, g, chain):
                n = 4 * i + before(it, g, lambda *s: 1)
                src, free = filled(i, it, g, "logits")
                v.tensor_tensor(logits[:], src[:, 0:NT * 16].rearrange("p (t c) -> p t c", t=NT)[:, :, 0:E + 1],
                                b2rh[:].unsqueeze(1).to_broadcast([P, NT, E + 1]), ALU.add).then_inc(free, 1)
                freed(i, it, g, "logits")
                if it == 1:
                    v.memset(top_f[:], 0.0)
                    for t in range(NT):
                        last = v.max(top[:, t, :], logits[:, t, 0:E])
                    last.then_inc(dve_step, 1)
                    dve.wait_ge(dve_step, chain.next())
                    v.tensor_tensor(gates[:, :, 0], top[:, :, 0], top[:, :, 1], ALU.subtract)
                v.tensor_copy(gates[:, :, 1], logits[:, :, E]).then_inc(gates_ready, 1)
                if it == 1:
                    for t in range(NT):
                        last = v.max_index(top_at[:, t, :], top[:, t, :], logits[:, t, 0:E])
                    last.then_inc(dve_step, 1)
                    dve.wait_ge(dve_step, chain.next())
                    v.tensor_copy(top_f[:], top_at[:, :, 0:2]).then_inc(dve_step, 1)
                    dve.wait_ge(dve_step, chain.next())
                    for t in range(NT):
                        for k in range(2):
                            last = v.tensor_scalar(onehot[g][:, t, k], numbers[:], top_f[:, t, k:k + 1], None,
                                                   ALU.is_equal)
                    last.then_inc(onehot_ready, 1)

            def stream_weights(i, it, g, chain):
                n = 4 * i + before(it, g, lambda *s: 1)
                dve.wait_ge(gates_done, n + 1)
                if it == 1:
                    v.tensor_scalar(weights[g][:, :, 1], gates_t[:, :, 0], 0.5, 0.5, ALU.mult, ALU.add)
                    v.tensor_scalar(weights[g][:, :, 2], gates_t[:, :, 0], -0.5, 0.5, ALU.mult,
                                    ALU.add).then_inc(dve_step, 1)
                    dve.wait_ge(dve_step, chain.next())
                    v.tensor_scalar(weights[g][:, :, 1:3], weights[g][:, :, 1:3], gate[:, 1:2], None, ALU.mult)
                    v.tensor_copy(weights[g][:, :, 0], gate[:, 0:1].to_broadcast([P, NT]))
                v.tensor_scalar(halt[:], gates_t[:, :, 1], -0.5, -0.5, ALU.mult, ALU.add).then_inc(dve_step, 1)
                dve.wait_ge(dve_step, chain.next())
                v.tensor_tensor(nw[g][:], weights[g][:], halt[:].unsqueeze(2).to_broadcast([P, NT, STREAMS]),
                                ALU.mult).then_inc(dve_step, 1)
                dve.wait_ge(dve_step, chain.next())
                v.tensor_scalar(nwx[g][:], nw[g][:], 0.5 * DT, None, ALU.mult).then_inc(weights_done, 1)
                dve.wait_ge(weights_done, n + 1)

            def hidden(i, it, g, chain):
                freed(i, it, g, f"h{EC}")
                v.tensor_copy(shared_h1[0:HID, :], shared_hl[0:HID, :])
                v.tensor_tensor(shared_hl[HID:P, :], g32[HID:P, EC, :], shared_hl[HID:P, :],
                                ALU.subtract).then_inc(h_ready, 1)
                if it == 1:
                    src, free = filled(i, it, g, "onehot")
                    v.tensor_copy(onehotT[g][0:3 * E].rearrange("p k n -> p (k n)"),
                                  src[0:3 * E, :].bitcast(F16)).then_inc(free, 1)
                for c in range(EC):
                    freed(i, it, g, f"h{c}")
                    v.tensor_tensor(gp[:, 1, c, :], g32[:, c, :], gp[:, 0, c, :], ALU.subtract).then_inc(dve_step, 1)
                    dve.wait_ge(dve_step, chain.next())
                    if it == 1:
                        freed(i, it, g, f"mask0{c}")
                        src, free = filled(i, it, g, f"mask1{c}")
                        v.tensor_copy(masks[g][:, 1, c, :], src).then_inc(free, 1)
                        freed(i, it, g, f"mask1{c}")
                    for k in range(2):
                        last = v.tensor_tensor(routed[:, k, :, c, :], gp[:, :, c, :],
                                               masks[g][:, k, c, :].unsqueeze(1).to_broadcast([P, 2, TOK]), ALU.mult)
                    last.then_inc(h_ready, 1)

            def control(i, it, g, t):
                n = 4 * i + before(it, g, lambda *s: 1)
                for s in range(STREAMS):
                    dve.wait_ge(tanh_done, STREAMS * (NT * n + t) + s + 1)
                    at_b = 2 * D if it == 2 else D
                    v.tensor_scalar(sp[:, t, s, :], ctrl_ps(s)[:, at_b:at_b + D], 0.0, None,
                                    ALU.max).then_inc(ctrl_freed[s], 1)
                    b = ctrl[:, t, s, 2 * D:]
                    v.scalar_tensor_tensor(b, b, -1.0, b, ALU.mult, ALU.max).then_inc(abs_ready, 1)

            def update(i, it, g, t, chain):
                n = 4 * i + before(it, g, lambda *s: 1)
                a, gg = ctrl[:, t, :, 0:D], ctrl[:, t, :, D:2 * D]
                dve.wait_ge(spx_ready, NT * n + t + 1 + 1)
                if it == 2:
                    v.scalar_tensor_tensor(a, a, 1.0, vh[g][:, t, :].unsqueeze(1).to_broadcast(
                 [P, STREAMS, D]), ALU.add, ALU.mult).then_inc(dve_step, 1)
                    dve.wait_ge(dve_step, chain.next())
                    v.tensor_tensor(sp[:, t], sp[:, t], a, ALU.subtract).then_inc(dve_step, 1)
                    dve.wait_ge(dve_step, chain.next())
                v.scalar_tensor_tensor(gg, gg, 1.0, sp[:, t], ALU.add, ALU.mult).then_inc(dve_step, 1)
                dve.wait_ge(dve_step, chain.next())
                src = x1 if it == 1 else x2
                x_new, v_new = x2[g][:, t, :], vh[g][:, t, :]
                for s in range(STREAMS):
                    if it == 1:
                        if s == 0:
                            v.tensor_scalar(v_new, sp[:, t, s, :], nw[g][:, t, s:s + 1], None, ALU.mult)
                        else:
                            v.scalar_tensor_tensor(v_new, sp[:, t, s, :], nw[g][:, t, s:s + 1], v_new,
                                                   ALU.mult, ALU.add)
                    last = v.scalar_tensor_tensor(x_new, ctrl[:, t, s, D:2 * D], nwx[g][:, t, s:s + 1],
                                                  src[g][:, t, :] if s == 0 else x_new, ALU.mult, ALU.add)
                    if s < 2:
                        last.then_inc(dve_step, 1)
                        dve.wait_ge(dve_step, chain.next())
                last.then_inc(tile_done, 1)

            def halve(i, g, chain):
                freed(i, 2, g, "v1")
                v.tensor_scalar(vh[g][:], vh[g][:], 0.5, None, ALU.mult).then_inc(dve_step, 1)
                dve.wait_ge(dve_step, chain.next())

            def refined_hidden(i, g):
                for c in range(RC):
                    freed(i, 3, g, f"h{c}")
                    v.tensor_tensor(gp[:, 1, c, :], g32[:, c, :], gp[:, 0, c, :], ALU.subtract).then_inc(h_ready, 1)

            def refine(i, g, chain):
                n = PAIR * i + g
                for u in range(2):
                    s = slice(2 * u, 2 * u + 2)
                    dve.wait_ge(ctrl_filled[u], CTRL_ROUND[u] * i + 4 * NT + g + 1)
                    v.tensor_tensor(res[:, s, :], ctrl_ps(u)[:, 0:2 * D].rearrange("p (t d) -> p t d", d=D),
                                    rf_b2[:].unsqueeze(1).to_broadcast([P, 2, D]), ALU.add).then_inc(ctrl_freed[u], 1)
                dve.wait_ge(ctrl_freed[1], CTRL_ROUND[1] * i + 4 * NT + g + 1 + 1)
                v.tensor_tensor(res[:], res[:], iw[:].unsqueeze(1).to_broadcast([P, NT, D]), ALU.mult).then_inc(dve_step, 1)
                dve.wait_ge(dve_step, chain.next())
                for u in range(2):
                    s = slice(2 * u, 2 * u + 2)
                    v.scalar_tensor_tensor(res[:, s, :], x1[g][:, s, :], 2.0, res[:, s, :], ALU.mult,
                                           ALU.add).then_inc(res_ready, 1)
                dve.wait_ge(res_ready, 2 * n + 2)
                layer_norm(dve, nc, dve_step, chain, res, norm, norm_sems, n)
                dve.wait_ge(final_stored, 16 * n + 1)
                normalised(nc, final, res, norm).then_inc(final_ready, 1)

            def body(i, more):
                chain = Steps(DVE_ROUND, i)
                for it, g in STAGES:
                    nxt = after(i, it, g, more)
                    earlier = STAGES[STAGES.index((it, g)) - 1]
                    if it == 3:
                        refined_hidden(i, g)
                        if g == 0:
                            update(i, *earlier, 2, chain)
                            update(i, *earlier, 3, chain)
                        if nxt:
                            low_parts(*nxt)
                        refine(i, g, chain)
                        continue
                    if it == 2:
                        halve(i, g, chain)
                    route(i, it, g, chain)
                    hidden(i, it, g, chain)
                    stream_weights(i, it, g, chain)
                    for t in range(NT):
                        control(i, it, g, t)
                        if t < 2:
                            if (it, g) != (1, 0):
                                update(i, *earlier, t + 2, chain)
                        else:
                            update(i, it, g, t - 2, chain)
                        if t == 2:
                            low_parts(*nxt)
                chain.end()

            low_parts(0, *STAGES[0])
            rounds(dve, body)

        @block.tensor
        def _(pe):
            t_ = nc.tensor
            pe.wait_ge(consts, 2)
            pe.wait_ge(loaded, 16 * LOAD_COUNT)
            pe.wait_ge(weights_ready, 1)
            pe.wait_ge(rows_in, 16 * 6)

            def ring(i, it, g, what):
                bank, use = place[it, g, what]
                pe.wait_ge(ring_freed[bank], FILLS * i + use + 1)
                return ps[:, bank, :], ring_filled[bank]

            def freed(i, it, g, what):
                bank, use = place[it, g, what]
                pe.wait_ge(ring_freed[bank], FILLS * i + use + 1 + 1)

            def transposes(i, it, g, name, src):
                for c in range(KC):
                    dst, done = ring(i, it, g, f"{name}{c}")
                    for t in range(NT):
                        last = t_.transpose(dst[:, t * P:(t + 1) * P], src[:, t, c * P:(c + 1) * P], ident[:])
                    last.then_inc(done, 1)

            def split_products(out, pairs):
                n = len(pairs)
                for j, (stationary, moving) in enumerate(pairs):
                    t_.matmul(out, stationary[0], moving[0], start=(j == 0), stop=False)
                    t_.matmul(out, stationary[1], moving[0], start=False, stop=False)
                    last = t_.matmul(out, stationary[0], moving[1], start=False, stop=(j == n - 1))
                return last

            def onehots(i, it, g):
                pe.wait_ge(onehot_ready, PAIR * i + g + 1)
                dst, done = ring(i, it, g, "onehot")
                dst = dst[0:3 * E, :].bitcast(F16)
                for k in range(2):
                    for t in range(NT):
                        last = t_.transpose(dst[:, (k * NT + t) * P:(k * NT + t + 1) * P],
                                            onehot[g][:, t, k].rearrange("p a e -> p (a e)"), identb[:])
                last.then_inc(done, 1)
                freed(i, it, g, "onehot")

            def chunk(i, it, g, c, moving):
                dst, done = ring(i, it, g, f"h{c}")
                cols = slice(c * P, (c + 1) * P)
                split_products(dst, [((w1[:, 0, j, cols], w1[:, 1, j, cols]), m)
                                     for j, m in enumerate(moving)]).then_inc(done, 1)

            def mask(i, it, g, k, c):
                dst, done = ring(i, it, g, f"mask{k}{c}")
                t_.matmul(dst, spread[:, c, :], onehotT[g][:, k, :], start=True, stop=True).then_inc(done, 1)

            def hidden(i, it, g):
                freed(i, it, g, "x0")
                freed(i, it, g, "x1")
                dst, done = ring(i, it, g, "rh")
                for c in range(KC):
                    last = t_.matmul(dst, wrh[:, c, :], xT32[:, c, :], start=(c == 0), stop=(c == KC - 1))
                last.then_inc(done, 1)
                pe.wait_ge(xlow_ready, 6 * i + before(it, g, lambda *s: 1) + 1 + 1)
                moving = [(xTp[g][:, 0, c, :], xTp[g][:, 1, c, :]) for c in range(KC)]
                if it == 2:
                    pe.wait_ge(vlow_ready, 2 * i + g + 1 + 1)
                    moving += [(vTp[g][:, 0, c, :], vTp[g][:, 1, c, :]) for c in range(KC)]
                chunk(i, it, g, EC, moving)
                freed(i, it, g, "rh")
                dst, done = ring(i, it, g, "logits")
                for t in range(NT):
                    last = t_.matmul(dst[:, 16 * t:16 * t + E + 1], rh[:, t * P:(t + 1) * P], w2rh[:],
                                     start=True, stop=True)
                last.then_inc(done, 1)
                chunk(i, it, g, 0, moving)
                if it == 1:
                    onehots(i, it, g)
                chunk(i, it, g, 1, moving)
                if it == 1:
                    for c in range(2):
                        mask(i, it, g, 0, c)
                        mask(i, it, g, 1, c)
                for c in range(2, EC):
                    chunk(i, it, g, c, moving)
                    if it == 1:
                        mask(i, it, g, 0, c)
                        mask(i, it, g, 1, c)

            def control(i, it, g, t):
                n = before(it, g, lambda *s: 1)
                h0 = H_ROUND * i + before(it, g, hs)
                cols = ((0, 2 * D), (2 * D, CTRL)) if it == 2 else ((D, CTRL),)
                tok = slice(t * P, (t + 1) * P)
                for s in range(STREAMS):
                    if t == 0 and s < 2:
                        pe.wait_ge(h_ready, h0 + (1 if s == 0 else FC) + 1)
                    pe.wait_ge(ctrl_freed[s], CTRL_ROUND[s] * i + NT * n + t + 1)
                    if s == 0:
                        terms = [(shared_hl[:, tok], w2_shared_top[:]), (shared_h1[:, tok], w2_shared_low[:])]
                    else:
                        k = s - 1
                        terms = [(onehotT[g][:, k, tok], b2_parts[:])]
                        for c in range(EC):
                            terms += [(routed[:, k, 0, c, tok], w2[:, 0, c, :]),
                                      (routed[:, k, 0, c, tok], w2[:, 1, c, :]),
                                      (routed[:, k, 1, c, tok], w2[:, 0, c, :])]
                    for j, (stationary, moving) in enumerate(terms):
                        for a, z in cols:
                            last = t_.matmul(ctrl_ps(s)[:, a - cols[0][0]:z - cols[0][0]], stationary,
                                             moving[:, a:z], start=(j == 0), stop=(j == len(terms) - 1))
                    last.then_inc(ctrl_filled[s], 1)

            def refine_hidden(i, g):
                pe.wait_ge(xlow_ready, 6 * i + before(3, g, lambda *s: 1) + 1 + 1)
                for c in range(RC):
                    dst, done = ring(i, 3, g, f"h{c}")
                    cols = slice(c * P, (c + 1) * P)
                    split_products(dst, [((rf1[:, 0, j, cols], rf1[:, 1, j, cols]),
                                          (xTp[g][:, 0, j, :], xTp[g][:, 1, j, :]))
                                         for j in range(KC)]).then_inc(done, 1)

            def refine_out(i, g):
                pe.wait_ge(h_ready, H_ROUND * i + before(3, g, hs) + RC + 1)
                for t in range(NT):
                    u, tok = t // 2, slice(t * P, (t + 1) * P)
                    if t % 2 == 0:
                        pe.wait_ge(ctrl_freed[u], CTRL_ROUND[u] * i + 4 * NT + g + 1)
                    last = split_products(ctrl_ps(u)[:, (t % 2) * D:(t % 2 + 1) * D],
                                          [((gp[:, 0, c, tok], gp[:, 1, c, tok]), (rf2[:, 0, c, :], rf2[:, 1, c, :]))
                                           for c in range(RC)])
                    if t % 2:
                        last.then_inc(ctrl_filled[u], 1)

            def transpose_state(i, it, g):
                if it == 1:
                    pe.wait_ge(x_full[g], 16 * (i + 1))
                else:
                    pe.wait_ge(tile_done, NT * (4 * i + PAIR * (it - 2) + g + 1) + NT)
                transposes(i, it, g, "x", (x1 if it == 1 else x2)[g])
                if it == 2:
                    transposes(i, it, g, "v", vh[g])

            def body(i, more):
                for it, g in STAGES:
                    nxt = after(i, it, g, more)
                    if it < 3:
                        hidden(i, it, g)
                        for t in range(NT):
                            control(i, it, g, t)
                            if t == 2:
                                transpose_state(*nxt)
                    else:
                        refine_hidden(i, g)
                        refine_out(i, g)
                        if nxt:
                            transpose_state(*nxt)

            transpose_state(0, *STAGES[0])
            rounds(pe, body)


def build(nc, args, out):
    a = dict(zip([n.replace("L0_", "") for n in _INS], args))
    parts_dram = nc.dram_tensor("parts_dram", [SEQS, 2, 3, 2, P, TOK], BF16).ap()
    normed_dram = nc.dram_tensor("normed_dram", [SEQS, TOK, D], F32).ap()
    attention(nc, a["attn_encodings"], a["attn_attn_W"], a["attn_attn_b"], a["attn_out_W"], a["attn_out_b"],
              parts_dram, normed_dram)
    experts(nc, {n[4:]: x for n, x in a.items() if n.startswith("ffn_")}, normed_dram, out)


_INS = ['L0_attn_encodings', 'L0_attn_attn_W', 'L0_attn_attn_b', 'L0_attn_out_W', 'L0_attn_out_b',
        'L0_ffn_integration_weight', 'L0_ffn_mu', 'L0_ffn_router_w1', 'L0_ffn_router_b1', 'L0_ffn_router_w2',
        'L0_ffn_router_b2', 'L0_ffn_halt_w1', 'L0_ffn_halt_b1', 'L0_ffn_halt_w2', 'L0_ffn_halt_b2',
        'L0_ffn_expert_w1', 'L0_ffn_expert_b1', 'L0_ffn_expert_w2', 'L0_ffn_expert_b2', 'L0_ffn_shared_w1',
        'L0_ffn_shared_b1', 'L0_ffn_shared_w2', 'L0_ffn_shared_b2', 'L0_ffn_shared_weight',
        'L0_ffn_refine_w1', 'L0_ffn_refine_b1', 'L0_ffn_refine_w2', 'L0_ffn_refine_b2']


def kernel(**inputs):
    import numpy as _np
    import concourse.bacc as _bacc
    from concourse import mybir as _mybir
    from concourse.bass_utils import run_bass_kernel_spmd as _run

    nc = _bacc.Bacc("TRN2", target_bir_lowering=False, num_devices=1)
    arrays, args = {}, []
    for name in _INS:
        a = _np.ascontiguousarray(inputs[name])
        if a.ndim == 0:
            a = a.reshape(1)
        arrays[f"in_{name}"] = a
        args.append(nc.dram_tensor(f"in_{name}", a.shape, _mybir.dt.from_np(a.dtype), kind="ExternalInput").ap())
    out = nc.dram_tensor("out_0", (SEQS, TOK, D), F32, kind="ExternalOutput").ap()
    build(nc, args, out)
    r = _run(nc, [arrays], core_ids=[0])
    return r.results[0]["out_0"]
```

```python
from contextlib import ExitStack

import concourse.bass as bass
from concourse import mybir

ALU = mybir.AluOpType
ACT = mybir.ActivationFunctionType
AX = mybir.AxisListType
F32 = mybir.dt.float32
BF16 = mybir.dt.bfloat16
F16 = mybir.dt.float16
U32 = mybir.dt.uint32

P = 128
SEQS = 8
TOK = 512
NT = TOK // P
D = 256
KC = D // P
HEADS = 16
HS = D // HEADS
HPC = P // HS
STACK = 6 * HS
QK_SCALE = 1.0 / 4.0
VW = 32
NEG = -1.0e30
EPS = 1e-5
Q_PARTS = (0, 0, 0, 1, 1, 2)
K_PARTS = (0, 1, 2, 0, 1, 0)

E = 8
HID = 64
EC = E * HID // P
FC = EC + 1
HCOLS = FC * P
CTRL = 3 * D
RH = 2 * D
RC = RH // P
DT = 0.1
STREAMS = 3


class Steps:

    def __init__(self, per_round, rnd, before=0):
        self.before, self.per_round, self.n = rnd * per_round + before, per_round, 0

    def next(self):
        self.n += 1
        return self.before + self.n

    def end(self):
        assert self.n == self.per_round, (self.n, self.per_round)


NORM_STEPS = 6


def norm_buffers(sb, tag):
    shapes = {"stats": [P, NT, 6], "mv": [P, NT, 2], "var": [P, NT], "log": [P, NT], "rstd": [P, NT], "tmp": [P, NT]}
    return {name: sb(f"{tag}_{name}", shape, F32) for name, shape in shapes.items()}


def variance(dve, nc, step, steps, res, n, var_ready):
    v = nc.vector
    for t in range(NT):
        last = v.bn_stats(n["stats"][:, t, :], res[:, t, :])
    last.then_inc(step, 1)
    dve.wait_ge(step, steps.next())
    v.memset(n["tmp"][:], 0.0)
    for t in range(NT):
        last = v.bn_aggr(n["mv"][:, t, :], n["stats"][:, t, :])
    last.then_inc(step, 1)
    dve.wait_ge(step, steps.next())
    v.tensor_scalar(n["var"][:], n["mv"][:, :, 1], EPS, None, ALU.add).then_inc(var_ready, 1)


def reciprocal_root(dve, nc, step, steps, n, rstd_raw, rnd):
    v, y, tmp = nc.vector, n["rstd"][:], n["tmp"][:]
    dve.wait_ge(rstd_raw, rnd + 1)
    v.tensor_tensor(tmp, y, y, ALU.mult).then_inc(step, 1)
    dve.wait_ge(step, steps.next())
    v.tensor_tensor(tmp, tmp, n["var"][:], ALU.mult).then_inc(step, 1)
    dve.wait_ge(step, steps.next())
    v.tensor_scalar(tmp, tmp, -0.5, 1.5, ALU.mult, ALU.add).then_inc(step, 1)
    dve.wait_ge(step, steps.next())
    v.tensor_tensor(y, y, tmp, ALU.mult).then_inc(step, 1)
    dve.wait_ge(step, steps.next())
    steps.end()


def rsqrt_guess(act, nc, n, sems, rnd):
    var_ready, rstd_step, rstd_raw = sems
    act.wait_ge(var_ready, rnd + 1)
    nc.scalar.activation(n["log"][:], n["var"][:], ACT.Ln).then_inc(rstd_step, 1)
    act.wait_ge(rstd_step, rnd + 1)
    nc.scalar.activation(n["rstd"][:], n["log"][:], ACT.Exp, scale=-0.5).then_inc(rstd_raw, 1)


def normalised(nc, out, res, n):
    for t in range(NT):
        last = nc.vector.tensor_scalar(out[:, t, :], res[:, t, :], n["mv"][:, t, 0:1], n["rstd"][:, t:t + 1],
                                       ALU.subtract, ALU.mult)
    return last


def attention(nc, encodings, attn_W, attn_b, out_W, out_b, parts_dram, normed_dram):
    with ExitStack() as ctx:
        def sb(name, shape, dt):
            return ctx.enter_context(nc.sbuf_tensor(name, shape, dt))

        primed = []

        def sem(name, start=0):
            s = ctx.enter_context(nc.semaphore(name))
            if start:
                primed.append((s, start))
            return s

        ps = ctx.enter_context(nc.psum_tensor("att_ps", [P, 8, 512], F32))
        MAIN, MAXIMA, OUTPUTS, TURNED = 4, 4, 6, 7

        wqk = sb("wqk", [P, KC, 2, D], F32)
        wv = sb("wv", [P, KC, D], F32)
        wo = sb("wo", [P, KC, D], F32)
        bias_row = sb("bias_row", [1, 2, D], F32)
        bias_qk = sb("bias_qk", [P, 4], F32)
        bias_v = sb("bias_v", [P, D], F32)
        bias_o = sb("bias_o", [P, D], F32)
        one = sb("one", [1, 2], F32)
        ident = sb("ident", [P, P], F32)
        identb = sb("identb", [P, P], BF16)
        mask_q = sb("mask_q", [P, P], BF16)
        mask_k = sb("mask_k", [P, P], BF16)
        x_in = [sb(f"x_in{p}", [P, NT, D], F32) for p in range(2)]
        xo = [sb(f"xo{p}", [P, NT, D], F32) for p in range(2)]
        xT = sb("xT", [P, KC, TOK], F32)
        qk32 = sb("qk32", [P, 4, TOK], F32)
        parts = sb("parts", [P, 3, 4, TOK], BF16)
        q_stack = [sb(f"q_stack{p}", [STACK + 2, HEADS, TOK], BF16) for p in range(2)]
        k_stack = [sb(f"k_stack{p}", [STACK + 2, HEADS, TOK], BF16) for p in range(2)]
        values = [sb(f"values{p}", [P, NT, HEADS, VW], F32) for p in range(2)]
        probs = sb("probs", [P, 4, 5, TOK], F32)
        neg_max = sb("neg_max", [P, 2 * HEADS, NT], F32)
        max_parts = sb("max_parts", [HEADS * NT, 2, P], BF16)
        heads_out = sb("heads_out", [P, TOK], F32)
        rden = sb("rden", [P, NT, 4], F32)
        attn = sb("attn", [P, NT, D], F32)
        attnT = sb("attnT", [P, KC, TOK], F32)
        res = sb("res", [P, NT, D], F32)
        norm = norm_buffers(sb, "att")
        normed = sb("normed", [P, NT, D], F32)

        weights_in = sem("weights_in")
        const_step = sem("const_step")
        consts = sem("consts")
        bias_ps = sem("bias_ps")
        bias_ok = sem("bias_ok")
        x_full = [sem(f"x_full{p}") for p in range(2)]
        x_added = sem("x_added")
        main_filled = [sem(f"main_filled{i}") for i in range(MAIN)]
        main_freed = [sem(f"main_freed{i}", 1) for i in range(MAIN)]
        max_filled = [sem(f"max_filled{i}") for i in range(2)]
        max_freed = [sem(f"max_freed{i}", 1) for i in range(2)]
        split_step = sem("split_step")
        parts_ready = sem("parts_ready", 1)
        parts_stored = sem("parts_stored", 1)
        stack_full = [[sem(f"stack_full{p}{m}") for m in range(2)] for p in range(2)]
        outputs_filled = sem("outputs_filled")
        turned_filled = sem("turned_filled")
        max_step = sem("max_step")
        max_ready = sem("max_ready", 1)
        max_rows_full = [sem(f"max_rows_full{p}") for p in range(2)]
        heads_ready = sem("heads_ready", 1)
        attn_step = sem("attn_step")
        attn_ready = sem("attn_ready", 1)
        res_ready = sem("res_ready")
        norm_step = sem("norm_step")
        norm_sems = (sem("var_ready"), sem("rstd_step"), sem("rstd_raw"))
        normed_ready = sem("normed_ready")
        normed_stored = sem("normed_stored", 1)

        PAIRS = HEADS // 2
        BLOCKS = 5
        MAX_USES = PAIRS * BLOCKS // 2
        MAX_AT = ((0, 1), (2,), (3,), (4,), (5,), (6,), (7,), ())
        WEIGHT_LOADS = KC * 3 + 5
        FRONT = ["x0", "x1", "q0", "q1", "k0", "k1", "v0", "v1"]
        TAIL = ["a0", "a1", "o0", "o1"]

        def fills(tail, front):
            names = []
            for j in range(PAIRS):
                names += [f"e{j}{u}" for u in range(BLOCKS)]
                if tail and j in (1, 2):
                    names += TAIL[2 * j - 2:2 * j]
                if front and j in (2, 3, 4):
                    names += FRONT[2 * j - 4:2 * j - 2]
            return names + (FRONT[6:] if front else [])

        class Step:

            def __init__(self, b, half, p, uses, names):
                self.b, self.half, self.p, self.uses, self.names = b, half, p, uses, names
                self.tail, self.front = "a0" in names and "e00" in names, "x0" in names

            def spot(self, name):
                n = self.names.index(name)
                return n % MAIN, self.uses + n // MAIN

        FIRST = 2 * len(FRONT) // MAIN
        SECOND = FIRST + len(fills(False, True)) // MAIN
        FULL = len(fills(True, True)) // MAIN
        STEP_6 = SECOND + 5 * FULL
        STEP_7 = STEP_6 + len(fills(True, False)) // MAIN
        STEP_8 = STEP_7 + len(fills(True, False)) // MAIN

        def sequences(eng, front, maxima, step, tail):
            for b in range(2):
                front(Step(b - 2, -1, b, b * len(FRONT) // MAIN, FRONT))
            maxima(0, 0, 0)
            step(Step(0, 0, 0, FIRST, fills(False, True)), True)
            with eng.Fori(0, 2) as i:
                step(Step(2 * i + 1, i, 1, 2 * FULL * i + SECOND, fills(True, True)), True)
                step(Step(2 * i + 2, i + 1, 0, 2 * FULL * i + SECOND + FULL, fills(True, True)), True)
            step(Step(5, 2, 1, SECOND + 4 * FULL, fills(True, True)), True)
            step(Step(6, 3, 0, STEP_6, fills(True, False)), True)
            step(Step(7, 3, 1, STEP_7, fills(True, False)), False)
            tail(Step(8, 4, 0, STEP_8, TAIL))

        block = ctx.enter_context(nc.Block())
        x_dram = encodings.rearrange("s (t p) d -> s p t d", p=P)
        normed_out = normed_dram.rearrange("s (t p) d -> s p t d", p=P)

        @block.sync
        def _(sp):
            for s, start in primed:
                sp.sem_inc(s, start)
            w_cols = attn_W.rearrange("(c p) (h t d) -> t c p h d", p=P, t=3, d=HS)
            b_cols = attn_b.rearrange("(h t d) -> t h d", t=3, d=HS)
            sp.dma_start(x_in[0][:], x_dram[0]).then_inc(x_full[0], 16)
            for c in range(KC):
                for t in range(2):
                    sp.dma_start(wqk[:, c, t, :].rearrange("p (h d) -> p h d", d=HS),
                                 w_cols[t, c]).then_inc(weights_in, 16)
                sp.dma_start(wv[:, c, :].rearrange("p (h d) -> p h d", d=HS), w_cols[2, c]).then_inc(weights_in, 16)
            sp.dma_start(wo[:], out_W.rearrange("(c p) n -> p c n", p=P)).then_inc(weights_in, 16)
            for t in range(2):
                sp.dma_start(bias_row[0:1, t, :].rearrange("p (h d) -> p h d", d=HS),
                             b_cols[t].unsqueeze(0)).then_inc(weights_in, 16)
            sp.dma_start(bias_v[:].rearrange("p (h d) -> p h d", d=HS),
                         b_cols[2].partition_broadcast(P)).then_inc(weights_in, 16)
            sp.dma_start(bias_o[:], out_b.partition_broadcast(P)).then_inc(weights_in, 16)
            sp.dma_start(x_in[1][:], x_dram[1]).then_inc(x_full[1], 16)

            def store_parts(s):
                for half in range(2):
                    sp.wait_ge(parts_ready, 2 * s + half + 1 + 1)
                    for part in range(3):
                        sp.dma_start(parts_dram[s, half, part].rearrange("m f n -> f m n"),
                                     parts[:, part, 2 * half:2 * half + 2, :]).then_inc(parts_stored, 16)
                sp.wait_ge(parts_stored, 96 * (s + 1) + 1)

            def load_stacks(s, p, m):
                heads = slice(m * HEADS // 2, (m + 1) * HEADS // 2)
                for half, stack, rows in ((0, q_stack[p], Q_PARTS), (1, k_stack[p], K_PARTS)):
                    for j, part in enumerate(rows):
                        sp.dma_start(stack[j * HS:(j + 1) * HS, heads, :],
                                     parts_dram[s, half, part, m].rearrange("(h i) n -> i h n", i=HS)
                                     ).then_inc(stack_full[p][m], 16)

            def front(st):
                store_parts(st.b + 2)
                for m in range(2):
                    load_stacks(st.b + 2, st.p, m)

            def maxima(s, p, nth):
                sp.wait_ge(max_ready, s + 1 + 1)
                for part in range(2):
                    sp.dma_start(q_stack[p][STACK + part:STACK + part + 1, :, :],
                                 max_parts[:, part, :]).then_inc(max_rows_full[p], 16)

            def load_x(s, p):
                sp.wait_ge(x_added, s - 1)
                sp.dma_start(x_in[p][:], x_dram[s]).then_inc(x_full[p], 16)

            def tail(st):
                sp.wait_ge(normed_ready, st.b)
                sp.dma_start(normed_out[st.b - 1], normed[:]).then_inc(normed_stored, 16)

            def step(st, more):
                b, p = st.b, st.p
                if isinstance(b, int) and b == 0:
                    load_x(2, 0)
                if st.tail:
                    tail(st)
                if st.front and not (isinstance(b, int) and b == 5):
                    load_x(b + 3, 1 - p)
                if st.front:
                    store_parts(b + 2)
                    load_stacks(b + 2, p, 0)
                if more:
                    maxima(b + 1, 1 - p, 0)
                if st.front:
                    bank, use = st.spot("e74")
                    sp.wait_ge(main_filled[bank], use + 1)
                    load_stacks(b + 2, p, 1)

            sequences(sp, front, maxima, step, tail)
            sp.wait_ge(normed_stored, 16 * SEQS + 1)

        @block.gpsimd
        def _(pool):
            steps = Steps(0, 0)
            g = nc.gpsimd
            g.memset(ident[:], 1.0).then_inc(const_step, 1)
            pool.wait_ge(const_step, steps.next())
            g.affine_select(out=ident[:], in_=ident[:], compare_op=ALU.is_equal, fill=0.0,
                            base=0, pattern=[[-1, P]], channel_multiplier=1).then_inc(const_step, 1)
            pool.wait_ge(const_step, steps.next())
            g.tensor_copy(identb[:], ident[:]).then_inc(const_step, 1)
            pool.wait_ge(const_step, steps.next())
            for mask, step in ((mask_q, 1), (mask_k, -1)):
                g.memset(mask[:], 0.0).then_inc(const_step, 1)
                pool.wait_ge(const_step, steps.next())
                g.affine_select(out=mask[:], in_=mask[:], compare_op=ALU.is_ge, fill=NEG,
                                base=0, pattern=[[-step, P]], channel_multiplier=step).then_inc(const_step, 1)
                pool.wait_ge(const_step, steps.next())
            g.memset(neg_max[:, HEADS:, :], 0.0).then_inc(const_step, 1)
            pool.wait_ge(const_step, steps.next())
            g.memset(one[:], 1.0).then_inc(consts, 1)
            pool.wait_ge(consts, 1)
            for p in range(2):
                g.memset(values[p][:], 0.0).then_inc(const_step, 1)
                pool.wait_ge(const_step, steps.next())
                g.memset(values[p][:, :, :, HS:HS + 1], 1.0).then_inc(const_step, 1)
                pool.wait_ge(const_step, steps.next())
            g.memset(k_stack[0][STACK:STACK + 2, :, :], 1.0).then_inc(const_step, 1)
            pool.wait_ge(const_step, steps.next())
            g.memset(k_stack[1][STACK:STACK + 2, :, :], 1.0).then_inc(consts, 1)
            pool.wait_ge(consts, 2)
            pool.wait_ge(weights_in, 16 * WEIGHT_LOADS)

            def residual(b, p, nth):
                pool.wait_ge(x_full[p], 16 * (nth + 1))
                if not (isinstance(b, int) and b < 2):
                    pool.wait_ge(res_ready, b - 1)
                g.tensor_tensor(xo[p][:], x_in[p][:], bias_o[:].unsqueeze(1).to_broadcast([P, NT, D]),
                                ALU.add).then_inc(x_added, 1)

            residual(0, 0, 0)
            residual(1, 1, 0)
            with pool.Fori(1, SEQS // 2) as i:
                residual(2 * i, 0, i)
                residual(2 * i + 1, 1, i)

        @block.scalar
        def _(act):
            nc.scalar.preload_act_table_set("natural_log_exp_and_others")
            act.wait_ge(bias_ps, 1)
            nc.scalar.mul(bias_qk[:, 0:2], ps[:, OUTPUTS, 0:2], QK_SCALE)
            nc.scalar.copy(bias_qk[:, 2:4], ps[:, OUTPUTS, 2:4]).then_inc(bias_ok, 1)
            act.wait_ge(bias_ok, 1)

            def filled(st, name):
                bank, use = st.spot(name)
                act.wait_ge(main_filled[bank], use + 1)
                return ps[:, bank, :], main_freed[bank]

            def turn_x(st):
                src, free = filled(st, "x0")
                nc.scalar.copy(xT[:, 0, :], src).then_inc(free, 1)

            def project(st, kind):
                s = st.b + 2
                if kind == "q":
                    act.wait_ge(parts_ready, 2 * s + 1)
                    act.wait_ge(parts_stored, 96 * s + 1)
                scale = QK_SCALE if kind == "q" else 1.0
                for c in range(KC):
                    m = c + (0 if kind == "q" else KC)
                    src, free = filled(st, f"{kind}{c}")
                    nc.scalar.activation(qk32[:, m, :], src, ACT.Identity, bias=bias_qk[:, m:m + 1], scale=scale)
                    nc.scalar.activation(parts[:, 0, m, :], src, ACT.Identity, bias=bias_qk[:, m:m + 1],
                                         scale=scale).then_inc(free, 1)

            def front(st):
                turn_x(st)
                project(st, "q")
                project(st, "k")

            def maxima(s, p, nth):
                pass

            def heads(b, g):
                act.wait_ge(outputs_filled, 4 * b + g + 1)
                nc.scalar.copy(heads_out[:], ps[:, OUTPUTS, :]).then_inc(heads_ready, 1)

            def turn_attn(st):
                src, free = filled(st, "a0")
                nc.scalar.copy(attnT[:, 0, :], src).then_inc(free, 1)

            def tail(st):
                heads(st.b - 1, 3)
                turn_attn(st)
                rsqrt_guess(act, nc, norm, norm_sems, st.b - 1)

            def step(st, more):
                b = st.b
                for pair in range(PAIRS):
                    if pair in (4, 6):
                        heads(b, pair // 2 - 2)
                    for u in range(BLOCKS):
                        src, free = filled(st, f"e{pair}{u}")
                        nc.scalar.activation(probs[:, pair % 4, u, :], src, ACT.Exp).then_inc(free, 1)
                    if st.tail and pair == 0:
                        heads(b - 1, 3)
                    if st.tail and pair == 1:
                        turn_attn(st)
                    if st.front and pair == 2:
                        turn_x(st)
                    if st.front and pair == 3:
                        project(st, "q")
                    if st.tail and pair == 3:
                        rsqrt_guess(act, nc, norm, norm_sems, b - 1)
                    if st.front and pair == 4:
                        project(st, "k")
                heads(b, 2)

            sequences(act, front, maxima, step, tail)

        @block.vector
        def _(dve):
            v = nc.vector

            def filled(st, name):
                bank, use = st.spot(name)
                dve.wait_ge(main_filled[bank], use + 1)
                return ps[:, bank, :], main_freed[bank]

            def turn_x(st):
                src, free = filled(st, "x1")
                v.tensor_copy(xT[:, 1, :], src).then_inc(free, 1)

            def split(st, kind):
                half = 0 if kind == "q" else 1
                steps = Steps(2, 2 * (st.b + 2) + half)
                s = slice(2 * half, 2 * half + 2)
                for c in range(KC):
                    bank, use = st.spot(f"{kind}{c}")
                    dve.wait_ge(main_freed[bank], use + 1 + 1)
                v.tensor_tensor(qk32[:, s, :], qk32[:, s, :], parts[:, 0, s, :], ALU.subtract).then_inc(split_step, 1)
                dve.wait_ge(split_step, steps.next())
                v.tensor_copy(parts[:, 1, s, :], qk32[:, s, :]).then_inc(split_step, 1)
                dve.wait_ge(split_step, steps.next())
                v.tensor_tensor(parts[:, 2, s, :], qk32[:, s, :], parts[:, 1, s, :],
                                ALU.subtract).then_inc(parts_ready, 1)

            def take_values(st):
                if isinstance(st.b, int) and st.b == -2:
                    dve.wait_ge(consts, 2)
                for c in range(2):
                    src, free = filled(st, f"v{c}")
                    for t in range(2):
                        last = v.tensor_tensor(
                            values[st.p][:, 2 * c + t, :, 0:HS],
                            src[:, t * D:(t + 1) * D].rearrange("p (h d) -> p h d", d=HS),
                            bias_v[:].rearrange("p (h d) -> p h d", d=HS), ALU.add)
                    last.then_inc(free, 1)

            def front(st):
                turn_x(st)
                split(st, "q")
                split(st, "k")
                take_values(st)

            def row_max(out, scores):
                return v.tensor_reduce(out, scores, AX.X, ALU.max, negate=True)

            def pair_maxima(s, pair):
                for u in range(BLOCKS):
                    k = BLOCKS * pair + u
                    dve.wait_ge(max_filled[k % 2], MAX_USES * s + k // 2 + 1)
                    bank, h = ps[:, MAXIMA + k % 2, :], 2 * pair + u // 3
                    if u in (0, 3):
                        last = row_max(neg_max[:, h, 3:4], bank)
                    elif u in (1, 4):
                        row_max(neg_max[:, h, 0:1], bank[:, 0:P])
                        last = row_max(neg_max[:, h, 2:3], bank[:, P:])
                    else:
                        last = row_max(neg_max[:, 2 * pair:2 * pair + 2, 1:2],
                                       bank.rearrange("p (a k) -> p a k", a=2))
                    last.then_inc(max_freed[k % 2], 1)

            def split_maxima(s):
                dve.wait_ge(turned_filled, 5 * s - 1 if not (isinstance(s, int) and s == 0) else 1)
                mx = ps[0:HEADS * NT, TURNED, 0:P]
                v.tensor_copy(max_parts[:, 0, :], mx).then_inc(max_step, 1)
                dve.wait_ge(max_step, s + 1)
                v.tensor_tensor(max_parts[:, 1, :], mx, max_parts[:, 0, :], ALU.subtract).then_inc(max_ready, 1)

            def maxima(s, p, nth):
                for pair in range(PAIRS):
                    pair_maxima(s, pair)
                split_maxima(s)

            def normalise_heads(b, g, after_maxima):
                dve.wait_ge(turned_filled, 5 * b + g + after_maxima + 2)
                o = ps[:, TURNED, :].rearrange("p (t j c) -> p t j c", t=NT, c=VW)
                v.reciprocal(rden[:], o[:, :, :, HS]).then_inc(attn_step, 1)
                dve.wait_ge(attn_step, 4 * b + g + 1)
                v.tensor_tensor(attn[:, :, g * 4 * HS:(g + 1) * 4 * HS].rearrange("p t (j d) -> p t j d", d=HS),
                                o[:, :, :, 0:HS], rden[:].unsqueeze(3).to_broadcast([P, NT, 4, HS]),
                                ALU.mult).then_inc(attn_ready, 1)

            def turn_attn(st):
                src, free = filled(st, "a1")
                v.tensor_copy(attnT[:, 1, :], src).then_inc(free, 1)

            def residual(st):
                dve.wait_ge(x_added, st.b)
                for u in range(2):
                    src, free = filled(st, f"o{u}")
                    v.tensor_tensor(res[:, 2 * u:2 * u + 2, :], src.rearrange("p (t d) -> p t d", d=D),
                                    xo[1 - st.p][:, 2 * u:2 * u + 2, :], ALU.add).then_inc(free, 1)
                for u in range(2):
                    bank, use = st.spot(f"o{u}")
                    dve.wait_ge(main_freed[bank], use + 1 + 1)
                v.memset(norm["tmp"][:], 0.0).then_inc(res_ready, 1)

            def finish(st, steps):
                reciprocal_root(dve, nc, norm_step, steps, norm, norm_sems[2], st.b - 1)
                dve.wait_ge(normed_stored, 16 * (st.b - 1) + 1)
                normalised(nc, normed, res, norm).then_inc(normed_ready, 1)

            def tail(st):
                normalise_heads(st.b - 1, 3, 0)
                turn_attn(st)
                residual(st)
                steps = Steps(NORM_STEPS, st.b - 1)
                variance(dve, nc, norm_step, steps, res, norm, norm_sems[0])
                finish(st, steps)

            def step(st, more):
                b = st.b
                for pair in range(PAIRS):
                    if more:
                        for m in MAX_AT[pair]:
                            pair_maxima(b + 1, m)
                    if st.tail and pair == 0:
                        normalise_heads(b - 1, 3, 1)
                    if st.tail and pair == 1:
                        turn_attn(st)
                    if st.tail and pair == 2:
                        residual(st)
                    if st.front and pair == 2:
                        turn_x(st)
                    if st.tail and pair == 3:
                        steps = Steps(NORM_STEPS, b - 1)
                        variance(dve, nc, norm_step, steps, res, norm, norm_sems[0])
                    if st.front and pair == 3:
                        split(st, "q")
                    if st.tail and pair == 4:
                        finish(st, steps)
                    if pair in (4, 6):
                        normalise_heads(b, pair // 2 - 2, 0)
                    if st.front and pair == 4:
                        split(st, "k")
                if more:
                    split_maxima(b + 1)
                normalise_heads(b, 2, 1 if more else 0)
                if st.front:
                    take_values(st)

            sequences(dve, front, maxima, step, tail)

        @block.tensor
        def _(pe):
            t_ = nc.tensor
            pe.wait_ge(consts, 1)
            pe.wait_ge(weights_in, 16 * WEIGHT_LOADS)
            for m in range(4):
                last = t_.matmul(ps[:, OUTPUTS, m:m + 1], bias_row[0:1, m // 2, (m % 2) * P:(m % 2 + 1) * P],
                                 one[0:1, 0:1], start=True, stop=True)
            last.then_inc(bias_ps, 1)

            def ring(st, name):
                bank, use = st.spot(name)
                pe.wait_ge(main_freed[bank], use + 1)
                return ps[:, bank, :], main_filled[bank]

            def freed(st, name):
                bank, use = st.spot(name)
                pe.wait_ge(main_freed[bank], use + 1 + 1)

            def turn(st, name, src):
                for c in range(KC):
                    dst, done = ring(st, f"{name}{c}")
                    for t in range(NT):
                        last = t_.transpose(dst[:, t * P:(t + 1) * P], src[:, t, c * P:(c + 1) * P], ident[:])
                    last.then_inc(done, 1)

            def turn_x(st):
                pe.wait_ge(x_full[st.p], 16 * (st.half + 2))
                turn(st, "x", x_in[st.p])

            def project(st, kind):
                if kind == "q":
                    freed(st, "x0")
                    freed(st, "x1")
                for m in range(KC):
                    dst, done = ring(st, f"{kind}{m}")
                    for c in range(KC):
                        last = t_.matmul(dst, wqk[:, c, 0 if kind == "q" else 1, m * P:(m + 1) * P],
                                         xT[:, c, :], start=(c == 0), stop=(c == KC - 1))
                    last.then_inc(done, 1)

            def project_rows(st, name, src, w):
                for u in range(2):
                    dst, done = ring(st, f"{name}{u}")
                    for t in range(2):
                        tok = slice((2 * u + t) * P, (2 * u + t + 1) * P)
                        for c in range(KC):
                            last = t_.matmul(dst[:, t * D:(t + 1) * D], src[:, c, tok], w[:, c, :],
                                             start=(c == 0), stop=(c == KC - 1))
                    last.then_inc(done, 1)

            def front(st):
                turn_x(st)
                project(st, "q")
                project(st, "k")
                project_rows(st, "v", xT, wv)

            def scores(out, stationary, moving, mask, at):
                t_.matmul(out, stationary, moving, start=True, stop=False)
                return t_.matmul(out[:, at:at + P], identb[:], mask, start=False, stop=True)

            def by_query(p, h, i, out):
                return scores(out, q_stack[p][0:STACK, h, i * P:(i + 1) * P], k_stack[p][0:STACK, h, 0:(i + 1) * P],
                              mask_q[:], i * P)

            def by_key(p, h, i, out):
                return scores(out, k_stack[p][:, h, i * P:(i + 1) * P], q_stack[p][:, h, i * P:TOK], mask_k[:], 0)

            def fill(kind, p, pair, u, bank, blocks):
                four, one_and_three, two = blocks
                h = 2 * pair + u // 3
                if u in (0, 3):
                    return kind(p, h, four, bank)
                if u in (1, 4):
                    for i, cols in one_and_three:
                        last = kind(p, h, i, bank[:, cols])
                    return last
                kind(p, 2 * pair, two, bank[:, 0:2 * P])
                return kind(p, 2 * pair + 1, two, bank[:, 2 * P:])

            def pair_maxima(s, p, nth, pair):
                if pair in (0, PAIRS // 2):
                    pe.wait_ge(stack_full[p][pair // (PAIRS // 2)], 16 * 12 * (nth + 1))
                for u in range(BLOCKS):
                    k = BLOCKS * pair + u
                    pe.wait_ge(max_freed[k % 2], MAX_USES * s + k // 2 + 1)
                    fill(by_query, p, pair, u, ps[:, MAXIMA + k % 2, :],
                         (3, ((0, slice(0, P)), (2, slice(P, 4 * P))), 1)).then_inc(max_filled[k % 2], 1)

            def turn_maxima(s):
                for k in range(2):
                    pe.wait_ge(max_freed[k], MAX_USES * (s + 1) + 1)
                if not (isinstance(s, int) and s == 0):
                    pe.wait_ge(attn_ready, 4 * (s - 1) + 2 + 1)
                t_.transpose(ps[:, TURNED, 0:P], neg_max[:].rearrange("p h t -> p (h t)"),
                             ident[:]).then_inc(turned_filled, 1)

            def maxima(s, p, nth):
                for pair in range(PAIRS):
                    pair_maxima(s, p, nth, pair)
                turn_maxima(s)

            def outputs(st, g, blocks):
                for u in range(BLOCKS):
                    freed(st, f"e{2 * g + 1}{u}")
                if 0 in blocks:
                    pe.wait_ge(heads_ready, 4 * st.b + g + 1)
                for i in blocks:
                    for j in range(4):
                        h, slot = 4 * g + j, (2 * g + j // 2) % 4
                        u0 = 3 * (j % 2)
                        src = {0: (u0, slice(0, TOK)), 1: (u0 + 1, slice(0, 3 * P)),
                               2: (2, slice((j % 2) * 2 * P, (j % 2 + 1) * 2 * P)),
                               3: (u0 + 1, slice(3 * P, TOK))}[i]
                        last = t_.matmul(ps[VW * j:VW * (j + 1), OUTPUTS, i * P:TOK], values[st.p][:, i, h, :],
                                         probs[:, slot, src[0], src[1]], start=(i == 0), stop=(i == NT - 1))
                return last

            def turn_heads(b, g, after_maxima):
                pe.wait_ge(heads_ready, 4 * b + g + 1 + 1)
                if after_maxima:
                    pe.wait_ge(max_ready, b + 2 + 1)
                else:
                    pe.wait_ge(attn_ready, 4 * b + g + 1)
                for t in range(NT):
                    last = t_.transpose(ps[:, TURNED, t * P:(t + 1) * P], heads_out[:, t * P:(t + 1) * P], ident[:])
                last.then_inc(turned_filled, 1)

            def turn_attn(st):
                pe.wait_ge(attn_ready, 4 * st.b + 1)
                turn(st, "a", attn)

            def project_out(st):
                freed(st, "a0")
                freed(st, "a1")
                project_rows(st, "o", attnT, wo)

            def tail(st):
                turn_heads(st.b - 1, 3, False)
                turn_attn(st)
                project_out(st)

            def step(st, more):
                b, p = st.b, st.p
                pe.wait_ge(max_rows_full[p], 32 * (st.half + 1))
                for pair in range(PAIRS):
                    for u in range(BLOCKS):
                        dst, done = ring(st, f"e{pair}{u}")
                        fill(by_key, p, pair, u, dst,
                             (0, ((1, slice(0, 3 * P)), (3, slice(3 * P, TOK))), 2)).then_inc(done, 1)
                    if more:
                        for m in MAX_AT[pair]:
                            pair_maxima(b + 1, 1 - p, st.half + p, m)
                    if st.tail and pair == 0:
                        turn_heads(b - 1, 3, False)
                    if st.tail and pair == 1:
                        turn_attn(st)
                    if st.tail and pair == 2:
                        project_out(st)
                    if st.front and pair == 2:
                        turn_x(st)
                    if st.front and pair == 3:
                        project(st, "q")
                    if st.front and pair == 4:
                        project(st, "k")
                    if pair in (2, 4, 6):
                        outputs(st, pair // 2 - 1, (0, 1))
                    if pair in (3, 5, 7):
                        outputs(st, pair // 2 - 1, (2, 3)).then_inc(outputs_filled, 1)
                    if pair in (4, 6):
                        turn_heads(b, pair // 2 - 2, False)
                if more:
                    turn_maxima(b + 1)
                outputs(st, 3, (0, 1))
                turn_heads(b, 2, more)
                outputs(st, 3, (2, 3)).then_inc(outputs_filled, 1)
                if st.front:
                    project_rows(st, "v", xT, wv)

            sequences(pe, front, maxima, step, tail)


def experts(nc, w, normed_dram, out):
    with ExitStack() as ctx:
        def sb(name, shape, dt):
            return ctx.enter_context(nc.sbuf_tensor(name, shape, dt))

        primed = []

        def sem(name, start=0):
            s = ctx.enter_context(nc.semaphore(name))
            if start:
                primed.append((s, start))
            return s

        UPDATE_STEPS = {1: 3, 2: 5, 3: 0}
        DVE_STEPS = {1: 6 + EC, 2: 3 + EC, 3: 0}
        GROUPS, PAIR = SEQS, 2
        ps = ctx.enter_context(nc.psum_tensor("exp_ps", [P, 8, 512], F32))

        def ctrl_ps(s):
            return ps[:, 2 + 2 * s:4 + 2 * s, :].rearrange("p a n -> p (a n)")

        w1 = sb("w1", [P, 2, 2 * KC, HCOLS], F16)
        w2 = sb("w2", [P, 2, EC, CTRL], F16)
        w2_shared_top = sb("w2_shared_top", [P, CTRL], F16)
        w2_shared_low = sb("w2_shared_low", [P, CTRL], F16)
        b2_parts = sb("b2_parts", [P, CTRL], F16)
        rf1 = sb("rf1", [P, 2, KC, RH], F16)
        rf2 = sb("rf2", [P, 2, RC, D], F16)
        wrh = sb("wrh", [P, KC, P], F32)
        w2rh = sb("w2rh", [P, E + 1], F32)
        b1 = sb("b1", [P, FC], F32)
        rf_b1 = sb("rf_b1", [P, RC], F32)
        brh = sb("brh", [P, 1], F32)
        b2rh = sb("b2rh", [P, E + 1], F32)
        mu = sb("mu", [P, D], F32)
        iw = sb("iw", [P, D], F32)
        rf_b2 = sb("rf_b2", [P, D], F32)
        half = sb("half", [P, 1], F32)
        gate_in = sb("gate_in", [P, 1], F32)
        gate_t = sb("gate_t", [P, 1], F32)
        gate = sb("gate", [P, 2], F32)
        ident = sb("e_ident", [P, P], F32)
        identb = sb("e_identb", [P, P], F16)
        spread = sb("spread", [P, EC, P], F16)
        numbers = sb("numbers", [P, 3, E], F32)

        def two(name, shape, dt):
            return [sb(f"{name}{g}", shape, dt) for g in range(PAIR)]

        x1 = two("x1", [P, NT, D], F32)
        x2 = two("x2", [P, NT, D], F32)
        vh = two("vh", [P, NT, D], F32)
        xTp = two("xTp", [P, 2, KC, TOK], F16)
        vTp = two("vTp", [P, 2, KC, TOK], F16)
        onehot = two("onehot", [P, NT, 2, 3, E], F16)
        onehotT = two("onehotT", [P, 2, TOK], F16)
        masks = two("masks", [P, 2, EC, TOK], F16)
        weights = two("weights", [P, NT, STREAMS], F32)
        nw = two("nw", [P, NT, STREAMS], F32)
        nwx = two("nwx", [P, NT, STREAMS], F32)
        xT32 = sb("xT32", [P, KC, TOK], F32)
        xm = sb("xm", [P, NT, D], F32)
        v_or_res = sb("v_or_res", [P, KC * TOK], F32)
        vT32 = v_or_res[:].rearrange("p (c n) -> p c n", c=KC)
        res = v_or_res[:].rearrange("p (t d) -> p t d", t=NT)
        rh = sb("rh", [P, TOK], F32)
        g32 = sb("g32", [P, FC, TOK], F32)
        gp = sb("gp", [P, 2, EC, TOK], F16)
        routed = sb("routed", [P, 2, 2, EC, TOK], F16)
        shared_hl = sb("shared_hl", [P, TOK], F16)
        shared_h1 = sb("shared_h1", [P, TOK], F16)
        ctrl = sb("ctrl", [P, NT, STREAMS, CTRL], F32)
        sp = sb("sp", [P, NT, STREAMS, D], F32)
        logits = sb("logits", [P, NT, E + 1], F32)
        top = sb("top", [P, NT, 8], F32)
        top_at = sb("top_at", [P, NT, 8], U32)
        top_f = sb("top_f", [P, NT, 2], F32)
        gates = sb("gates", [P, NT, 2], F32)
        gates_t = sb("gates_t", [P, NT, 2], F32)
        halt = sb("halt", [P, NT], F32)
        norm = norm_buffers(sb, "exp")
        final = sb("final", [P, NT, D], F32)

        loaded = sem("loaded")
        const_step = sem("e_const_step")
        consts = sem("e_consts")
        setup_step = sem("setup_step")
        gate_ready = sem("gate_ready")
        biases_split = sem("biases_split")
        weights_ready = sem("weights_ready")
        rows_in = sem("rows_in")
        x_full = [sem(f"e_x_full{g}") for g in range(PAIR)]
        ring_filled = [sem(f"ring_filled{i}") for i in range(2)]
        ring_freed = [sem(f"ring_freed{i}", 1) for i in range(2)]
        ctrl_filled = [sem(f"ctrl_filled{s}") for s in range(STREAMS)]
        ctrl_freed = [sem(f"ctrl_freed{s}", 1) for s in range(STREAMS)]
        xlow_ready = sem("xlow_ready", 1)
        vlow_ready = sem("vlow_ready", 1)
        gates_ready = sem("gates_ready")
        gates_done = sem("gates_done")
        weights_done = sem("weights_done")
        onehot_ready = sem("onehot_ready")
        h_ready = sem("h_ready", 1)
        tanh_done = sem("tanh_done")
        abs_ready = sem("abs_ready")
        ln_ready = sem("ln_ready")
        xm_ready = sem("xm_ready")
        spx_ready = sem("spx_ready", 1)
        x1_kept = sem("x1_kept")
        pool_step = sem("pool_step")
        tile_done = sem("tile_done", NT)
        dve_step = sem("dve_step")
        refine_step = sem("refine_step")
        update_step = sem("update_step")
        norm_step = sem("e_norm_step")
        norm_sems = (sem("e_var_ready"), sem("e_rstd_step"), sem("e_rstd_raw"))
        res_ready = sem("e_res_ready")
        final_ready = sem("final_ready", 1)
        final_stored = sem("final_stored", 1)

        FIRST = [(1, 0), (1, 1)]
        ROUND = [(2, 0), (2, 1), (3, 0), (1, 0), (3, 1), (1, 1)]
        LAST = [(2, 0), (2, 1), (3, 0), (3, 1)]
        ROUNDS = GROUPS // PAIR - 1
        FILLS = {1: ["x0", "x1", "rh", "h4", "logits", "h0", "onehot", "h1", "mask00", "mask10", "mask01", "mask11",
                     "h2", "mask02", "mask12", "h3", "mask03", "mask13"],
                 2: ["x0", "x1", "v0", "v1", "rh", "h4", "logits", "h0", "h1", "h2", "h3"],
                 3: ["x0", "x1", "h0", "h1", "h2", "h3"]}

        class Stage:

            def __init__(self, order, at, i):
                self.order, self.at, self.i = order, at, i
                self.it, self.g = order[at]
                self.pair = 0 if i is None else i + 1 if order is ROUND and self.it == 1 else i

            def before(self, of):
                here = sum(of(it) for it, _ in self.order[:self.at])
                if self.i is None:
                    return here
                return self.i * sum(of(it) for it, _ in ROUND) + (sum(of(it) for it, _ in FIRST) + here)

            def kinds(self, *its):
                return self.before(lambda it: it in its)

            @property
            def controls(self):
                return self.kinds(1, 2)

            def slot_uses(self, s):
                return self.before(lambda it: NT if it < 3 else int(s < 2))

            def spot(self, what):
                n = sum(len(FILLS[it]) for it, _ in self.order[:self.at]) + FILLS[self.it].index(what)
                if self.i is None:
                    return n % 2, n // 2
                first, each = (sum(len(FILLS[it]) for it, _ in o) for o in (FIRST, ROUND))
                assert first % 2 == each % 2 == 0
                return n % 2, self.i * (each // 2) + (first // 2 + n // 2)

            @property
            def last_stage(self):
                if self.at:
                    return Stage(self.order, self.at - 1, self.i)
                if self.i is None:
                    return None
                if isinstance(self.i, int) and self.i == 0:
                    return Stage(FIRST, 1, None)
                return Stage(ROUND, len(ROUND) - 1, self.i - 1)

            @property
            def next_stage(self):
                if self.at + 1 < len(self.order):
                    return Stage(self.order, self.at + 1, self.i)
                if self.order is FIRST:
                    return Stage(ROUND, 0, 0)
                return Stage(ROUND, 0, self.i + 1) if self.order is ROUND else None

            @property
            def ends_alone(self):
                return self.order is LAST and self.it == 3

        def hs(it):
            return FC if it < 3 else RC

        LOAD_COUNT = 3 * 2 * KC + 3 * 5 + 10 + 6 + 2
        block = ctx.enter_context(nc.Block())
        x_dram = normed_dram.rearrange("s (t p) d -> s p t d", p=P)
        out_dram = out.rearrange("s (t p) d -> s p t d", p=P)
        stage = ctrl[:].rearrange("p t s n -> p (t s n)")
        at = 0

        def staged(shape):
            nonlocal at
            n = shape[0] * shape[1]
            view = stage[:, at:at + n].rearrange("p (a b) -> p a b", a=shape[0])
            at += n
            return view

        w1_32, w2_32, w2s_32 = staged((2 * KC, HCOLS)), staged((EC, CTRL)), staged((1, CTRL))
        rf1_32, rf2_32, b2_32 = staged((KC, RH)), staged((RC, D)), staged((1, CTRL))
        b2e32, b2s32 = b2_32[0:E, 0, :], b2_32[32:33, 0, :]
        b2_split = sp[:].rearrange("p t s d -> p (t s d)").bitcast(F16)[:, 0:3 * CTRL].rearrange(
            "p (a n) -> p a n", a=3)
        b2e_split, b2s_split = b2_split[0:E], b2_split[32:33]
        COLUMNS = ((0, 0), (1, 2), (2, 1))

        def stages(eng, stage):
            for at in range(len(FIRST)):
                stage(Stage(FIRST, at, None))
            with eng.Fori(0, ROUNDS) as i:
                for at in range(len(ROUND)):
                    stage(Stage(ROUND, at, i))
            for at in range(len(LAST)):
                stage(Stage(LAST, at, ROUNDS))

        @block.sync
        def _(sync):
            for s, start in primed:
                sync.sem_inc(s, start)
            count = 0

            def load(dst, src):
                nonlocal count
                count += 1
                sync.dma_start(dst, src).then_inc(loaded, 16)

            for g in range(PAIR):
                sync.dma_start(x1[g][:], x_dram[g]).then_inc(x_full[g], 16)
            for c in range(2 * KC):
                load(w1_32[:, c, 0:E * HID].rearrange("p (e h) -> p e h", h=HID),
                     w["expert_w1"].rearrange("e (c p) h -> c p e h", p=P)[c])
                for r in range(2):
                    load(w1_32[:, c, E * HID + r * HID:E * HID + (r + 1) * HID],
                         w["shared_w1"][c * P:(c + 1) * P, :])
            w2_rows = w["expert_w2"].rearrange("e h n -> (e h) n").rearrange("(c p) n -> p c n", p=P)
            for dst, src in COLUMNS:
                d, s = slice(dst * D, (dst + 1) * D), slice(src * D, (src + 1) * D)
                load(w2_32[:, :, d], w2_rows[:, :, s])
                for r in range(2):
                    load(w2s_32[r * HID:(r + 1) * HID, 0, d], w["shared_w2"][:, s])
                load(b2e32[:, d], w["expert_b2"][:, s])
                load(b2s32[:, d], w["shared_b2"][s].unsqueeze(0))
            load(rf1_32, w["refine_w1"].rearrange("(c p) n -> p c n", p=P))
            load(rf2_32, w["refine_w2"].rearrange("(c p) n -> p c n", p=P))
            load(wrh[:, :, 0:HID], w["router_w1"].rearrange("(c p) n -> p c n", p=P))
            load(wrh[:, :, HID:P], w["halt_w1"].rearrange("(c p) n -> p c n", p=P))
            load(b2rh[:, 0:E], w["router_b2"].partition_broadcast(P))
            load(b2rh[:, E:E + 1], w["halt_b2"].partition_broadcast(P))
            load(mu[:], w["mu"].partition_broadcast(P))
            load(iw[:], w["integration_weight"].partition_broadcast(P))
            load(rf_b2[:], w["refine_b2"].partition_broadcast(P))
            load(gate_in[:], w["shared_weight"].partition_broadcast(P))
            with nc.allow_non_contiguous_dma(reason="biases as columns"):
                load(b1[:, 0:EC], w["expert_b1"].rearrange("e h -> (e h)").rearrange("(c p) -> p c", p=P))
                for r in range(2):
                    load(b1[r * HID:(r + 1) * HID, EC:FC], w["shared_b1"].unsqueeze(1))
                load(rf_b1[:], w["refine_b1"].rearrange("(c p) -> p c", p=P))
                load(brh[0:HID, :], w["router_b1"].unsqueeze(1))
                load(brh[HID:P, :], w["halt_b1"].unsqueeze(1))
            sync.wait_ge(consts, 1)
            load(w2rh[0:HID, 0:E], w["router_w2"])
            load(w2rh[HID:P, E:E + 1], w["halt_w2"])
            assert count == LOAD_COUNT, count
            sync.wait_ge(biases_split, 1)
            for part in range(3):
                sync.dma_start(w2_shared_low[HID + part:HID + part + 1, :],
                               b2s_split[:, part, :]).then_inc(rows_in, 16)
                sync.dma_start(b2_parts[part * E:(part + 1) * E, :], b2e_split[:, part, :]).then_inc(rows_in, 16)

            def store(i, g):
                sync.wait_ge(final_ready, PAIR * i + g + 1 + 1)
                sync.dma_start(out_dram[PAIR * i + g], final[:]).then_inc(final_stored, 16)

            def reload(i, g):
                sync.wait_ge(x1_kept, PAIR * i + g + 1)
                sync.dma_start(x1[g][:], x_dram[PAIR * (i + 1) + g]).then_inc(x_full[g], 16)

            with sync.Fori(0, ROUNDS) as i:
                for g in range(PAIR):
                    reload(i, g)
                for g in range(PAIR):
                    store(i, g)
            for g in range(PAIR):
                store(ROUNDS, g)
            sync.wait_ge(final_stored, 16 * GROUPS + 1)

        @block.gpsimd
        def _(pool):
            steps = Steps(0, 0)
            gp_ = nc.gpsimd
            gp_.memset(w2rh[:], 0.0).then_inc(consts, 1)
            pool.wait_ge(consts, 1)
            gp_.memset(ident[:], 1.0).then_inc(const_step, 1)
            pool.wait_ge(const_step, steps.next())
            gp_.affine_select(out=ident[:], in_=ident[:], compare_op=ALU.is_equal, fill=0.0,
                              base=0, pattern=[[-1, P]], channel_multiplier=1).then_inc(const_step, 1)
            pool.wait_ge(const_step, steps.next())
            gp_.tensor_copy(identb[:], ident[:]).then_inc(const_step, 1)
            pool.wait_ge(const_step, steps.next())
            gp_.memset(half[:], 0.5).then_inc(const_step, 1)
            pool.wait_ge(const_step, steps.next())
            gp_.memset(spread[:], 1.0).then_inc(const_step, 1)
            pool.wait_ge(const_step, steps.next())
            gp_.affine_select(out=spread[:], in_=spread[:], compare_op=ALU.is_equal, fill=0.0, base=0,
                              pattern=[[-2, EC], [-1, 2], [0, HID]], channel_multiplier=1).then_inc(const_step, 1)
            pool.wait_ge(const_step, steps.next())
            for e in range(E):
                gp_.memset(numbers[:, :, e:e + 1], float(e)).then_inc(const_step, 1)
                pool.wait_ge(const_step, steps.next())
            for g in range(PAIR):
                gp_.memset(onehotT[g][:], 0.0).then_inc(const_step, 1)
                pool.wait_ge(const_step, steps.next())
            gp_.memset(b2_parts[:], 0.0).then_inc(const_step, 1)
            pool.wait_ge(const_step, steps.next())
            gp_.memset(w2_shared_low[:], 0.0).then_inc(const_step, 1)
            pool.wait_ge(const_step, steps.next())
            gp_.memset(shared_h1[:], 1.0).then_inc(consts, 1)
            pool.wait_ge(consts, 2)
            pool.wait_ge(loaded, 16 * LOAD_COUNT)

            def keep_x1(st):
                bank, use = st.spot("x1")
                pool.wait_ge(ring_filled[bank], use + 1)
                gp_.tensor_tensor(x2[st.g][:], x1[st.g][:], x1[st.g][:], ALU.add).then_inc(x1_kept, 1)

            def stage(st):
                n, g, nxt = st.controls, st.g, st.next_stage
                if st.it == 3:
                    if nxt and nxt.it == 3:
                        keep_x1(nxt)
                    return
                if st.it == 1:
                    pool.wait_ge(x_full[g], 16 * (st.pair + 1))
                else:
                    pool.wait_ge(tile_done, NT * (n - 1) + NT)
                pool.wait_ge(spx_ready, NT * n + 1)
                src = x1 if st.it == 1 else x2
                gp_.tensor_tensor(xm[:], src[g][:], mu[:].unsqueeze(1).to_broadcast([P, NT, D]),
                                  ALU.subtract).then_inc(xm_ready, 1)
                pool.wait_ge(xm_ready, n + 1)
                for t in range(NT):
                    if t == 2 and nxt.it == 3:
                        keep_x1(nxt)
                    pool.wait_ge(ln_ready, NT * n + t + 1)
                    gp_.tensor_tensor(sp[:, t], sp[:, t], ctrl[:, t, :, 2 * D:], ALU.subtract).then_inc(pool_step, 1)
                    pool.wait_ge(pool_step, NT * n + t + 1)
                    gp_.tensor_tensor(sp[:, t], sp[:, t], xm[:, t, :].unsqueeze(1).to_broadcast([P, STREAMS, D]),
                                      ALU.mult).then_inc(spx_ready, 1)

            stages(pool, stage)

        @block.scalar
        def _(act):
            nc.scalar.preload_act_table_set("gelu_and_others")
            act.wait_ge(loaded, 16 * LOAD_COUNT)
            nc.scalar.activation(gate_t[:], gate_in[:], ACT.Tanh, scale=0.5).then_inc(gate_ready, 1)

            def filled(st, what):
                bank, use = st.spot(what)
                act.wait_ge(ring_filled[bank], use + 1)
                return ps[:, bank, :], ring_freed[bank]

            def transposed(st):
                g = st.g
                act.wait_ge(xlow_ready, st.kinds(1, 2, 3) + 1)
                for c in range(KC):
                    src, free = filled(st, f"x{c}")
                    nc.scalar.copy(xT32[:, c, :], src)
                    nc.scalar.copy(xTp[g][:, 0, c, :], src).then_inc(free, 1)
                if st.it == 2:
                    act.wait_ge(vlow_ready, st.kinds(2) + 1)
                    act.wait_ge(final_ready, st.kinds(3) + 1)
                    for c in range(KC):
                        src, free = filled(st, f"v{c}")
                        nc.scalar.copy(vT32[:, c, :], src)
                        nc.scalar.copy(vTp[g][:, 0, c, :], src).then_inc(free, 1)

            def gelu(st, c):
                bias = b1 if st.it < 3 else rf_b1
                src, free = filled(st, f"h{c}")
                nc.scalar.activation(g32[:, c, :], src, ACT.Gelu, bias=bias[:, c:c + 1])
                high = shared_hl[:] if c == EC else gp[:, 0, c, :]
                nc.scalar.activation(high, src, ACT.Gelu, bias=bias[:, c:c + 1]).then_inc(free, 1)

            def softplus_logs(st, tiles, refined=None):
                n = st.controls
                nc.scalar.preload_act_table_set("natural_log_exp_and_others")
                for t in tiles:
                    act.wait_ge(abs_ready, STREAMS * (NT * n + t + 1))
                    b = ctrl[:, t, :, 2 * D:]
                    nc.scalar.activation(b, b, ACT.Ln, scale=0.5, bias=half[:, 0:1]).then_inc(ln_ready, 1)
                if refined:
                    rsqrt_guess(act, nc, norm, norm_sems, refined.kinds(3))
                nc.scalar.preload_act_table_set("gelu_and_others")

            def tanhs(st, t):
                act.wait_ge(tile_done, NT * (st.controls - 1) + t + 1 + NT)
                for s in range(STREAMS):
                    act.wait_ge(ctrl_filled[s], st.slot_uses(s) + t + 1)
                    cols = slice(0, CTRL) if st.it == 2 else slice(D, CTRL)
                    width = CTRL if st.it == 2 else 2 * D
                    nc.scalar.activation(ctrl[:, t, s, cols], ctrl_ps(s)[:, 0:width], ACT.Tanh,
                                         scale=0.5).then_inc(tanh_done, 1)

            def stage(st):
                it, g, n, last, nxt = st.it, st.g, st.controls, st.last_stage, st.next_stage
                if it < 3:
                    src, free = filled(st, "rh")
                    nc.scalar.activation(rh[:], src, ACT.Gelu, bias=brh[:, 0:1]).then_inc(free, 1)
                act.wait_ge(h_ready, st.before(hs) + 1)
                if last and last.it == 3:
                    act.wait_ge(ctrl_filled[1], last.slot_uses(1) + 1)
                if it < 3:
                    gelu(st, EC)
                    gelu(st, 0)
                    act.wait_ge(gates_ready, n + 1)
                    nc.scalar.activation(gates_t[:], gates[:], ACT.Tanh, scale=0.5).then_inc(gates_done, 1)
                else:
                    gelu(st, 0)
                for c in range(1, EC if it < 3 else RC):
                    gelu(st, c)
                    if it == 1:
                        for m in ((0, 1) if c == 1 else (c,)):
                            src, free = filled(st, f"mask0{m}")
                            nc.scalar.copy(masks[g][:, 0, m, :], src).then_inc(free, 1)
                if nxt and it == 3 and nxt.it < 3:
                    transposed(nxt)
                if last and last.it < 3:
                    softplus_logs(last, (2, 3))
                if it < 3:
                    tanhs(st, 0)
                    tanhs(st, 1)
                    softplus_logs(st, (0, 1), last if last and last.it == 3 else None)
                    tanhs(st, 2)
                    transposed(nxt)
                    tanhs(st, 3)
                elif st.ends_alone:
                    if nxt:
                        transposed(nxt)
                    nc.scalar.preload_act_table_set("natural_log_exp_and_others")
                    rsqrt_guess(act, nc, norm, norm_sems, st.kinds(3))
                    nc.scalar.preload_act_table_set("gelu_and_others")

            transposed(Stage(FIRST, 0, None))
            stages(act, stage)

        @block.vector
        def _(dve):
            v = nc.vector
            setup = Steps(0, 0)
            dve.wait_ge(loaded, 16 * LOAD_COUNT)
            dve.wait_ge(consts, 2)
            v.tensor_copy(w1[:, 0], w1_32)
            v.tensor_copy(w2[:, 0], w2_32)
            v.tensor_copy(w2_shared_top[:], w2s_32[:, 0, :])
            v.tensor_copy(rf1[:, 0], rf1_32)
            v.tensor_copy(rf2[:, 0], rf2_32)
            v.tensor_copy(b2e_split[:, 0, :], b2e32)
            v.tensor_copy(b2s_split[:, 0, :], b2s32).then_inc(setup_step, 1)
            dve.wait_ge(setup_step, setup.next())
            v.tensor_tensor(b2e32, b2e32, b2e_split[:, 0, :], ALU.subtract)
            v.tensor_tensor(b2s32, b2s32, b2s_split[:, 0, :], ALU.subtract).then_inc(setup_step, 1)
            dve.wait_ge(setup_step, setup.next())
            v.tensor_copy(b2e_split[:, 1, :], b2e32)
            v.tensor_copy(b2s_split[:, 1, :], b2s32).then_inc(setup_step, 1)
            dve.wait_ge(setup_step, setup.next())
            v.tensor_tensor(b2e_split[:, 2, :], b2e32, b2e_split[:, 1, :], ALU.subtract)
            v.tensor_tensor(b2s_split[:, 2, :], b2s32, b2s_split[:, 1, :],
                            ALU.subtract).then_inc(biases_split, 1)
            v.tensor_tensor(w1[:, 1], w1_32, w1[:, 0], ALU.subtract)
            v.tensor_tensor(w2[:, 1], w2_32, w2[:, 0], ALU.subtract)
            v.tensor_tensor(w2_shared_low[0:HID, :], w2s_32[0:HID, 0, :], w2_shared_top[0:HID, :], ALU.subtract)
            v.tensor_tensor(rf1[:, 1], rf1_32, rf1[:, 0], ALU.subtract)
            v.tensor_tensor(rf2[:, 1], rf2_32, rf2[:, 0], ALU.subtract).then_inc(weights_ready, 1)
            dve.wait_ge(weights_ready, 1)
            dve.wait_ge(gate_ready, 1)
            v.tensor_scalar(gate[:, 0:1], gate_t[:], 0.5, 0.5, ALU.mult, ALU.add)
            v.tensor_scalar(gate[:, 1:2], gate_t[:], -0.5, 0.5, ALU.mult, ALU.add).then_inc(setup_step, 1)
            dve.wait_ge(setup_step, setup.next())

            def filled(st, what):
                bank, use = st.spot(what)
                dve.wait_ge(ring_filled[bank], use + 1)
                return ps[:, bank, :], ring_freed[bank]

            def freed(st, what):
                bank, use = st.spot(what)
                dve.wait_ge(ring_freed[bank], use + 1 + 1)

            def low_parts(st):
                g = st.g
                freed(st, "x0")
                freed(st, "x1")
                v.tensor_tensor(xTp[g][:, 1], xT32[:], xTp[g][:, 0], ALU.subtract).then_inc(xlow_ready, 1)
                if st.it == 2:
                    freed(st, "v0")
                    freed(st, "v1")
                    v.tensor_tensor(vTp[g][:, 1], vT32[:], vTp[g][:, 0], ALU.subtract).then_inc(vlow_ready, 1)

            def route(st, chain):
                it, g, n = st.it, st.g, st.controls
                src, free = filled(st, "logits")
                v.tensor_tensor(logits[:], src[:, 0:NT * 16].rearrange("p (t c) -> p t c", t=NT)[:, :, 0:E + 1],
                                b2rh[:].unsqueeze(1).to_broadcast([P, NT, E + 1]), ALU.add).then_inc(free, 1)
                freed(st, "logits")
                if it == 1:
                    v.memset(top_f[:], 0.0)
                    for t in range(NT):
                        last = v.max(top[:, t, :], logits[:, t, 0:E])
                    last.then_inc(dve_step, 1)
                    dve.wait_ge(dve_step, chain.next())
                    v.tensor_tensor(gates[:, :, 0], top[:, :, 0], top[:, :, 1], ALU.subtract)
                v.tensor_copy(gates[:, :, 1], logits[:, :, E]).then_inc(gates_ready, 1)
                if it == 1:
                    for t in range(NT):
                        last = v.max_index(top_at[:, t, :], top[:, t, :], logits[:, t, 0:E])
                    last.then_inc(dve_step, 1)
                    dve.wait_ge(dve_step, chain.next())
                    v.tensor_copy(top_f[:], top_at[:, :, 0:2]).then_inc(dve_step, 1)
                    dve.wait_ge(dve_step, chain.next())
                    for t in range(NT):
                        for k in range(2):
                            last = v.tensor_scalar(onehot[g][:, t, k], numbers[:], top_f[:, t, k:k + 1], None,
                                                   ALU.is_equal)
                    last.then_inc(onehot_ready, 1)

            def stream_weights(st, chain):
                it, g, n = st.it, st.g, st.controls
                dve.wait_ge(gates_done, n + 1)
                if it == 1:
                    v.tensor_scalar(weights[g][:, :, 1], gates_t[:, :, 0], 0.5, 0.5, ALU.mult, ALU.add)
                    v.tensor_scalar(weights[g][:, :, 2], gates_t[:, :, 0], -0.5, 0.5, ALU.mult,
                                    ALU.add).then_inc(dve_step, 1)
                    dve.wait_ge(dve_step, chain.next())
                    v.tensor_scalar(weights[g][:, :, 1:3], weights[g][:, :, 1:3], gate[:, 1:2], None, ALU.mult)
                    v.tensor_copy(weights[g][:, :, 0], gate[:, 0:1].to_broadcast([P, NT]))
                v.tensor_scalar(halt[:], gates_t[:, :, 1], -0.5, -0.5, ALU.mult, ALU.add).then_inc(dve_step, 1)
                dve.wait_ge(dve_step, chain.next())
                v.tensor_tensor(nw[g][:], weights[g][:], halt[:].unsqueeze(2).to_broadcast([P, NT, STREAMS]),
                                ALU.mult).then_inc(dve_step, 1)
                dve.wait_ge(dve_step, chain.next())
                v.tensor_scalar(nwx[g][:], nw[g][:], 0.5 * DT, None, ALU.mult).then_inc(weights_done, 1)
                dve.wait_ge(weights_done, n + 1)

            def hidden(st, chain):
                it, g = st.it, st.g
                freed(st, f"h{EC}")
                v.tensor_copy(shared_h1[0:HID, :], shared_hl[0:HID, :])
                v.tensor_tensor(shared_hl[HID:P, :], g32[HID:P, EC, :], shared_hl[HID:P, :],
                                ALU.subtract).then_inc(h_ready, 1)
                if it == 1:
                    src, free = filled(st, "onehot")
                    v.tensor_copy(onehotT[g][0:3 * E].rearrange("p k n -> p (k n)"),
                                  src[0:3 * E, :].bitcast(F16)).then_inc(free, 1)
                for c in range(EC):
                    freed(st, f"h{c}")
                    v.tensor_tensor(gp[:, 1, c, :], g32[:, c, :], gp[:, 0, c, :], ALU.subtract).then_inc(dve_step, 1)
                    dve.wait_ge(dve_step, chain.next())
                    if it == 1:
                        freed(st, f"mask0{c}")
                        src, free = filled(st, f"mask1{c}")
                        v.tensor_copy(masks[g][:, 1, c, :], src).then_inc(free, 1)
                        freed(st, f"mask1{c}")
                    for k in range(2):
                        last = v.tensor_tensor(routed[:, k, :, c, :], gp[:, :, c, :],
                                               masks[g][:, k, c, :].unsqueeze(1).to_broadcast([P, 2, TOK]), ALU.mult)
                    last.then_inc(h_ready, 1)

            def control(st, t):
                it, g, n = st.it, st.g, st.controls
                for s in range(STREAMS):
                    dve.wait_ge(tanh_done, STREAMS * (NT * n + t) + s + 1)
                    at_b = 2 * D if it == 2 else D
                    v.tensor_scalar(sp[:, t, s, :], ctrl_ps(s)[:, at_b:at_b + D], 0.0, None,
                                    ALU.max).then_inc(ctrl_freed[s], 1)
                    b = ctrl[:, t, s, 2 * D:]
                    v.scalar_tensor_tensor(b, b, -1.0, b, ALU.mult, ALU.max).then_inc(abs_ready, 1)

            def update(st, t):
                it, g, n = st.it, st.g, st.controls
                steps = Steps(UPDATE_STEPS[it], t, st.before(lambda it: NT * UPDATE_STEPS[it]))
                a, gg = ctrl[:, t, :, 0:D], ctrl[:, t, :, D:2 * D]
                dve.wait_ge(spx_ready, NT * n + t + 1 + 1)
                if it == 2:
                    v.scalar_tensor_tensor(a, a, 1.0, vh[g][:, t, :].unsqueeze(1).to_broadcast(
                 [P, STREAMS, D]), ALU.add, ALU.mult).then_inc(update_step, 1)
                    dve.wait_ge(update_step, steps.next())
                    v.tensor_tensor(sp[:, t], sp[:, t], a, ALU.subtract).then_inc(update_step, 1)
                    dve.wait_ge(update_step, steps.next())
                v.scalar_tensor_tensor(gg, gg, 1.0, sp[:, t], ALU.add, ALU.mult).then_inc(update_step, 1)
                dve.wait_ge(update_step, steps.next())
                src = x1 if it == 1 else x2
                x_new, v_new = x2[g][:, t, :], vh[g][:, t, :]
                for s in range(STREAMS):
                    if it == 1:
                        if s == 0:
                            v.tensor_scalar(v_new, sp[:, t, s, :], nw[g][:, t, s:s + 1], None, ALU.mult)
                        else:
                            v.scalar_tensor_tensor(v_new, sp[:, t, s, :], nw[g][:, t, s:s + 1], v_new,
                                                   ALU.mult, ALU.add)
                    last = v.scalar_tensor_tensor(x_new, ctrl[:, t, s, D:2 * D], nwx[g][:, t, s:s + 1],
                                                  src[g][:, t, :] if s == 0 else x_new, ALU.mult, ALU.add)
                    if s < 2:
                        last.then_inc(update_step, 1)
                        dve.wait_ge(update_step, steps.next())
                last.then_inc(tile_done, 1)

            def halve(st, chain):
                g = st.g
                freed(st, "v1")
                v.tensor_scalar(vh[g][:], vh[g][:], 0.5, None, ALU.mult).then_inc(dve_step, 1)
                dve.wait_ge(dve_step, chain.next())

            def refined_hidden(st):
                for c in range(RC):
                    freed(st, f"h{c}")
                    v.tensor_tensor(gp[:, 1, c, :], g32[:, c, :], gp[:, 0, c, :], ALU.subtract).then_inc(h_ready, 1)

            def refine(st):
                g, n = st.g, st.kinds(3)
                for u in range(2):
                    s = slice(2 * u, 2 * u + 2)
                    dve.wait_ge(ctrl_filled[u], st.slot_uses(u) + 1)
                    v.tensor_tensor(res[:, s, :], ctrl_ps(u)[:, 0:2 * D].rearrange("p (t d) -> p t d", d=D),
                                    rf_b2[:].unsqueeze(1).to_broadcast([P, 2, D]), ALU.add).then_inc(ctrl_freed[u], 1)
                dve.wait_ge(ctrl_freed[1], st.slot_uses(1) + 1 + 1)
                v.tensor_tensor(res[:], res[:], iw[:].unsqueeze(1).to_broadcast([P, NT, D]), ALU.mult).then_inc(refine_step, 1)
                dve.wait_ge(refine_step, n + 1)
                dve.wait_ge(x1_kept, n + 1)
                for u in range(2):
                    s = slice(2 * u, 2 * u + 2)
                    v.tensor_tensor(res[:, s, :], res[:, s, :], x2[g][:, s, :], ALU.add).then_inc(res_ready, 1)
                dve.wait_ge(res_ready, 2 * n + 2)
                steps = Steps(NORM_STEPS, n)
                variance(dve, nc, norm_step, steps, res, norm, norm_sems[0])
                return steps

            def finish(st, steps):
                n = st.kinds(3)
                reciprocal_root(dve, nc, norm_step, steps, norm, norm_sems[2], n)
                dve.wait_ge(final_stored, 16 * n + 1)
                normalised(nc, final, res, norm).then_inc(final_ready, 1)

            def stage(st):
                it, g, last, nxt = st.it, st.g, st.last_stage, st.next_stage
                chain = Steps(DVE_STEPS[it], 0, st.before(lambda it: DVE_STEPS[it]))
                if it == 3:
                    refined_hidden(st)
                    if nxt and nxt.it < 3:
                        low_parts(nxt)
                    if st.ends_alone:
                        if last.it < 3:
                            update(last, 2)
                            update(last, 3)
                        if nxt:
                            low_parts(nxt)
                        finish(st, refine(st))
                    return
                if it == 2:
                    halve(st, chain)
                route(st, chain)
                hidden(st, chain)
                refined = last if last and last.it == 3 else None
                if refined:
                    norm_steps = refine(refined)
                stream_weights(st, chain)
                unfinished = refined.last_stage if refined else last
                for t in range(NT):
                    control(st, t)
                    if t < 2:
                        if unfinished:
                            update(unfinished, t + 2)
                    else:
                        update(st, t - 2)
                    if t == 2:
                        if refined:
                            finish(refined, norm_steps)
                        low_parts(nxt)
                chain.end()

            low_parts(Stage(FIRST, 0, None))
            stages(dve, stage)

        @block.tensor
        def _(pe):
            t_ = nc.tensor
            pe.wait_ge(consts, 2)
            pe.wait_ge(loaded, 16 * LOAD_COUNT)
            pe.wait_ge(weights_ready, 1)
            pe.wait_ge(rows_in, 16 * 6)

            def ring(st, what):
                bank, use = st.spot(what)
                pe.wait_ge(ring_freed[bank], use + 1)
                return ps[:, bank, :], ring_filled[bank]

            def freed(st, what):
                bank, use = st.spot(what)
                pe.wait_ge(ring_freed[bank], use + 1 + 1)

            def transposes(st, name, src):
                for c in range(KC):
                    dst, done = ring(st, f"{name}{c}")
                    for t in range(NT):
                        last = t_.transpose(dst[:, t * P:(t + 1) * P], src[:, t, c * P:(c + 1) * P], ident[:])
                    last.then_inc(done, 1)

            def split_products(out, pairs, ready=None):
                n = len(pairs)
                for j, (stationary, moving) in enumerate(pairs):
                    if ready is not None:
                        pe.wait_ge(h_ready, ready + j + 1)
                    t_.matmul(out, stationary[0], moving[0], start=(j == 0), stop=False)
                    t_.matmul(out, stationary[1], moving[0], start=False, stop=False)
                    last = t_.matmul(out, stationary[0], moving[1], start=False, stop=(j == n - 1))
                return last

            def onehots(st):
                g = st.g
                pe.wait_ge(onehot_ready, st.kinds(1) + 1)
                dst, done = ring(st, "onehot")
                dst = dst[0:3 * E, :].bitcast(F16)
                for k in range(2):
                    for t in range(NT):
                        last = t_.transpose(dst[:, (k * NT + t) * P:(k * NT + t + 1) * P],
                                            onehot[g][:, t, k].rearrange("p a e -> p (a e)"), identb[:])
                last.then_inc(done, 1)
                freed(st, "onehot")

            def chunk(st, c, moving):
                dst, done = ring(st, f"h{c}")
                cols = slice(c * P, (c + 1) * P)
                split_products(dst, [((w1[:, 0, j, cols], w1[:, 1, j, cols]), m)
                                     for j, m in enumerate(moving)]).then_inc(done, 1)

            def mask(st, k, c):
                dst, done = ring(st, f"mask{k}{c}")
                t_.matmul(dst, spread[:, c, :], onehotT[st.g][:, k, :], start=True, stop=True).then_inc(done, 1)

            def hidden(st):
                it, g = st.it, st.g
                freed(st, "x0")
                freed(st, "x1")
                dst, done = ring(st, "rh")
                for c in range(KC):
                    last = t_.matmul(dst, wrh[:, c, :], xT32[:, c, :], start=(c == 0), stop=(c == KC - 1))
                last.then_inc(done, 1)
                pe.wait_ge(xlow_ready, st.kinds(1, 2, 3) + 1 + 1)
                moving = [(xTp[g][:, 0, c, :], xTp[g][:, 1, c, :]) for c in range(KC)]
                if it == 2:
                    pe.wait_ge(vlow_ready, st.kinds(2) + 1 + 1)
                    moving += [(vTp[g][:, 0, c, :], vTp[g][:, 1, c, :]) for c in range(KC)]
                chunk(st, EC, moving)
                freed(st, "rh")
                dst, done = ring(st, "logits")
                for t in range(NT):
                    last = t_.matmul(dst[:, 16 * t:16 * t + E + 1], rh[:, t * P:(t + 1) * P], w2rh[:],
                                     start=True, stop=True)
                last.then_inc(done, 1)
                chunk(st, 0, moving)
                if it == 1:
                    onehots(st)
                chunk(st, 1, moving)
                if it == 1:
                    for c in range(2):
                        mask(st, 0, c)
                        mask(st, 1, c)
                for c in range(2, EC):
                    chunk(st, c, moving)
                    if it == 1:
                        mask(st, 0, c)
                        mask(st, 1, c)

            def control(st, t):
                it, g, h0 = st.it, st.g, st.before(hs)
                cols = ((0, 2 * D), (2 * D, CTRL)) if it == 2 else ((D, CTRL),)
                tok = slice(t * P, (t + 1) * P)
                for s in range(STREAMS):
                    if t == 0 and s == 0:
                        pe.wait_ge(h_ready, h0 + 1 + 1)
                    pe.wait_ge(ctrl_freed[s], st.slot_uses(s) + t + 1)
                    if s == 0:
                        terms = [(shared_hl[:, tok], w2_shared_top[:]), (shared_h1[:, tok], w2_shared_low[:])]
                    else:
                        k = s - 1
                        terms = [(onehotT[g][:, k, tok], b2_parts[:])]
                        for c in range(EC):
                            terms += [(routed[:, k, 0, c, tok], w2[:, 0, c, :]),
                                      (routed[:, k, 0, c, tok], w2[:, 1, c, :]),
                                      (routed[:, k, 1, c, tok], w2[:, 0, c, :])]
                    for j, (stationary, moving) in enumerate(terms):
                        if t == 0 and s == 1 and j % 3 == 1:
                            pe.wait_ge(h_ready, h0 + 1 + j // 3 + 1 + 1)
                        for a, z in cols:
                            last = t_.matmul(ctrl_ps(s)[:, a - cols[0][0]:z - cols[0][0]], stationary,
                                             moving[:, a:z], start=(j == 0), stop=(j == len(terms) - 1))
                    last.then_inc(ctrl_filled[s], 1)

            def refine_hidden(st):
                g = st.g
                pe.wait_ge(xlow_ready, st.kinds(1, 2, 3) + 1 + 1)
                for c in range(RC):
                    dst, done = ring(st, f"h{c}")
                    cols = slice(c * P, (c + 1) * P)
                    split_products(dst, [((rf1[:, 0, j, cols], rf1[:, 1, j, cols]),
                                          (xTp[g][:, 0, j, :], xTp[g][:, 1, j, :]))
                                         for j in range(KC)]).then_inc(done, 1)

            def refine_out(st):
                for t in range(NT):
                    u, tok = t // 2, slice(t * P, (t + 1) * P)
                    if t % 2 == 0:
                        pe.wait_ge(ctrl_freed[u], st.slot_uses(u) + 1)
                    ready = st.before(hs) + 1 if t == 0 else None
                    last = split_products(ctrl_ps(u)[:, (t % 2) * D:(t % 2 + 1) * D],
                                          [((gp[:, 0, c, tok], gp[:, 1, c, tok]), (rf2[:, 0, c, :], rf2[:, 1, c, :]))
                                           for c in range(RC)], ready)
                    if t % 2:
                        last.then_inc(ctrl_filled[u], 1)

            def transpose_state(st):
                g = st.g
                if st.it == 1:
                    pe.wait_ge(x_full[g], 16 * (st.pair + 1))
                else:
                    under_way = 0 if st.ends_alone and st.g == 1 else 1
                    pe.wait_ge(tile_done, NT * (st.controls - under_way) + NT)
                transposes(st, "x", (x1 if st.it == 1 else x2)[g])
                if st.it == 2:
                    transposes(st, "v", vh[g])

            def stage(st):
                nxt = st.next_stage
                if st.it < 3:
                    hidden(st)
                    for t in range(NT):
                        control(st, t)
                        if t == 2:
                            transpose_state(nxt)
                else:
                    refine_hidden(st)
                    if nxt and nxt.it < 3:
                        transpose_state(nxt)
                    refine_out(st)
                    if nxt and nxt.it == 3:
                        transpose_state(nxt)

            transpose_state(Stage(FIRST, 0, None))
            stages(pe, stage)


def build(nc, args, out):
    a = dict(zip([n.replace("L0_", "") for n in _INS], args))
    parts_dram = nc.dram_tensor("parts_dram", [SEQS, 2, 3, 2, P, TOK], BF16).ap()
    normed_dram = nc.dram_tensor("normed_dram", [SEQS, TOK, D], F32).ap()
    attention(nc, a["attn_encodings"], a["attn_attn_W"], a["attn_attn_b"], a["attn_out_W"], a["attn_out_b"],
              parts_dram, normed_dram)
    experts(nc, {n[4:]: x for n, x in a.items() if n.startswith("ffn_")}, normed_dram, out)


_INS = ['L0_attn_encodings', 'L0_attn_attn_W', 'L0_attn_attn_b', 'L0_attn_out_W', 'L0_attn_out_b',
        'L0_ffn_integration_weight', 'L0_ffn_mu', 'L0_ffn_router_w1', 'L0_ffn_router_b1', 'L0_ffn_router_w2',
        'L0_ffn_router_b2', 'L0_ffn_halt_w1', 'L0_ffn_halt_b1', 'L0_ffn_halt_w2', 'L0_ffn_halt_b2',
        'L0_ffn_expert_w1', 'L0_ffn_expert_b1', 'L0_ffn_expert_w2', 'L0_ffn_expert_b2', 'L0_ffn_shared_w1',
        'L0_ffn_shared_b1', 'L0_ffn_shared_w2', 'L0_ffn_shared_b2', 'L0_ffn_shared_weight',
        'L0_ffn_refine_w1', 'L0_ffn_refine_b1', 'L0_ffn_refine_w2', 'L0_ffn_refine_b2']


def kernel(**inputs):
    import numpy as _np
    import concourse.bacc as _bacc
    from concourse import mybir as _mybir
    from concourse.bass_utils import run_bass_kernel_spmd as _run

    nc = _bacc.Bacc("TRN2", target_bir_lowering=False, num_devices=1)
    arrays, args = {}, []
    for name in _INS:
        a = _np.ascontiguousarray(inputs[name])
        if a.ndim == 0:
            a = a.reshape(1)
        arrays[f"in_{name}"] = a
        args.append(nc.dram_tensor(f"in_{name}", a.shape, _mybir.dt.from_np(a.dtype), kind="ExternalInput").ap())
    out = nc.dram_tensor("out_0", (SEQS, TOK, D), F32, kind="ExternalOutput").ap()
    build(nc, args, out)
    r = _run(nc, [arrays], core_ids=[0])
    return r.results[0]["out_0"]
```

```python
from contextlib import ExitStack

from concourse import mybir

ALU = mybir.AluOpType
ACT = mybir.ActivationFunctionType
AX = mybir.AxisListType
F32 = mybir.dt.float32
BF16 = mybir.dt.bfloat16
F16 = mybir.dt.float16
U32 = mybir.dt.uint32

P = 128
SEQS = 8
TOK = 512
NT = TOK // P
D = 256
KC = D // P
HEADS = 16
HS = D // HEADS
STACK = 6 * HS
QK_SCALE = 1.0 / 4.0
VW = 32
NEG = -1.0e30
EPS = 1e-5
Q_PARTS = (0, 0, 0, 1, 1, 2)
K_PARTS = (0, 1, 2, 0, 1, 0)

E = 8
HID = 64
EC = E * HID // P
FC = EC + 1
HCOLS = FC * P
CTRL = 3 * D
RH = 2 * D
RC = RH // P
DT = 0.1
STREAMS = 3


class Steps:

    def __init__(self, per_round, rnd, before=0):
        self.before, self.per_round, self.n = rnd * per_round + before, per_round, 0

    def next(self):
        self.n += 1
        return self.before + self.n

    def end(self):
        assert self.n == self.per_round, (self.n, self.per_round)


NORM_STEPS = 6


def norm_buffers(sb, tag):
    shapes = {"stats": [P, NT, 6], "mv": [P, NT, 2], "var": [P, NT], "log": [P, NT], "rstd": [P, NT], "tmp": [P, NT]}
    return {name: sb(f"{tag}_{name}", shape, F32) for name, shape in shapes.items()}


def variance(dve, nc, step, steps, res, n, var_ready):
    v = nc.vector
    for t in range(NT):
        last = v.bn_stats(n["stats"][:, t, :], res[:, t, :])
    last.then_inc(step, 1)
    dve.wait_ge(step, steps.next())
    v.memset(n["tmp"][:], 0.0)
    for t in range(NT):
        last = v.bn_aggr(n["mv"][:, t, :], n["stats"][:, t, :])
    last.then_inc(step, 1)
    dve.wait_ge(step, steps.next())
    v.tensor_scalar(n["var"][:], n["mv"][:, :, 1], EPS, None, ALU.add).then_inc(var_ready, 1)


def reciprocal_root(dve, nc, step, steps, n, rstd_raw, rnd):
    v, y, tmp = nc.vector, n["rstd"][:], n["tmp"][:]
    dve.wait_ge(rstd_raw, rnd + 1)
    v.tensor_tensor(tmp, y, y, ALU.mult).then_inc(step, 1)
    dve.wait_ge(step, steps.next())
    v.tensor_tensor(tmp, tmp, n["var"][:], ALU.mult).then_inc(step, 1)
    dve.wait_ge(step, steps.next())
    v.tensor_scalar(tmp, tmp, -0.5, 1.5, ALU.mult, ALU.add).then_inc(step, 1)
    dve.wait_ge(step, steps.next())
    v.tensor_tensor(y, y, tmp, ALU.mult).then_inc(step, 1)
    dve.wait_ge(step, steps.next())
    steps.end()


def rsqrt_guess(act, nc, n, sems, rnd):
    var_ready, rstd_step, rstd_raw = sems
    act.wait_ge(var_ready, rnd + 1)
    nc.scalar.activation(n["log"][:], n["var"][:], ACT.Ln).then_inc(rstd_step, 1)
    act.wait_ge(rstd_step, rnd + 1)
    nc.scalar.activation(n["rstd"][:], n["log"][:], ACT.Exp, scale=-0.5).then_inc(rstd_raw, 1)


def normalised(nc, out, res, n):
    for t in range(NT):
        last = nc.vector.tensor_scalar(out[:, t, :], res[:, t, :], n["mv"][:, t, 0:1], n["rstd"][:, t:t + 1],
                                       ALU.subtract, ALU.mult)
    return last


def attention(nc, encodings, attn_W, attn_b, out_W, out_b, parts_dram, normed_dram):
    with ExitStack() as ctx:
        def sb(name, shape, dt):
            return ctx.enter_context(nc.sbuf_tensor(name, shape, dt))

        primed = []

        def sem(name, start=0):
            s = ctx.enter_context(nc.semaphore(name))
            if start:
                primed.append((s, start))
            return s

        ps = ctx.enter_context(nc.psum_tensor("att_ps", [P, 8, 512], F32))
        MAIN, MAXIMA, OUTPUTS, TURNED = 4, 4, 6, 7

        wqk = sb("wqk", [P, KC, 2, D], F32)
        wv = sb("wv", [P, KC, D], F32)
        wo = sb("wo", [P, KC, D], F32)
        bias_row = sb("bias_row", [1, 2, D], F32)
        bias_qk = sb("bias_qk", [P, 4], F32)
        bias_v = sb("bias_v", [P, D], F32)
        bias_o = sb("bias_o", [P, D], F32)
        one = sb("one", [1, 2], F32)
        wait_carrier = sb("wait_carrier", [P, 2], F32)
        ident = sb("ident", [P, P], F32)
        identb = sb("identb", [P, P], BF16)
        mask_q = sb("mask_q", [P, P], BF16)
        x_in = [sb(f"x_in{p}", [P, NT, D], F32) for p in range(2)]
        xo = [sb(f"xo{p}", [P, NT, D], F32) for p in range(2)]
        xT = sb("xT", [P, KC, TOK], F32)
        qk32 = sb("qk32", [P, 4, TOK], F32)
        parts = sb("parts", [P, 3, 4, TOK], BF16)
        q_stack = [sb(f"q_stack{p}", [STACK + 2, HEADS, TOK], BF16) for p in range(2)]
        k_stack = [sb(f"k_stack{p}", [STACK + 2, HEADS, TOK], BF16) for p in range(2)]
        values = [sb(f"values{p}", [P, NT, HEADS, VW], F32) for p in range(2)]
        probs = sb("probs", [P, 4, 5, TOK], F32)
        neg_max = sb("neg_max", [P, 2 * HEADS, NT], F32)
        max_parts = sb("max_parts", [HEADS * NT, 2, P], BF16)
        heads_out = sb("heads_out", [P, TOK], F32)
        rden = sb("rden", [P, NT, 4], F32)
        attn = sb("attn", [P, NT, D], F32)
        attnT = sb("attnT", [P, KC, TOK], F32)
        res = sb("res", [P, NT, D], F32)
        norm = norm_buffers(sb, "att")
        normed = sb("normed", [P, NT, D], F32)

        weights_in = sem("weights_in")
        const_step = sem("const_step")
        consts = sem("consts")
        bias_ps = sem("bias_ps")
        bias_ok = sem("bias_ok")
        x_full = [sem(f"x_full{p}") for p in range(2)]
        x_added = sem("x_added")
        main_filled = [sem(f"main_filled{i}") for i in range(MAIN)]
        main_freed = [sem(f"main_freed{i}", 1) for i in range(MAIN)]
        max_filled = [sem(f"max_filled{i}") for i in range(2)]
        max_freed = [sem(f"max_freed{i}", 1) for i in range(2)]
        split_step = sem("split_step")
        middle_ready = sem("middle_ready")
        parts_ready = sem("parts_ready", 1)
        parts_stored = sem("parts_stored", 1)
        stack_full = [[sem(f"stack_full{p}{m}") for m in range(2)] for p in range(2)]
        outputs_filled = sem("outputs_filled")
        turned_filled = sem("turned_filled")
        max_step = sem("max_step")
        max_ready = sem("max_ready", 1)
        max_rows_full = [sem(f"max_rows_full{p}") for p in range(2)]
        probs_masked = sem("probs_masked", 1)
        heads_ready = sem("heads_ready", 1)
        attn_step = sem("attn_step")
        attn_ready = sem("attn_ready", 1)
        res_ready = sem("res_ready")
        norm_step = sem("norm_step")
        norm_sems = (sem("var_ready"), sem("rstd_step"), sem("rstd_raw"))
        normed_ready = sem("normed_ready")
        normed_stored = sem("normed_stored", 1)

        PAIRS = HEADS // 2
        BLOCKS = 5
        MAX_USES = PAIRS * BLOCKS // 2
        MAX_AT = ((0, 1), (2,), (3,), (4,), (5,), (6,), (7,), ())
        WEIGHT_LOADS = KC * 3 + 5
        FRONT = ["x0", "x1", "q0", "q1", "k0", "k1", "v0", "v1"]
        TAIL = ["a0", "a1", "o0", "o1"]

        def fills(tail, front, late):
            names = []
            for j in range(PAIRS):
                names += [f"e{j}{u}" for u in range(BLOCKS)]
                if late and j == 0:
                    names += FRONT[6:]
                if tail and j in (2, 3):
                    names += TAIL[2 * j - 4:2 * j - 2]
                if front and j in (1, 2, 3):
                    names += FRONT[2 * j - 2:2 * j]
            return names

        class Step:

            def __init__(self, b, half, p, before, names, rounds=0):
                self.b, self.half, self.p, self.before, self.names, self.rounds = b, half, p, before, names, rounds
                self.tail, self.front, self.late = ("a0" in names and "e00" in names, "x0" in names,
                                                    "v0" in names and "e00" in names)

            def spot(self, name):
                n = self.before + self.names.index(name)
                return n % MAIN, self.rounds + n // MAIN

        AT_0 = 2 * len(FRONT)
        AT_1 = AT_0 + len(fills(False, True, False))
        FULL = fills(True, True, True)
        AT_6 = AT_1 + 5 * len(FULL)
        AT_7 = AT_6 + len(fills(True, False, True))
        AT_8 = AT_7 + len(fills(True, False, False))
        EACH = 2 * len(FULL) // MAIN
        assert len(FULL) % MAIN == 0

        block = ctx.enter_context(nc.Block())
        x_dram = encodings.rearrange("s (t p) d -> s p t d", p=P)
        normed_out = normed_dram.rearrange("s (t p) d -> s p t d", p=P)

        def sequences(eng, front, maxima, step, tail):
            for b in range(2):
                front(Step(b - 2, -1, b, b * len(FRONT), FRONT))
            maxima(0, 0, 0)
            step(Step(0, 0, 0, AT_0, fills(False, True, False)), True)
            with eng.Fori(0, 2) as i:
                step(Step(2 * i + 1, i, 1, AT_1, FULL, EACH * i), True)
                step(Step(2 * i + 2, i + 1, 0, AT_1 + len(FULL), FULL, EACH * i), True)
            step(Step(5, 2, 1, AT_1 + 4 * len(FULL), FULL), True)
            step(Step(6, 3, 0, AT_6, fills(True, False, True)), True)
            step(Step(7, 3, 1, AT_7, fills(True, False, False)), False)
            tail(Step(8, 4, 0, AT_8, TAIL))

        @block.sync
        def _(sp):
            for s, start in primed:
                sp.sem_inc(s, start)
            w_cols = attn_W.rearrange("(c p) (h t d) -> t c p h d", p=P, t=3, d=HS)
            b_cols = attn_b.rearrange("(h t d) -> t h d", t=3, d=HS)
            sp.dma_start(x_in[0][:], x_dram[0]).then_inc(x_full[0], 16)
            for c in range(KC):
                for t in range(2):
                    sp.dma_start(wqk[:, c, t, :].rearrange("p (h d) -> p h d", d=HS),
                                 w_cols[t, c]).then_inc(weights_in, 16)
                sp.dma_start(wv[:, c, :].rearrange("p (h d) -> p h d", d=HS), w_cols[2, c]).then_inc(weights_in, 16)
            sp.dma_start(wo[:], out_W.rearrange("(c p) n -> p c n", p=P)).then_inc(weights_in, 16)
            for t in range(2):
                sp.dma_start(bias_row[0:1, t, :].rearrange("p (h d) -> p h d", d=HS),
                             b_cols[t].unsqueeze(0)).then_inc(weights_in, 16)
            sp.dma_start(bias_v[:].rearrange("p (h d) -> p h d", d=HS),
                         b_cols[2].partition_broadcast(P)).then_inc(weights_in, 16)
            sp.dma_start(bias_o[:], out_b.partition_broadcast(P)).then_inc(weights_in, 16)
            sp.dma_start(x_in[1][:], x_dram[1]).then_inc(x_full[1], 16)

            def store_parts(s):
                for half in range(2):
                    sp.wait_ge(parts_ready, 2 * s + half + 1 + 1)
                    for part in range(3):
                        sp.dma_start(parts_dram[s, half, part].rearrange("m f n -> f m n"),
                                     parts[:, part, 2 * half:2 * half + 2, :]).then_inc(parts_stored, 16)
                sp.wait_ge(parts_stored, 96 * (s + 1) + 1)

            def load_stacks(s, p, m):
                heads = slice(m * HEADS // 2, (m + 1) * HEADS // 2)
                for half, stack, rows in ((0, q_stack[p], Q_PARTS), (1, k_stack[p], K_PARTS)):
                    for j, part in enumerate(rows):
                        sp.dma_start(stack[j * HS:(j + 1) * HS, heads, :],
                                     parts_dram[s, half, part, m].rearrange("(h i) n -> i h n", i=HS)
                                     ).then_inc(stack_full[p][m], 16)

            def front(st):
                store_parts(st.b + 2)
                for m in range(2):
                    load_stacks(st.b + 2, st.p, m)

            def maxima(s, p, nth):
                sp.wait_ge(max_ready, s + 1 + 1)
                for part in range(2):
                    sp.dma_start(q_stack[p][STACK + part:STACK + part + 1, :, :],
                                 max_parts[:, part, :]).then_inc(max_rows_full[p], 16)

            def load_x(s, p):
                sp.wait_ge(x_added, s - 1)
                sp.dma_start(x_in[p][:], x_dram[s]).then_inc(x_full[p], 16)

            def tail(st):
                sp.wait_ge(normed_ready, st.b)
                sp.dma_start(normed_out[st.b - 1], normed[:]).then_inc(normed_stored, 16)

            def step(st, more):
                b, p = st.b, st.p
                if isinstance(b, int) and b == 0:
                    load_x(2, 0)
                if st.front:
                    store_parts(b + 2)
                    load_stacks(b + 2, p, 0)
                if st.front and not (isinstance(b, int) and b == 5):
                    load_x(b + 3, 1 - p)
                if more:
                    maxima(b + 1, 1 - p, 0)
                if st.front:
                    bank, use = st.spot("e74")
                    sp.wait_ge(main_filled[bank], use + 1)
                    load_stacks(b + 2, p, 1)
                if st.tail:
                    tail(st)

            sequences(sp, front, maxima, step, tail)
            sp.wait_ge(normed_stored, 16 * SEQS + 1)

        @block.gpsimd
        def _(pool):
            steps = Steps(0, 0)
            g = nc.gpsimd
            g.memset(ident[:], 1.0).then_inc(const_step, 1)
            pool.wait_ge(const_step, steps.next())
            g.affine_select(out=ident[:], in_=ident[:], compare_op=ALU.is_equal, fill=0.0,
                            base=0, pattern=[[-1, P]], channel_multiplier=1).then_inc(const_step, 1)
            pool.wait_ge(const_step, steps.next())
            g.tensor_copy(identb[:], ident[:]).then_inc(const_step, 1)
            pool.wait_ge(const_step, steps.next())
            g.memset(mask_q[:], 0.0).then_inc(const_step, 1)
            pool.wait_ge(const_step, steps.next())
            g.affine_select(out=mask_q[:], in_=mask_q[:], compare_op=ALU.is_ge, fill=NEG,
                            base=0, pattern=[[-1, P]], channel_multiplier=1).then_inc(const_step, 1)
            pool.wait_ge(const_step, steps.next())
            g.memset(neg_max[:, HEADS:, :], 0.0).then_inc(const_step, 1)
            pool.wait_ge(const_step, steps.next())
            g.memset(wait_carrier[:], 0.0).then_inc(const_step, 1)
            pool.wait_ge(const_step, steps.next())
            g.memset(one[:], 1.0).then_inc(consts, 1)
            pool.wait_ge(consts, 1)
            for p in range(2):
                g.memset(values[p][:], 0.0).then_inc(const_step, 1)
                pool.wait_ge(const_step, steps.next())
                g.memset(values[p][:, :, :, HS:HS + 1], 1.0).then_inc(const_step, 1)
                pool.wait_ge(const_step, steps.next())
            g.memset(k_stack[0][STACK:STACK + 2, :, :], 1.0).then_inc(const_step, 1)
            pool.wait_ge(const_step, steps.next())
            g.memset(k_stack[1][STACK:STACK + 2, :, :], 1.0).then_inc(consts, 1)
            pool.wait_ge(consts, 2)
            pool.wait_ge(weights_in, 16 * WEIGHT_LOADS)

            def residual(b, p, nth):
                pool.wait_ge(x_full[p], 16 * (nth + 1))
                if not (isinstance(b, int) and b < 2):
                    pool.wait_ge(res_ready, b - 1)
                g.tensor_tensor(xo[p][:], x_in[p][:], bias_o[:].unsqueeze(1).to_broadcast([P, NT, D]),
                                ALU.add).then_inc(x_added, 1)

            def mask_probs(st, pair):
                pool.wait_ge(probs_masked, 4 * (PAIRS * st.b + pair) + 1)
                for u in range(BLOCKS):
                    bank, use = st.spot(f"e{pair}{u}")
                    pool.wait_ge(main_freed[bank], use + 1 + 1)
                g.tensor_tensor(wait_carrier[:, 0:1], wait_carrier[:, 1:2], wait_carrier[:, 1:2],
                                ALU.add).then_inc(probs_masked, 1)
                buffer = probs[:, pair % 4]
                for blocks, pattern in ((buffer[:, :, 0:P], [[0, BLOCKS], [1, P]]),
                                        (buffer[:, 1:5:3, 3 * P:], [[0, 2], [1, P]]),
                                        (buffer[:, 2, 2 * P:3 * P], [[1, P]])):
                    g.affine_select(out=blocks, in_=blocks, compare_op=ALU.is_ge, fill=0.0, base=0,
                                    pattern=pattern, channel_multiplier=-1).then_inc(probs_masked, 1)

            def low_parts(st, half):
                s = slice(2 * half, 2 * half + 2)
                pool.wait_ge(middle_ready, 2 * (st.b + 2) + half + 1)
                g.tensor_tensor(parts[:, 2, s, :], qk32[:, s, :], parts[:, 1, s, :],
                                ALU.subtract).then_inc(parts_ready, 1)

            def front(st):
                for half in range(2):
                    low_parts(st, half)

            def step(st, more):
                for pair in range(PAIRS):
                    mask_probs(st, pair)
                    if st.front and pair in (2, 3):
                        low_parts(st, pair - 2)
                    if st.tail and more and pair == 5:
                        residual(st.b + 1, 1 - st.p, st.half + st.p)

            residual(0, 0, 0)
            residual(1, 1, 0)
            sequences(pool, front, lambda s, p, nth: None, step, lambda st: None)

        @block.scalar
        def _(act):
            nc.scalar.preload_act_table_set("natural_log_exp_and_others")
            act.wait_ge(bias_ps, 1)
            nc.scalar.mul(bias_qk[:, 0:2], ps[:, OUTPUTS, 0:2], QK_SCALE)
            nc.scalar.copy(bias_qk[:, 2:4], ps[:, OUTPUTS, 2:4]).then_inc(bias_ok, 1)
            act.wait_ge(bias_ok, 1)

            def filled(st, name):
                bank, use = st.spot(name)
                act.wait_ge(main_filled[bank], use + 1)
                return ps[:, bank, :], main_freed[bank]

            def turn_x(st):
                src, free = filled(st, "x0")
                nc.scalar.copy(xT[:, 0, :], src).then_inc(free, 1)

            def project(st, kind):
                s = st.b + 2
                if kind == "q":
                    act.wait_ge(parts_ready, 2 * s + 1)
                    act.wait_ge(parts_stored, 96 * s + 1)
                scale = QK_SCALE if kind == "q" else 1.0
                for c in range(KC):
                    m = c + (0 if kind == "q" else KC)
                    src, free = filled(st, f"{kind}{c}")
                    nc.scalar.activation(qk32[:, m, :], src, ACT.Identity, bias=bias_qk[:, m:m + 1], scale=scale)
                    nc.scalar.activation(parts[:, 0, m, :], src, ACT.Identity, bias=bias_qk[:, m:m + 1],
                                         scale=scale).then_inc(free, 1)

            def front(st):
                turn_x(st)
                project(st, "q")
                project(st, "k")

            def maxima(s, p, nth):
                pass

            def heads(b, g):
                act.wait_ge(outputs_filled, 4 * b + g + 1)
                nc.scalar.copy(heads_out[:], ps[:, OUTPUTS, :]).then_inc(heads_ready, 1)

            def turn_attn(st):
                src, free = filled(st, "a0")
                nc.scalar.copy(attnT[:, 0, :], src).then_inc(free, 1)

            def tail(st):
                heads(st.b - 1, 3)
                turn_attn(st)
                rsqrt_guess(act, nc, norm, norm_sems, st.b - 1)

            def step(st, more):
                b = st.b
                for pair in range(PAIRS):
                    if pair in (4, 6):
                        heads(b, pair // 2 - 2)
                    for u in range(BLOCKS):
                        src, free = filled(st, f"e{pair}{u}")
                        nc.scalar.activation(probs[:, pair % 4, u, :], src, ACT.Exp).then_inc(free, 1)
                    if st.tail and pair == 0:
                        heads(b - 1, 3)
                    if st.tail and pair == 2:
                        turn_attn(st)
                    if st.front and pair == 1:
                        turn_x(st)
                    if st.front and pair == 2:
                        project(st, "q")
                    if st.tail and pair == 5:
                        rsqrt_guess(act, nc, norm, norm_sems, b - 1)
                    if st.front and pair == 3:
                        project(st, "k")
                heads(b, 2)

            sequences(act, front, maxima, step, tail)

        @block.vector
        def _(dve):
            v = nc.vector

            def filled(st, name):
                bank, use = st.spot(name)
                dve.wait_ge(main_filled[bank], use + 1)
                return ps[:, bank, :], main_freed[bank]

            def turn_x(st):
                src, free = filled(st, "x1")
                v.tensor_copy(xT[:, 1, :], src).then_inc(free, 1)

            def split(st, kind):
                half = 0 if kind == "q" else 1
                steps = Steps(1, 2 * (st.b + 2) + half)
                s = slice(2 * half, 2 * half + 2)
                for c in range(KC):
                    bank, use = st.spot(f"{kind}{c}")
                    dve.wait_ge(main_freed[bank], use + 1 + 1)
                v.tensor_tensor(qk32[:, s, :], qk32[:, s, :], parts[:, 0, s, :], ALU.subtract).then_inc(split_step, 1)
                dve.wait_ge(split_step, steps.next())
                v.tensor_copy(parts[:, 1, s, :], qk32[:, s, :]).then_inc(middle_ready, 1)

            def take_values(st, p):
                if isinstance(st.b, int) and st.b == -2:
                    dve.wait_ge(consts, 2)
                for c in range(2):
                    src, free = filled(st, f"v{c}")
                    for t in range(2):
                        last = v.tensor_tensor(
                            values[p][:, 2 * c + t, :, 0:HS],
                            src[:, t * D:(t + 1) * D].rearrange("p (h d) -> p h d", d=HS),
                            bias_v[:].rearrange("p (h d) -> p h d", d=HS), ALU.add)
                    last.then_inc(free, 1)

            def front(st):
                turn_x(st)
                split(st, "q")
                split(st, "k")
                take_values(st, st.p)

            def row_max(out, scores):
                return v.tensor_reduce(out, scores, AX.X, ALU.max, negate=True)

            def pair_maxima(s, pair):
                for u in range(BLOCKS):
                    k = BLOCKS * pair + u
                    dve.wait_ge(max_filled[k % 2], MAX_USES * s + k // 2 + 1)
                    bank, h = ps[:, MAXIMA + k % 2, :], 2 * pair + u // 3
                    if u in (0, 3):
                        last = row_max(neg_max[:, h, 3:4], bank)
                    elif u in (1, 4):
                        row_max(neg_max[:, h, 0:1], bank[:, 0:P])
                        last = row_max(neg_max[:, h, 2:3], bank[:, P:])
                    else:
                        last = row_max(neg_max[:, 2 * pair:2 * pair + 2, 1:2],
                                       bank.rearrange("p (a k) -> p a k", a=2))
                    last.then_inc(max_freed[k % 2], 1)

            def split_maxima(s):
                dve.wait_ge(turned_filled, 5 * s - 1 if not (isinstance(s, int) and s == 0) else 1)
                mx = ps[0:HEADS * NT, TURNED, 0:P]
                v.tensor_copy(max_parts[:, 0, :], mx).then_inc(max_step, 1)
                dve.wait_ge(max_step, s + 1)
                v.tensor_tensor(max_parts[:, 1, :], mx, max_parts[:, 0, :], ALU.subtract).then_inc(max_ready, 1)

            def maxima(s, p, nth):
                for pair in range(PAIRS):
                    pair_maxima(s, pair)
                split_maxima(s)

            def normalise_heads(b, g, after_maxima):
                dve.wait_ge(turned_filled, 5 * b + g + after_maxima + 2)
                o = ps[:, TURNED, :].rearrange("p (t j c) -> p t j c", t=NT, c=VW)
                v.reciprocal(rden[:], o[:, :, :, HS]).then_inc(attn_step, 1)
                dve.wait_ge(attn_step, 4 * b + g + 1)
                v.tensor_tensor(attn[:, :, g * 4 * HS:(g + 1) * 4 * HS].rearrange("p t (j d) -> p t j d", d=HS),
                                o[:, :, :, 0:HS], rden[:].unsqueeze(3).to_broadcast([P, NT, 4, HS]),
                                ALU.mult).then_inc(attn_ready, 1)

            def turn_attn(st):
                src, free = filled(st, "a1")
                v.tensor_copy(attnT[:, 1, :], src).then_inc(free, 1)

            def residual(st):
                dve.wait_ge(x_added, st.b)
                for u in range(2):
                    src, free = filled(st, f"o{u}")
                    v.tensor_tensor(res[:, 2 * u:2 * u + 2, :], src.rearrange("p (t d) -> p t d", d=D),
                                    xo[1 - st.p][:, 2 * u:2 * u + 2, :], ALU.add).then_inc(free, 1)
                for u in range(2):
                    bank, use = st.spot(f"o{u}")
                    dve.wait_ge(main_freed[bank], use + 1 + 1)
                v.memset(norm["tmp"][:], 0.0).then_inc(res_ready, 1)

            def finish(st, steps):
                reciprocal_root(dve, nc, norm_step, steps, norm, norm_sems[2], st.b - 1)
                dve.wait_ge(normed_stored, 16 * (st.b - 1) + 1)
                normalised(nc, normed, res, norm).then_inc(normed_ready, 1)

            def tail(st):
                normalise_heads(st.b - 1, 2, 0)
                normalise_heads(st.b - 1, 3, 0)
                turn_attn(st)
                residual(st)
                steps = Steps(NORM_STEPS, st.b - 1)
                variance(dve, nc, norm_step, steps, res, norm, norm_sems[0])
                finish(st, steps)

            def step(st, more):
                b = st.b
                for pair in range(PAIRS):
                    if more:
                        for m in MAX_AT[pair]:
                            pair_maxima(b + 1, m)
                    if st.tail and pair == 0:
                        normalise_heads(b - 1, 2, 1)
                    if st.late and pair == 0:
                        take_values(st, 1 - st.p)
                    if st.tail and pair == 1:
                        normalise_heads(b - 1, 3, 1)
                    if st.tail and pair == 2:
                        turn_attn(st)
                    if st.front and pair == 1:
                        turn_x(st)
                    if st.tail and pair == 3:
                        residual(st)
                    if st.front and pair == 2:
                        split(st, "q")
                    if st.tail and pair == 5:
                        steps = Steps(NORM_STEPS, b - 1)
                        variance(dve, nc, norm_step, steps, res, norm, norm_sems[0])
                    if pair in (4, 6):
                        normalise_heads(b, pair // 2 - 2, 0)
                    if more and pair == 6:
                        split_maxima(b + 1)
                    if st.front and pair == 3:
                        split(st, "k")
                if st.tail:
                    finish(st, steps)

            sequences(dve, front, maxima, step, tail)

        @block.tensor
        def _(pe):
            t_ = nc.tensor
            pe.wait_ge(consts, 1)
            pe.wait_ge(weights_in, 16 * WEIGHT_LOADS)
            for m in range(4):
                last = t_.matmul(ps[:, OUTPUTS, m:m + 1], bias_row[0:1, m // 2, (m % 2) * P:(m % 2 + 1) * P],
                                 one[0:1, 0:1], start=True, stop=True)
            last.then_inc(bias_ps, 1)

            def ring(st, name):
                bank, use = st.spot(name)
                pe.wait_ge(main_freed[bank], use + 1)
                return ps[:, bank, :], main_filled[bank]

            def freed(st, name, before):
                bank, use = st.spot(name)
                if st.spot(before)[0] != bank:
                    pe.wait_ge(main_freed[bank], use + 1 + 1)

            def turn(st, name, src):
                for c in range(KC):
                    dst, done = ring(st, f"{name}{c}")
                    for t in range(NT):
                        last = t_.transpose(dst[:, t * P:(t + 1) * P], src[:, t, c * P:(c + 1) * P], ident[:])
                    last.then_inc(done, 1)

            def turn_x(st):
                pe.wait_ge(x_full[st.p], 16 * (st.half + 2))
                turn(st, "x", x_in[st.p])

            def project(st, kind):
                if kind == "q":
                    freed(st, "x0", "q0")
                    freed(st, "x1", "q0")
                for m in range(KC):
                    dst, done = ring(st, f"{kind}{m}")
                    for c in range(KC):
                        last = t_.matmul(dst, wqk[:, c, 0 if kind == "q" else 1, m * P:(m + 1) * P],
                                         xT[:, c, :], start=(c == 0), stop=(c == KC - 1))
                    last.then_inc(done, 1)

            def project_rows(st, name, src, w):
                for u in range(2):
                    dst, done = ring(st, f"{name}{u}")
                    for t in range(2):
                        tok = slice((2 * u + t) * P, (2 * u + t + 1) * P)
                        for c in range(KC):
                            last = t_.matmul(dst[:, t * D:(t + 1) * D], src[:, c, tok], w[:, c, :],
                                             start=(c == 0), stop=(c == KC - 1))
                    last.then_inc(done, 1)

            def front(st):
                turn_x(st)
                project(st, "q")
                project(st, "k")
                project_rows(st, "v", xT, wv)

            def scores(out, stationary, moving, mask, at):
                t_.matmul(out, stationary, moving, start=True, stop=False)
                return t_.matmul(out[:, at:at + P], identb[:], mask, start=False, stop=True)

            def by_query(p, h, i, out):
                return scores(out, q_stack[p][0:STACK, h, i * P:(i + 1) * P], k_stack[p][0:STACK, h, 0:(i + 1) * P],
                              mask_q[:], i * P)

            def by_key(p, h, i, out):
                return t_.matmul(out, k_stack[p][:, h, i * P:(i + 1) * P], q_stack[p][:, h, i * P:TOK],
                                 start=True, stop=True)

            def fill(kind, p, pair, u, bank, blocks):
                four, one_and_three, two = blocks
                h = 2 * pair + u // 3
                if u in (0, 3):
                    return kind(p, h, four, bank)
                if u in (1, 4):
                    for i, cols in one_and_three:
                        last = kind(p, h, i, bank[:, cols])
                    return last
                kind(p, 2 * pair, two, bank[:, 0:2 * P])
                return kind(p, 2 * pair + 1, two, bank[:, 2 * P:])

            def fill_maxima(s, p, nth, pair, u):
                if u == 0 and pair in (0, PAIRS // 2):
                    pe.wait_ge(stack_full[p][pair // (PAIRS // 2)], 16 * 12 * (nth + 1))
                k = BLOCKS * pair + u
                pe.wait_ge(max_freed[k % 2], MAX_USES * s + k // 2 + 1)
                fill(by_query, p, pair, u, ps[:, MAXIMA + k % 2, :],
                     (3, ((0, slice(0, P)), (2, slice(P, 4 * P))), 1)).then_inc(max_filled[k % 2], 1)

            def pair_maxima(s, p, nth, pair):
                for u in range(BLOCKS):
                    fill_maxima(s, p, nth, pair, u)

            def turn_maxima(s):
                for k in range(2):
                    pe.wait_ge(max_freed[k], MAX_USES * (s + 1) + 1)
                if not (isinstance(s, int) and s == 0):
                    pe.wait_ge(attn_ready, 4 * (s - 1) + 2 + 1)
                t_.transpose(ps[:, TURNED, 0:P], neg_max[:].rearrange("p h t -> p (h t)"),
                             ident[:]).then_inc(turned_filled, 1)

            def maxima(s, p, nth):
                for pair in range(PAIRS):
                    pair_maxima(s, p, nth, pair)
                turn_maxima(s)

            def outputs(b, p, g):
                pe.wait_ge(probs_masked, 4 * (PAIRS * b + 2 * g + 2) + 1)
                pe.wait_ge(heads_ready, 4 * b + g + 1)
                for i in range(NT):
                    for j in range(4):
                        h, slot = 4 * g + j, (2 * g + j // 2) % 4
                        u0 = 3 * (j % 2)
                        src = {0: (u0, slice(0, TOK)), 1: (u0 + 1, slice(0, 3 * P)),
                               2: (2, slice((j % 2) * 2 * P, (j % 2 + 1) * 2 * P)),
                               3: (u0 + 1, slice(3 * P, TOK))}[i]
                        last = t_.matmul(ps[VW * j:VW * (j + 1), OUTPUTS, i * P:TOK], values[p][:, i, h, :],
                                         probs[:, slot, src[0], src[1]], start=(i == 0), stop=(i == NT - 1))
                last.then_inc(outputs_filled, 1)

            def turn_heads(b, g, after_maxima):
                pe.wait_ge(heads_ready, 4 * b + g + 1 + 1)
                if after_maxima:
                    pe.wait_ge(max_ready, b + 2 + 1)
                else:
                    pe.wait_ge(attn_ready, 4 * b + g + 1)
                for t in range(NT):
                    last = t_.transpose(ps[:, TURNED, t * P:(t + 1) * P], heads_out[:, t * P:(t + 1) * P], ident[:])
                last.then_inc(turned_filled, 1)

            def turn_attn(st):
                pe.wait_ge(attn_ready, 4 * st.b + 1)
                turn(st, "a", attn)

            def project_out(st):
                freed(st, "a0", "o0")
                freed(st, "a1", "o0")
                project_rows(st, "o", attnT, wo)

            def tail(st):
                turn_heads(st.b - 1, 2, False)
                outputs(st.b - 1, 1 - st.p, 3)
                turn_heads(st.b - 1, 3, False)
                turn_attn(st)
                project_out(st)

            def step(st, more):
                b, p = st.b, st.p
                if more:
                    pair_maxima(b + 1, 1 - p, st.half + p, 0)
                pe.wait_ge(max_rows_full[p], 32 * (st.half + 1))
                for pair in range(PAIRS):
                    for u in range(BLOCKS):
                        dst, done = ring(st, f"e{pair}{u}")
                        fill(by_key, p, pair, u, dst,
                             (0, ((1, slice(0, 3 * P)), (3, slice(3 * P, TOK))), 2)).then_inc(done, 1)
                        if more:
                            for m in MAX_AT[pair][-1:]:
                                fill_maxima(b + 1, 1 - p, st.half + p, m, u)
                    if st.tail and pair == 0:
                        turn_heads(b - 1, 2, True)
                        outputs(b - 1, 1 - p, 3)
                    if st.late and pair == 0:
                        project_rows(st, "v", xT, wv)
                    if st.tail and pair == 1:
                        turn_heads(b - 1, 3, False)
                    if st.tail and pair == 2:
                        turn_attn(st)
                    if st.front and pair == 1:
                        turn_x(st)
                    if st.tail and pair == 3:
                        project_out(st)
                    if st.front and pair == 2:
                        project(st, "q")
                    if st.front and pair == 3:
                        project(st, "k")
                    if pair in (3, 5, 7):
                        outputs(b, p, pair // 2 - 1)
                    if pair in (4, 6):
                        turn_heads(b, pair // 2 - 2, False)
                    if more and pair == 6:
                        turn_maxima(b + 1)

            sequences(pe, front, maxima, step, tail)


def experts(nc, w, normed_dram, out):
    with ExitStack() as ctx:
        def sb(name, shape, dt):
            return ctx.enter_context(nc.sbuf_tensor(name, shape, dt))

        primed = []

        def sem(name, start=0):
            s = ctx.enter_context(nc.semaphore(name))
            if start:
                primed.append((s, start))
            return s

        UPDATE_STEPS = {1: 3, 2: 5, 3: 0}
        DVE_STEPS = {1: 6 + EC, 2: 3 + EC, 3: 0}
        GROUPS, PAIR = SEQS, 2
        ps = ctx.enter_context(nc.psum_tensor("exp_ps", [P, 8, 512], F32))

        def ctrl_ps(s):
            return ps[:, 2 + 2 * s:4 + 2 * s, :].rearrange("p a n -> p (a n)")

        def spare_ps(s):
            return ps[:, 3 + 2 * s, :]

        w1 = sb("w1", [P, 2, 2 * KC, HCOLS], F16)
        w2 = sb("w2", [P, 2, EC, CTRL], F16)
        w2_shared_top = sb("w2_shared_top", [P, CTRL], F16)
        w2_shared_low = sb("w2_shared_low", [P, CTRL], F16)
        b2_parts = sb("b2_parts", [P, CTRL], F16)
        rf1 = sb("rf1", [P, 2, KC, RH], F16)
        rf2 = sb("rf2", [P, 2, RC, D], F16)
        wrh = sb("wrh", [P, KC, P], F32)
        w2rh = sb("w2rh", [P, E + 1], F32)
        b1 = sb("b1", [P, FC], F32)
        rf_b1 = sb("rf_b1", [P, RC], F32)
        brh = sb("brh", [P, 1], F32)
        b2rh = sb("b2rh", [P, E + 1], F32)
        mu = sb("mu", [P, D], F32)
        iw = sb("iw", [P, D], F32)
        rf_b2 = sb("rf_b2", [P, D], F32)
        half = sb("half", [P, 1], F32)
        gate_in = sb("gate_in", [P, 1], F32)
        gate_t = sb("gate_t", [P, 1], F32)
        gate = sb("gate", [P, 2], F32)
        ident = sb("e_ident", [P, P], F32)
        identb = sb("e_identb", [P, P], F16)
        spread = sb("spread", [P, EC, P], F16)
        numbers = sb("numbers", [P, 3, E], F32)

        def two(name, shape, dt):
            return [sb(f"{name}{g}", shape, dt) for g in range(PAIR)]

        x1 = two("x1", [P, NT, D], F32)
        x2 = two("x2", [P, NT, D], F32)
        vh = two("vh", [P, NT, D], F32)
        xTp = two("xTp", [P, 2, KC, TOK], F16)
        vTp = two("vTp", [P, 2, KC, TOK], F16)
        onehot = two("onehot", [P, NT, 2, 3, E], F16)
        onehotT = two("onehotT", [P, 2, TOK], F16)
        masks = two("masks", [P, 2, EC, TOK], F16)
        weights = two("weights", [P, NT, STREAMS], F32)
        nw = two("nw", [P, NT, STREAMS], F32)
        nwx = two("nwx", [P, NT, STREAMS], F32)
        xT32 = sb("xT32", [P, KC, TOK], F32)
        xm = sb("xm", [P, NT, D], F32)
        v_or_res = sb("v_or_res", [P, KC * TOK], F32)
        vT32 = v_or_res[:].rearrange("p (c n) -> p c n", c=KC)
        res = v_or_res[:].rearrange("p (t d) -> p t d", t=NT)
        rh = sb("rh", [P, TOK], F32)
        g32 = sb("g32", [P, FC, TOK], F32)
        gp = sb("gp", [P, 2, EC, TOK], F16)
        routed = sb("routed", [P, 2, 2, EC, TOK], F16)
        shared_hl = sb("shared_hl", [P, TOK], F16)
        shared_h1 = sb("shared_h1", [P, TOK], F16)
        ctrl = sb("ctrl", [P, NT, STREAMS, CTRL], F32)
        sp = sb("sp", [P, NT, STREAMS, D], F32)
        logits = sb("logits", [P, NT, E + 1], F32)
        top = sb("top", [P, NT, 8], F32)
        top_at = sb("top_at", [P, NT, 8], U32)
        top_f = sb("top_f", [P, NT, 2], F32)
        gates = sb("gates", [P, NT, 2], F32)
        gates_t = sb("gates_t", [P, NT, 2], F32)
        halt = sb("halt", [P, NT], F32)
        norm = norm_buffers(sb, "exp")
        final = sb("final", [P, NT, D], F32)

        biases_in = sem("biases_in")
        w1_in = sem("w1_in")
        small_in = sem("small_in")
        w2_in = sem("w2_in")
        refine_in = sem("refine_in")
        const_step = sem("e_const_step")
        consts = sem("e_consts")
        setup_step = sem("setup_step")
        gate_ready = sem("gate_ready")
        biases_split = sem("biases_split")
        w1_high = sem("w1_high")
        w1_ready = sem("w1_ready")
        w2_high = sem("w2_high")
        w2_ready = sem("w2_ready")
        refine_high = sem("refine_high")
        refine_ready = sem("refine_ready")
        rows_in = sem("rows_in")
        x_full = [sem(f"e_x_full{g}") for g in range(PAIR)]
        ring_filled = [sem(f"ring_filled{i}") for i in range(2)]
        ring_freed = [sem(f"ring_freed{i}", 1) for i in range(2)]
        spare_filled = [sem(f"spare_filled{s}") for s in range(STREAMS)]
        spare_freed = [sem(f"spare_freed{s}") for s in range(STREAMS)]
        ctrl_filled = [sem(f"ctrl_filled{s}") for s in range(STREAMS)]
        ctrl_freed = [sem(f"ctrl_freed{s}", 1) for s in range(STREAMS)]
        xlow_ready = sem("xlow_ready", 1)
        vlow_ready = sem("vlow_ready", 1)
        gates_ready = sem("gates_ready")
        gates_done = sem("gates_done")
        weights_done = sem("weights_done")
        onehot_ready = sem("onehot_ready")
        h_ready = sem("h_ready", 1)
        tanh_done = sem("tanh_done")
        abs_ready = sem("abs_ready")
        ln_ready = sem("ln_ready")
        xm_ready = sem("xm_ready")
        spx_ready = sem("spx_ready", 1)
        x1_kept = sem("x1_kept")
        pool_step = sem("pool_step")
        tile_done = sem("tile_done", NT)
        dve_step = sem("dve_step")
        refine_step = sem("refine_step")
        update_step = sem("update_step")
        norm_step = sem("e_norm_step")
        norm_sems = (sem("e_var_ready"), sem("e_rstd_step"), sem("e_rstd_raw"))
        res_ready = sem("e_res_ready")
        final_ready = sem("final_ready", 1)
        final_stored = sem("final_stored", 1)

        FIRST = [(1, 0), (1, 1)]
        ROUND = [(2, 0), (2, 1), (3, 0), (1, 0), (3, 1), (1, 1)]
        LAST = [(2, 0), (2, 1), (3, 0), (3, 1)]
        ROUNDS = GROUPS // PAIR - 1
        SPARE = (0, 1, 2)
        FILLS = {1: ["x0", "x1", "rh", "h4", "logits", "onehot", "mask00", "mask10", "mask01", "mask11", "h3",
                     "mask02", "mask12", "mask03", "mask13"],
                 2: ["x0", "x1", "v0", "v1", "rh", "h4", "logits", "h0", "h1", "h2", "h3"],
                 3: ["x0", "x1", "h0", "h1", "h2", "h3"]}

        class Stage:

            def __init__(self, order, at, i):
                self.order, self.at, self.i = order, at, i
                self.it, self.g = order[at]
                self.pair = 0 if i is None else i + 1 if order is ROUND and self.it == 1 else i

            def before(self, of):
                here = sum(of(it) for it, _ in self.order[:self.at])
                if self.i is None:
                    return here
                return self.i * sum(of(it) for it, _ in ROUND) + (sum(of(it) for it, _ in FIRST) + here)

            def kinds(self, *its):
                return self.before(lambda it: it in its)

            @property
            def controls(self):
                return self.kinds(1, 2)

            def slot_uses(self, s):
                return self.before(lambda it: NT if it < 3 else int(s < 2))

            def spot(self, what):
                n = sum(len(FILLS[it]) for it, _ in self.order[:self.at]) + FILLS[self.it].index(what)
                if self.i is None:
                    return n % 2, n // 2
                first, each = (sum(len(FILLS[it]) for it, _ in o) for o in (FIRST, ROUND))
                assert first % 2 == each % 2 == 0
                return n % 2, self.i * (each // 2) + (first // 2 + n // 2)

            @property
            def last_stage(self):
                if self.at:
                    return Stage(self.order, self.at - 1, self.i)
                if self.i is None:
                    return None
                if isinstance(self.i, int) and self.i == 0:
                    return Stage(FIRST, 1, None)
                return Stage(ROUND, len(ROUND) - 1, self.i - 1)

            @property
            def next_stage(self):
                if self.at + 1 < len(self.order):
                    return Stage(self.order, self.at + 1, self.i)
                if self.order is FIRST:
                    return Stage(ROUND, 0, 0)
                return Stage(ROUND, 0, self.i + 1) if self.order is ROUND else None

            @property
            def ends_alone(self):
                return self.order is LAST and self.it == 3

        DVE_MASKS = (0,)

        def hs(it):
            return FC if it < 3 else RC

        SMALL = 2 + 1 + 2 + 4 + 4 + 1
        block = ctx.enter_context(nc.Block())
        x_dram = normed_dram.rearrange("s (t p) d -> s p t d", p=P)
        out_dram = out.rearrange("s (t p) d -> s p t d", p=P)
        stage = ctrl[:].rearrange("p t s n -> p (t s n)")
        at = 0

        def staged(shape):
            nonlocal at
            n = shape[0] * shape[1]
            view = stage[:, at:at + n].rearrange("p (a b) -> p a b", a=shape[0])
            at += n
            return view

        W1_COLS = (E + 1) * HID
        w1_32, w2_32, w2s_32 = staged((2 * KC, W1_COLS)), staged((EC, CTRL)), staged((1, CTRL))
        b2_32 = staged((1, CTRL))
        b2e32, b2s32 = b2_32[0:E, 0, :], b2_32[32:33, 0, :]
        b2_split = sp[:].rearrange("p t s d -> p (t s d)").bitcast(F16)[:, 0:3 * CTRL].rearrange(
            "p (a n) -> p a n", a=3)
        b2e_split, b2s_split = b2_split[0:E], b2_split[32:33]
        stage, at = masks[1][:].rearrange("p k c n -> p (k c n)").bitcast(F32), 0
        rf1_32, rf2_32 = staged((KC, RH)), staged((RC, D))

        def stages(eng, stage):
            for at in range(len(FIRST)):
                stage(Stage(FIRST, at, None))
            with eng.Fori(0, ROUNDS) as i:
                for at in range(len(ROUND)):
                    stage(Stage(ROUND, at, i))
            for at in range(len(LAST)):
                stage(Stage(LAST, at, ROUNDS))

        @block.sync
        def _(sync):
            for s, start in primed:
                sync.sem_inc(s, start)
            def load(dst, src, loaded):
                sync.dma_start(dst, src).then_inc(loaded, 16)

            load(x1[0][:], x_dram[0], x_full[0])
            load(b2e32, w["expert_b2"], biases_in)
            load(b2s32, w["shared_b2"].unsqueeze(0), biases_in)
            for c in range(2 * KC):
                load(w1_32[:, c, 0:E * HID].rearrange("p (e h) -> p e h", h=HID),
                     w["expert_w1"].rearrange("e (c p) h -> c p e h", p=P)[c], w1_in)
            load(w1_32[:, :, E * HID:], w["shared_w1"].rearrange("(c p) h -> p c h", p=P), w1_in)
            load(wrh[:, :, 0:HID], w["router_w1"].rearrange("(c p) n -> p c n", p=P), small_in)
            load(wrh[:, :, HID:P], w["halt_w1"].rearrange("(c p) n -> p c n", p=P), small_in)
            load(gate_in[:], w["shared_weight"].partition_broadcast(P), small_in)
            with nc.allow_non_contiguous_dma(reason="biases as columns"):
                load(brh[0:HID, :], w["router_b1"].unsqueeze(1), small_in)
                load(brh[HID:P, :], w["halt_b1"].unsqueeze(1), small_in)
                load(b1[:, 0:EC], w["expert_b1"].rearrange("e h -> (e h)").rearrange("(c p) -> p c", p=P), small_in)
                for r in range(2):
                    load(b1[r * HID:(r + 1) * HID, EC:FC], w["shared_b1"].unsqueeze(1), small_in)
                load(rf_b1[:], w["refine_b1"].rearrange("(c p) -> p c", p=P), small_in)
            sync.wait_ge(consts, 1)
            load(w2rh[0:HID, 0:E], w["router_w2"], small_in)
            load(w2rh[HID:P, E:E + 1], w["halt_w2"], small_in)
            load(b2rh[:, 0:E], w["router_b2"].partition_broadcast(P), small_in)
            load(b2rh[:, E:E + 1], w["halt_b2"].partition_broadcast(P), small_in)
            load(mu[:], w["mu"].partition_broadcast(P), small_in)
            load(w2_32, w["expert_w2"].rearrange("e h n -> (e h) n").rearrange("(c p) n -> p c n", p=P), w2_in)
            for r in range(2):
                load(w2s_32[r * HID:(r + 1) * HID, 0, :], w["shared_w2"], w2_in)
            sync.wait_ge(consts, 2)
            sync.wait_ge(biases_split, 1)
            for part in range(3):
                load(w2_shared_low[HID + part:HID + part + 1, :], b2s_split[:, part, :], rows_in)
                load(b2_parts[part * E:(part + 1) * E, :], b2e_split[:, part, :], rows_in)
            load(x1[1][:], x_dram[1], x_full[1])
            load(rf1_32, w["refine_w1"].rearrange("(c p) n -> p c n", p=P), refine_in)
            load(rf2_32, w["refine_w2"].rearrange("(c p) n -> p c n", p=P), refine_in)
            load(iw[:], w["integration_weight"].partition_broadcast(P), refine_in)
            load(rf_b2[:], w["refine_b2"].partition_broadcast(P), refine_in)

            def store(i, g):
                sync.wait_ge(final_ready, PAIR * i + g + 1 + 1)
                sync.dma_start(out_dram[PAIR * i + g], final[:]).then_inc(final_stored, 16)

            def reload(i, g):
                sync.wait_ge(x1_kept, PAIR * i + g + 1)
                sync.dma_start(x1[g][:], x_dram[PAIR * (i + 1) + g]).then_inc(x_full[g], 16)

            with sync.Fori(0, ROUNDS) as i:
                for g in range(PAIR):
                    reload(i, g)
                for g in range(PAIR):
                    store(i, g)
            for g in range(PAIR):
                store(ROUNDS, g)
            sync.wait_ge(final_stored, 16 * GROUPS + 1)

        @block.gpsimd
        def _(pool):
            steps = Steps(0, 0)
            gp_ = nc.gpsimd
            gp_.memset(w2rh[:], 0.0).then_inc(consts, 1)
            pool.wait_ge(consts, 1)
            gp_.memset(ident[:], 1.0).then_inc(const_step, 1)
            pool.wait_ge(const_step, steps.next())
            gp_.affine_select(out=ident[:], in_=ident[:], compare_op=ALU.is_equal, fill=0.0,
                              base=0, pattern=[[-1, P]], channel_multiplier=1).then_inc(const_step, 1)
            pool.wait_ge(const_step, steps.next())
            gp_.tensor_copy(identb[:], ident[:]).then_inc(const_step, 1)
            pool.wait_ge(const_step, steps.next())
            gp_.memset(half[:], 0.5).then_inc(const_step, 1)
            pool.wait_ge(const_step, steps.next())
            gp_.memset(spread[:], 1.0).then_inc(const_step, 1)
            pool.wait_ge(const_step, steps.next())
            gp_.affine_select(out=spread[:], in_=spread[:], compare_op=ALU.is_equal, fill=0.0, base=0,
                              pattern=[[-2, EC], [-1, 2], [0, HID]], channel_multiplier=1).then_inc(const_step, 1)
            pool.wait_ge(const_step, steps.next())
            for e in range(E):
                gp_.memset(numbers[:, :, e:e + 1], float(e)).then_inc(const_step, 1)
                pool.wait_ge(const_step, steps.next())
            for g in range(PAIR):
                gp_.memset(onehotT[g][:], 0.0).then_inc(const_step, 1)
                pool.wait_ge(const_step, steps.next())
            gp_.memset(b2_parts[:], 0.0).then_inc(const_step, 1)
            pool.wait_ge(const_step, steps.next())
            gp_.memset(w2_shared_low[:], 0.0).then_inc(const_step, 1)
            pool.wait_ge(const_step, steps.next())
            gp_.memset(shared_h1[:], 1.0).then_inc(consts, 1)
            pool.wait_ge(consts, 2)
            pool.wait_ge(refine_in, 16 * 4)
            gp_.tensor_copy(rf1[:, 0], rf1_32).then_inc(refine_high, 1)
            pool.wait_ge(refine_high, 1)
            gp_.tensor_copy(rf2[:, 0], rf2_32).then_inc(refine_high, 1)
            pool.wait_ge(refine_high, 2)
            gp_.tensor_tensor(rf1[:, 1], rf1_32, rf1[:, 0], ALU.subtract).then_inc(refine_ready, 1)
            pool.wait_ge(refine_ready, 1)
            gp_.tensor_tensor(rf2[:, 1], rf2_32, rf2[:, 0], ALU.subtract).then_inc(refine_ready, 1)
            pool.wait_ge(refine_ready, 2)
            pool.wait_ge(small_in, 16 * SMALL)

            def keep_x1(st):
                bank, use = st.spot("x1")
                pool.wait_ge(ring_filled[bank], use + 1)
                gp_.tensor_tensor(x2[st.g][:], x1[st.g][:], x1[st.g][:], ALU.add).then_inc(x1_kept, 1)

            def residual(st):
                n = st.kinds(3)
                for u in range(2):
                    pool.wait_ge(ctrl_freed[u], st.slot_uses(u) + 1 + 1)
                gp_.tensor_tensor(res[:], res[:], iw[:].unsqueeze(1).to_broadcast([P, NT, D]),
                                  ALU.mult).then_inc(refine_step, 1)
                pool.wait_ge(refine_step, n + 1)
                pool.wait_ge(x1_kept, n + 1)
                gp_.tensor_tensor(res[:], res[:], x2[st.g][:], ALU.add).then_inc(res_ready, 1)

            def stage(st):
                n, g, last, nxt = st.controls, st.g, st.last_stage, st.next_stage
                if st.it == 3:
                    if st.ends_alone:
                        residual(st)
                    if nxt and nxt.it == 3:
                        keep_x1(nxt)
                    return
                if st.it == 1:
                    pool.wait_ge(x_full[g], 16 * (st.pair + 1))
                else:
                    pool.wait_ge(tile_done, NT * (n - 1) + NT)
                pool.wait_ge(spx_ready, NT * n + 1)
                src = x1 if st.it == 1 else x2
                gp_.tensor_tensor(xm[:], src[g][:], mu[:].unsqueeze(1).to_broadcast([P, NT, D]),
                                  ALU.subtract).then_inc(xm_ready, 1)
                pool.wait_ge(xm_ready, n + 1)
                if last and last.it == 3:
                    residual(last)
                for t in range(NT):
                    if t == 2 and nxt.it == 3:
                        keep_x1(nxt)
                    pool.wait_ge(ln_ready, NT * n + t + 1)
                    gp_.tensor_tensor(sp[:, t], sp[:, t], ctrl[:, t, :, D:2 * D], ALU.subtract).then_inc(pool_step, 1)
                    pool.wait_ge(pool_step, NT * n + t + 1)
                    gp_.tensor_tensor(sp[:, t], sp[:, t], xm[:, t, :].unsqueeze(1).to_broadcast([P, STREAMS, D]),
                                      ALU.mult).then_inc(spx_ready, 1)

            stages(pool, stage)

        @block.scalar
        def _(act):
            nc.scalar.preload_act_table_set("gelu_and_others")
            act.wait_ge(w1_in, 16 * (2 * KC + 1))
            nc.scalar.copy(w1[:, 0, :, 0:W1_COLS], w1_32)
            nc.scalar.copy(w1[:, 0, :, W1_COLS:], w1_32[:, :, E * HID:]).then_inc(w1_high, 1)
            act.wait_ge(small_in, 16 * SMALL)
            nc.scalar.activation(gate_t[:], gate_in[:], ACT.Tanh, scale=0.5).then_inc(gate_ready, 1)

            def filled(st, what):
                bank, use = st.spot(what)
                act.wait_ge(ring_filled[bank], use + 1)
                return ps[:, bank, :], ring_freed[bank]

            def transposed(st):
                g = st.g
                act.wait_ge(xlow_ready, st.kinds(1, 2, 3) + 1)
                for c in range(KC):
                    src, free = filled(st, f"x{c}")
                    nc.scalar.copy(xT32[:, c, :], src)
                    nc.scalar.copy(xTp[g][:, 0, c, :], src).then_inc(free, 1)
                if st.it == 2:
                    act.wait_ge(vlow_ready, st.kinds(2) + 1)
                    act.wait_ge(final_ready, st.kinds(3) + 1)
                    for c in range(KC):
                        src, free = filled(st, f"v{c}")
                        nc.scalar.copy(vT32[:, c, :], src)
                        nc.scalar.copy(vTp[g][:, 0, c, :], src).then_inc(free, 1)

            def gelu(st, c):
                bias = b1 if st.it < 3 else rf_b1
                if st.it == 1 and c in SPARE:
                    act.wait_ge(spare_filled[c], st.kinds(1) + 1)
                    src, free = spare_ps(c), spare_freed[c]
                else:
                    src, free = filled(st, f"h{c}")
                nc.scalar.activation(g32[:, c, :], src, ACT.Gelu, bias=bias[:, c:c + 1])
                high = shared_hl[:] if c == EC else gp[:, 0, c, :]
                nc.scalar.activation(high, src, ACT.Gelu, bias=bias[:, c:c + 1]).then_inc(free, 1)

            def softplus_logs(st, tiles, refined=None):
                n = st.controls
                nc.scalar.preload_act_table_set("natural_log_exp_and_others")
                for t in tiles:
                    act.wait_ge(abs_ready, STREAMS * (NT * n + t + 1))
                    b = ctrl[:, t, :, D:2 * D]
                    nc.scalar.activation(b, b, ACT.Ln, scale=0.5, bias=half[:, 0:1]).then_inc(ln_ready, 1)
                if refined:
                    rsqrt_guess(act, nc, norm, norm_sems, refined.kinds(3))
                nc.scalar.preload_act_table_set("gelu_and_others")

            def tanhs(st, t):
                act.wait_ge(tile_done, NT * (st.controls - 1) + t + 1 + NT)
                for s in range(STREAMS):
                    act.wait_ge(ctrl_filled[s], st.slot_uses(s) + t + 1)
                    cols = slice(0, CTRL) if st.it == 2 else slice(D, CTRL)
                    width = CTRL if st.it == 2 else 2 * D
                    nc.scalar.activation(ctrl[:, t, s, cols], ctrl_ps(s)[:, 0:width], ACT.Tanh,
                                         scale=0.5).then_inc(tanh_done, 1)

            def stage(st):
                it, g, n, last, nxt = st.it, st.g, st.controls, st.last_stage, st.next_stage
                if it < 3:
                    src, free = filled(st, "rh")
                    nc.scalar.activation(rh[:], src, ACT.Gelu, bias=brh[:, 0:1]).then_inc(free, 1)
                act.wait_ge(h_ready, st.before(hs) + 1)
                if last and last.it == 3:
                    act.wait_ge(ctrl_filled[1], last.slot_uses(1) + 1)
                if it < 3:
                    gelu(st, EC)
                    gelu(st, 0)
                    act.wait_ge(gates_ready, n + 1)
                    nc.scalar.activation(gates_t[:], gates[:], ACT.Tanh, scale=0.5).then_inc(gates_done, 1)
                else:
                    gelu(st, 0)
                for c in range(1, EC if it < 3 else RC):
                    gelu(st, c)
                    if it == 1 and c in (1, 3):
                        for m in (c - 1, c):
                            for k in range(1 if m in DVE_MASKS else 2):
                                src, free = filled(st, f"mask{k}{m}")
                                nc.scalar.copy(masks[g][:, k, m, :], src).then_inc(free, 1)
                if nxt and it == 3 and nxt.it < 3:
                    transposed(nxt)
                if last and last.it < 3:
                    softplus_logs(last, (2, 3))
                if it < 3:
                    tanhs(st, 0)
                    tanhs(st, 1)
                    softplus_logs(st, (0, 1), last if last and last.it == 3 else None)
                    tanhs(st, 2)
                    transposed(nxt)
                    tanhs(st, 3)
                elif st.ends_alone:
                    if nxt:
                        transposed(nxt)
                    nc.scalar.preload_act_table_set("natural_log_exp_and_others")
                    rsqrt_guess(act, nc, norm, norm_sems, st.kinds(3))
                    nc.scalar.preload_act_table_set("gelu_and_others")

            transposed(Stage(FIRST, 0, None))
            act.wait_ge(w2_in, 16 * 3)
            nc.scalar.copy(w2[:, 0], w2_32)
            nc.scalar.copy(w2_shared_top[:], w2s_32[:, 0, :]).then_inc(w2_high, 1)
            stages(act, stage)

        @block.vector
        def _(dve):
            v = nc.vector
            setup = Steps(0, 0)
            dve.wait_ge(biases_in, 16 * 2)
            v.tensor_copy(b2e_split[:, 0, :], b2e32)
            v.tensor_copy(b2s_split[:, 0, :], b2s32).then_inc(setup_step, 1)
            dve.wait_ge(setup_step, setup.next())
            v.tensor_tensor(b2e32, b2e32, b2e_split[:, 0, :], ALU.subtract)
            v.tensor_tensor(b2s32, b2s32, b2s_split[:, 0, :], ALU.subtract).then_inc(setup_step, 1)
            dve.wait_ge(setup_step, setup.next())
            v.tensor_copy(b2e_split[:, 1, :], b2e32)
            v.tensor_copy(b2s_split[:, 1, :], b2s32).then_inc(setup_step, 1)
            dve.wait_ge(setup_step, setup.next())
            v.tensor_tensor(b2e_split[:, 2, :], b2e32, b2e_split[:, 1, :], ALU.subtract)
            v.tensor_tensor(b2s_split[:, 2, :], b2s32, b2s_split[:, 1, :],
                            ALU.subtract).then_inc(biases_split, 1)
            dve.wait_ge(w1_high, 1)
            v.tensor_tensor(w1[:, 1, :, 0:W1_COLS], w1_32, w1[:, 0, :, 0:W1_COLS], ALU.subtract)
            v.tensor_tensor(w1[:, 1, :, W1_COLS:], w1_32[:, :, E * HID:], w1[:, 0, :, W1_COLS:],
                            ALU.subtract).then_inc(w1_ready, 1)
            dve.wait_ge(consts, 2)
            dve.wait_ge(gate_ready, 1)
            v.tensor_scalar(gate[:, 0:1], gate_t[:], 0.5, 0.5, ALU.mult, ALU.add)
            v.tensor_scalar(gate[:, 1:2], gate_t[:], -0.5, 0.5, ALU.mult, ALU.add).then_inc(setup_step, 1)
            dve.wait_ge(setup_step, setup.next())

            def filled(st, what):
                bank, use = st.spot(what)
                dve.wait_ge(ring_filled[bank], use + 1)
                return ps[:, bank, :], ring_freed[bank]

            def freed(st, what):
                bank, use = st.spot(what)
                dve.wait_ge(ring_freed[bank], use + 1 + 1)

            def low_parts(st):
                g = st.g
                freed(st, "x0")
                freed(st, "x1")
                v.tensor_tensor(xTp[g][:, 1], xT32[:], xTp[g][:, 0], ALU.subtract).then_inc(xlow_ready, 1)
                if st.it == 2:
                    freed(st, "v0")
                    freed(st, "v1")
                    v.tensor_tensor(vTp[g][:, 1], vT32[:], vTp[g][:, 0], ALU.subtract).then_inc(vlow_ready, 1)

            def route(st, chain):
                it, g, n = st.it, st.g, st.controls
                src, free = filled(st, "logits")
                v.tensor_tensor(logits[:], src[:, 0:NT * 16].rearrange("p (t c) -> p t c", t=NT)[:, :, 0:E + 1],
                                b2rh[:].unsqueeze(1).to_broadcast([P, NT, E + 1]), ALU.add).then_inc(free, 1)
                freed(st, "logits")
                if it == 1:
                    v.memset(top_f[:], 0.0)
                    for t in range(NT):
                        last = v.max(top[:, t, :], logits[:, t, 0:E])
                    last.then_inc(dve_step, 1)
                    dve.wait_ge(dve_step, chain.next())
                    v.tensor_tensor(gates[:, :, 0], top[:, :, 0], top[:, :, 1], ALU.subtract)
                v.tensor_copy(gates[:, :, 1], logits[:, :, E]).then_inc(gates_ready, 1)
                if it == 1:
                    for t in range(NT):
                        last = v.max_index(top_at[:, t, :], top[:, t, :], logits[:, t, 0:E])
                    last.then_inc(dve_step, 1)
                    dve.wait_ge(dve_step, chain.next())
                    v.tensor_copy(top_f[:], top_at[:, :, 0:2]).then_inc(dve_step, 1)
                    dve.wait_ge(dve_step, chain.next())
                    for t in range(NT):
                        for k in range(2):
                            last = v.tensor_scalar(onehot[g][:, t, k], numbers[:], top_f[:, t, k:k + 1], None,
                                                   ALU.is_equal)
                    last.then_inc(onehot_ready, 1)

            def stream_weights(st, chain):
                it, g, n = st.it, st.g, st.controls
                dve.wait_ge(gates_done, n + 1)
                if it == 1:
                    v.tensor_scalar(weights[g][:, :, 1], gates_t[:, :, 0], 0.5, 0.5, ALU.mult, ALU.add)
                    v.tensor_scalar(weights[g][:, :, 2], gates_t[:, :, 0], -0.5, 0.5, ALU.mult,
                                    ALU.add).then_inc(dve_step, 1)
                    dve.wait_ge(dve_step, chain.next())
                    v.tensor_scalar(weights[g][:, :, 1:3], weights[g][:, :, 1:3], gate[:, 1:2], None, ALU.mult)
                    v.tensor_copy(weights[g][:, :, 0], gate[:, 0:1].to_broadcast([P, NT]))
                v.tensor_scalar(halt[:], gates_t[:, :, 1], -0.5, -0.5, ALU.mult, ALU.add).then_inc(dve_step, 1)
                dve.wait_ge(dve_step, chain.next())
                v.tensor_tensor(nw[g][:], weights[g][:], halt[:].unsqueeze(2).to_broadcast([P, NT, STREAMS]),
                                ALU.mult).then_inc(dve_step, 1)
                dve.wait_ge(dve_step, chain.next())
                v.tensor_scalar(nwx[g][:], nw[g][:], 0.5 * DT, None, ALU.mult).then_inc(weights_done, 1)
                dve.wait_ge(weights_done, n + 1)

            def hidden(st, chain):
                it, g = st.it, st.g
                freed(st, f"h{EC}")
                v.tensor_copy(shared_h1[0:HID, :], shared_hl[0:HID, :])
                v.tensor_tensor(shared_hl[HID:P, :], g32[HID:P, EC, :], shared_hl[HID:P, :],
                                ALU.subtract).then_inc(h_ready, 1)
                if it == 1:
                    src, free = filled(st, "onehot")
                    v.tensor_copy(onehotT[g][0:3 * E].rearrange("p k n -> p (k n)"),
                                  src[0:3 * E, :].bitcast(F16)).then_inc(free, 1)
                for c in range(EC):
                    if it == 1 and c in SPARE:
                        dve.wait_ge(spare_freed[c], st.kinds(1) + 1)
                    else:
                        freed(st, f"h{c}")
                    v.tensor_tensor(gp[:, 1, c, :], g32[:, c, :], gp[:, 0, c, :], ALU.subtract).then_inc(dve_step, 1)
                    dve.wait_ge(dve_step, chain.next())
                    if it == 1:
                        freed(st, f"mask0{c}")
                        if c in DVE_MASKS:
                            src, free = filled(st, f"mask1{c}")
                            v.tensor_copy(masks[g][:, 1, c, :], src).then_inc(free, 1)
                        freed(st, f"mask1{c}")
                    for k in range(2):
                        last = v.tensor_tensor(routed[:, k, :, c, :], gp[:, :, c, :],
                                               masks[g][:, k, c, :].unsqueeze(1).to_broadcast([P, 2, TOK]), ALU.mult)
                    last.then_inc(h_ready, 1)

            def control(st, t):
                it, g, n = st.it, st.g, st.controls
                for s in range(STREAMS):
                    dve.wait_ge(tanh_done, STREAMS * (NT * n + t) + s + 1)
                    at_b = D if it == 2 else 0
                    v.tensor_scalar(sp[:, t, s, :], ctrl_ps(s)[:, at_b:at_b + D], 0.0, None,
                                    ALU.max).then_inc(ctrl_freed[s], 1)
                    b = ctrl[:, t, s, D:2 * D]
                    v.scalar_tensor_tensor(b, b, -1.0, b, ALU.mult, ALU.max).then_inc(abs_ready, 1)

            def update(st, t):
                it, g, n = st.it, st.g, st.controls
                steps = Steps(UPDATE_STEPS[it], t, st.before(lambda it: NT * UPDATE_STEPS[it]))
                a, gg = ctrl[:, t, :, 0:D], ctrl[:, t, :, 2 * D:]
                dve.wait_ge(spx_ready, NT * n + t + 1 + 1)
                if it == 2:
                    v.scalar_tensor_tensor(a, a, 1.0, vh[g][:, t, :].unsqueeze(1).to_broadcast(
                 [P, STREAMS, D]), ALU.add, ALU.mult).then_inc(update_step, 1)
                    dve.wait_ge(update_step, steps.next())
                    v.tensor_tensor(sp[:, t], sp[:, t], a, ALU.subtract).then_inc(update_step, 1)
                    dve.wait_ge(update_step, steps.next())
                v.scalar_tensor_tensor(gg, gg, 1.0, sp[:, t], ALU.add, ALU.mult).then_inc(update_step, 1)
                dve.wait_ge(update_step, steps.next())
                src = x1 if it == 1 else x2
                x_new, v_new = x2[g][:, t, :], vh[g][:, t, :]
                for s in range(STREAMS):
                    if it == 1:
                        if s == 0:
                            v.tensor_scalar(v_new, sp[:, t, s, :], nw[g][:, t, s:s + 1], None, ALU.mult)
                        else:
                            v.scalar_tensor_tensor(v_new, sp[:, t, s, :], nw[g][:, t, s:s + 1], v_new,
                                                   ALU.mult, ALU.add)
                    last = v.scalar_tensor_tensor(x_new, ctrl[:, t, s, 2 * D:], nwx[g][:, t, s:s + 1],
                                                  src[g][:, t, :] if s == 0 else x_new, ALU.mult, ALU.add)
                    if s < 2:
                        last.then_inc(update_step, 1)
                        dve.wait_ge(update_step, steps.next())
                last.then_inc(tile_done, 1)

            def halve(st, chain):
                g = st.g
                freed(st, "v1")
                v.tensor_scalar(vh[g][:], vh[g][:], 0.5, None, ALU.mult).then_inc(dve_step, 1)
                dve.wait_ge(dve_step, chain.next())

            def refined_hidden(st):
                for c in range(RC):
                    freed(st, f"h{c}")
                    v.tensor_tensor(gp[:, 1, c, :], g32[:, c, :], gp[:, 0, c, :], ALU.subtract).then_inc(h_ready, 1)

            def take_refined(st):
                for u in range(2):
                    s = slice(2 * u, 2 * u + 2)
                    dve.wait_ge(ctrl_filled[u], st.slot_uses(u) + 1)
                    v.tensor_tensor(res[:, s, :], ctrl_ps(u)[:, 0:2 * D].rearrange("p (t d) -> p t d", d=D),
                                    rf_b2[:].unsqueeze(1).to_broadcast([P, 2, D]), ALU.add).then_inc(ctrl_freed[u], 1)

            def refine_variance(st):
                n = st.kinds(3)
                dve.wait_ge(res_ready, n + 1)
                steps = Steps(NORM_STEPS, n)
                variance(dve, nc, norm_step, steps, res, norm, norm_sems[0])
                return steps

            def finish(st, steps):
                n = st.kinds(3)
                reciprocal_root(dve, nc, norm_step, steps, norm, norm_sems[2], n)
                dve.wait_ge(final_stored, 16 * n + 1)
                normalised(nc, final, res, norm).then_inc(final_ready, 1)

            def stage(st):
                it, g, last, nxt = st.it, st.g, st.last_stage, st.next_stage
                chain = Steps(DVE_STEPS[it], 0, st.before(lambda it: DVE_STEPS[it]))
                if it == 3:
                    refined_hidden(st)
                    if nxt and nxt.it < 3:
                        low_parts(nxt)
                        take_refined(st)
                    if st.ends_alone:
                        if last.it < 3:
                            update(last, 2)
                            update(last, 3)
                        if nxt:
                            low_parts(nxt)
                        take_refined(st)
                        finish(st, refine_variance(st))
                    return
                if it == 2:
                    halve(st, chain)
                route(st, chain)
                hidden(st, chain)
                refined = last if last and last.it == 3 else None
                stream_weights(st, chain)
                unfinished = refined.last_stage if refined else last
                for t in range(NT):
                    control(st, t)
                    if t == 0 and refined:
                        norm_steps = refine_variance(refined)
                    if t < 2:
                        if unfinished:
                            update(unfinished, t + 2)
                    else:
                        update(st, t - 2)
                    if t == 2:
                        if refined:
                            finish(refined, norm_steps)
                        low_parts(nxt)
                chain.end()

            low_parts(Stage(FIRST, 0, None))
            dve.wait_ge(w2_high, 1)
            v.tensor_tensor(w2[:, 1], w2_32, w2[:, 0], ALU.subtract)
            v.tensor_tensor(w2_shared_low[0:HID, :], w2s_32[0:HID, 0, :], w2_shared_top[0:HID, :],
                            ALU.subtract).then_inc(w2_ready, 1)
            dve.wait_ge(small_in, 16 * SMALL)
            stages(dve, stage)

        @block.tensor
        def _(pe):
            t_ = nc.tensor
            pe.wait_ge(consts, 2)
            pe.wait_ge(small_in, 16 * SMALL)

            def ring(st, what):
                bank, use = st.spot(what)
                pe.wait_ge(ring_freed[bank], use + 1)
                return ps[:, bank, :], ring_filled[bank]

            def freed(st, what):
                bank, use = st.spot(what)
                pe.wait_ge(ring_freed[bank], use + 1 + 1)

            def transposes(st, name, src):
                for c in range(KC):
                    dst, done = ring(st, f"{name}{c}")
                    for t in range(NT):
                        last = t_.transpose(dst[:, t * P:(t + 1) * P], src[:, t, c * P:(c + 1) * P], ident[:])
                    last.then_inc(done, 1)

            def split_products(out, pairs, ready=None):
                n = len(pairs)
                for j, (stationary, moving) in enumerate(pairs):
                    if ready is not None:
                        pe.wait_ge(h_ready, ready + j + 1)
                    t_.matmul(out, stationary[0], moving[0], start=(j == 0), stop=False)
                    t_.matmul(out, stationary[1], moving[0], start=False, stop=False)
                    last = t_.matmul(out, stationary[0], moving[1], start=False, stop=(j == n - 1))
                return last

            def onehots(st):
                g = st.g
                pe.wait_ge(onehot_ready, st.kinds(1) + 1)
                dst, done = ring(st, "onehot")
                dst = dst[0:3 * E, :].bitcast(F16)
                for k in range(2):
                    for t in range(NT):
                        last = t_.transpose(dst[:, (k * NT + t) * P:(k * NT + t + 1) * P],
                                            onehot[g][:, t, k].rearrange("p a e -> p (a e)"), identb[:])
                last.then_inc(done, 1)
                freed(st, "onehot")

            def chunk(st, c, moving):
                if st.it == 1 and c in SPARE:
                    pe.wait_ge(ctrl_freed[c], st.slot_uses(c) + 1)
                    dst, done = spare_ps(c), spare_filled[c]
                else:
                    dst, done = ring(st, f"h{c}")
                cols = slice(c * P, (c + 1) * P)
                split_products(dst, [((w1[:, 0, j, cols], w1[:, 1, j, cols]), m)
                                     for j, m in enumerate(moving)]).then_inc(done, 1)

            def mask(st, k, c):
                dst, done = ring(st, f"mask{k}{c}")
                t_.matmul(dst, spread[:, c, :], onehotT[st.g][:, k, :], start=True, stop=True).then_inc(done, 1)

            def hidden(st):
                it, g = st.it, st.g
                freed(st, "x0")
                freed(st, "x1")
                dst, done = ring(st, "rh")
                for c in range(KC):
                    last = t_.matmul(dst, wrh[:, c, :], xT32[:, c, :], start=(c == 0), stop=(c == KC - 1))
                last.then_inc(done, 1)
                pe.wait_ge(xlow_ready, st.kinds(1, 2, 3) + 1 + 1)
                moving = [(xTp[g][:, 0, c, :], xTp[g][:, 1, c, :]) for c in range(KC)]
                if it == 2:
                    pe.wait_ge(vlow_ready, st.kinds(2) + 1 + 1)
                    moving += [(vTp[g][:, 0, c, :], vTp[g][:, 1, c, :]) for c in range(KC)]
                chunk(st, EC, moving)
                if it == 1:
                    chunk(st, 0, moving)
                freed(st, "rh")
                dst, done = ring(st, "logits")
                for t in range(NT):
                    last = t_.matmul(dst[:, 16 * t:16 * t + E + 1], rh[:, t * P:(t + 1) * P], w2rh[:],
                                     start=True, stop=True)
                last.then_inc(done, 1)
                if it == 2:
                    for c in range(EC):
                        chunk(st, c, moving)
                    return
                chunk(st, 1, moving)
                chunk(st, 2, moving)
                onehots(st)
                for c in range(2):
                    mask(st, 0, c)
                    mask(st, 1, c)
                chunk(st, 3, moving)
                for c in range(2, EC):
                    mask(st, 0, c)
                    mask(st, 1, c)

            def control(st, t):
                it, g, h0 = st.it, st.g, st.before(hs)
                cols = ((0, 2 * D), (2 * D, CTRL)) if it == 2 else ((D, CTRL),)
                tok = slice(t * P, (t + 1) * P)
                for s in range(STREAMS):
                    if t == 0 and s == 0:
                        pe.wait_ge(h_ready, h0 + 1 + 1)
                    pe.wait_ge(ctrl_freed[s], st.slot_uses(s) + t + 1)
                    if s == 0:
                        terms = [(shared_hl[:, tok], w2_shared_top[:]), (shared_h1[:, tok], w2_shared_low[:])]
                    else:
                        k = s - 1
                        terms = [(onehotT[g][:, k, tok], b2_parts[:])]
                        for c in range(EC):
                            terms += [(routed[:, k, 0, c, tok], w2[:, 0, c, :]),
                                      (routed[:, k, 0, c, tok], w2[:, 1, c, :]),
                                      (routed[:, k, 1, c, tok], w2[:, 0, c, :])]
                    for j, (stationary, moving) in enumerate(terms):
                        if t == 0 and s == 1 and j % 3 == 1:
                            pe.wait_ge(h_ready, h0 + 1 + j // 3 + 1 + 1)
                        for a, z in cols:
                            last = t_.matmul(ctrl_ps(s)[:, a - cols[0][0]:z - cols[0][0]], stationary,
                                             moving[:, a:z], start=(j == 0), stop=(j == len(terms) - 1))
                    last.then_inc(ctrl_filled[s], 1)

            def refine_hidden(st):
                g = st.g
                pe.wait_ge(xlow_ready, st.kinds(1, 2, 3) + 1 + 1)
                for c in range(RC):
                    dst, done = ring(st, f"h{c}")
                    cols = slice(c * P, (c + 1) * P)
                    split_products(dst, [((rf1[:, 0, j, cols], rf1[:, 1, j, cols]),
                                          (xTp[g][:, 0, j, :], xTp[g][:, 1, j, :]))
                                         for j in range(KC)]).then_inc(done, 1)

            def refine_out(st):
                for t in range(NT):
                    u, tok = t // 2, slice(t * P, (t + 1) * P)
                    if t % 2 == 0:
                        pe.wait_ge(ctrl_freed[u], st.slot_uses(u) + 1)
                    ready = st.before(hs) + 1 if t == 0 else None
                    last = split_products(ctrl_ps(u)[:, (t % 2) * D:(t % 2 + 1) * D],
                                          [((gp[:, 0, c, tok], gp[:, 1, c, tok]), (rf2[:, 0, c, :], rf2[:, 1, c, :]))
                                           for c in range(RC)], ready)
                    if t % 2:
                        last.then_inc(ctrl_filled[u], 1)

            def transpose_state(st):
                g = st.g
                if st.it == 1:
                    pe.wait_ge(x_full[g], 16 * (st.pair + 1))
                else:
                    under_way = 0 if st.ends_alone and st.g == 1 else 1
                    pe.wait_ge(tile_done, NT * (st.controls - under_way) + NT)
                transposes(st, "x", (x1 if st.it == 1 else x2)[g])
                if st.it == 2:
                    transposes(st, "v", vh[g])

            def stage(st):
                nxt = st.next_stage
                if st.order is FIRST and st.at == 0:
                    pe.wait_ge(w1_ready, 1)
                if st.order is FIRST and st.at == 1:
                    pe.wait_ge(refine_ready, 2)
                if st.it < 3:
                    hidden(st)
                    if st.order is FIRST and st.at == 0:
                        pe.wait_ge(w2_ready, 1)
                        pe.wait_ge(rows_in, 16 * 6)
                    for t in range(NT):
                        control(st, t)
                        if t == 2:
                            transpose_state(nxt)
                else:
                    refine_hidden(st)
                    if nxt and nxt.it < 3:
                        transpose_state(nxt)
                    refine_out(st)
                    if nxt and nxt.it == 3:
                        transpose_state(nxt)

            transpose_state(Stage(FIRST, 0, None))
            stages(pe, stage)


def build(nc, args, out):
    a = dict(zip([n.replace("L0_", "") for n in _INS], args))
    parts_dram = nc.dram_tensor("parts_dram", [SEQS, 2, 3, 2, P, TOK], BF16).ap()
    normed_dram = nc.dram_tensor("normed_dram", [SEQS, TOK, D], F32).ap()
    attention(nc, a["attn_encodings"], a["attn_attn_W"], a["attn_attn_b"], a["attn_out_W"], a["attn_out_b"],
              parts_dram, normed_dram)
    experts(nc, {n[4:]: x for n, x in a.items() if n.startswith("ffn_")}, normed_dram, out)


_INS = ['L0_attn_encodings', 'L0_attn_attn_W', 'L0_attn_attn_b', 'L0_attn_out_W', 'L0_attn_out_b',
        'L0_ffn_integration_weight', 'L0_ffn_mu', 'L0_ffn_router_w1', 'L0_ffn_router_b1', 'L0_ffn_router_w2',
        'L0_ffn_router_b2', 'L0_ffn_halt_w1', 'L0_ffn_halt_b1', 'L0_ffn_halt_w2', 'L0_ffn_halt_b2',
        'L0_ffn_expert_w1', 'L0_ffn_expert_b1', 'L0_ffn_expert_w2', 'L0_ffn_expert_b2', 'L0_ffn_shared_w1',
        'L0_ffn_shared_b1', 'L0_ffn_shared_w2', 'L0_ffn_shared_b2', 'L0_ffn_shared_weight',
        'L0_ffn_refine_w1', 'L0_ffn_refine_b1', 'L0_ffn_refine_w2', 'L0_ffn_refine_b2']


def kernel(**inputs):
    import numpy as _np
    import concourse.bacc as _bacc
    from concourse import mybir as _mybir
    from concourse.bass_utils import run_bass_kernel_spmd as _run

    nc = _bacc.Bacc("TRN2", target_bir_lowering=False, num_devices=1)
    arrays, args = {}, []
    for name in _INS:
        a = _np.ascontiguousarray(inputs[name])
        if a.ndim == 0:
            a = a.reshape(1)
        arrays[f"in_{name}"] = a
        args.append(nc.dram_tensor(f"in_{name}", a.shape, _mybir.dt.from_np(a.dtype), kind="ExternalInput").ap())
    out = nc.dram_tensor("out_0", (SEQS, TOK, D), F32, kind="ExternalOutput").ap()
    build(nc, args, out)
    r = _run(nc, [arrays], core_ids=[0])
    return r.results[0]["out_0"]
```
